# Optimizing a Trainium2 kernel written in Bass

```python
import numpy as np
import jax
import jax.numpy as jnp

def _softmax(x, axis=-1):
    return jax.nn.softmax(x, axis=axis)

def _gelu(x):
    return jax.nn.gelu(x, approximate=True)

def _silu(x):
    return jax.nn.silu(x)

def _sigmoid(x):
    return jax.nn.sigmoid(x)

def _layernorm(x, axis=-1, eps=1e-05):
    m = jnp.mean(x, axis=axis, keepdims=True)
    v = jnp.var(x, axis=axis, keepdims=True)
    return (x - m) / jnp.sqrt(v + eps)

def _scatter_add(tgt, idx, src, axis=0):
    return tgt.at[idx].add(src)

def _segment_sum(src, seg, n):
    return jax.ops.segment_sum(src, seg, n)
kernel_name = 'mk_gps_d1_gnn_r8_426c9a'

def setup_inputs(seed: int=0):
    np.random.seed(seed)
    _w = jnp.asarray

    def _rec_inputs():
        import jax
        import jax.numpy as jnp
        _gk = jax.random.key(seed)
        x = -0.0006008 + 1.001 * jax.random.normal(jax.random.fold_in(_gk, 1), (12500, 256), jnp.float32)
        src = jax.random.randint(jax.random.fold_in(_gk, 2), (200000,), 0, 12500, jnp.int32)
        dst = jnp.minimum((12500 * jax.random.uniform(jax.random.fold_in(_gk, 3), (200000,)) ** 2.0).astype(jnp.int32), 99999)
        _o = jnp.argsort(dst, stable=True)
        src = src[_o]
        dst = dst[_o]
        return (x, src, dst)
    x, src, dst = _rec_inputs()

    def _L0_gnn_setup():
        import jax, jax.numpy as jnp
        import numpy as np
        N_NODES = 1250
        N_EDGES = 40000
        D_IN = 256
        D_OUT = 256
        NEG_SLOPE = 0.2
        key = jax.random.key(seed)
        ks = jax.random.split(key, 8)
        feature = jax.random.normal(ks[0], (N_NODES, D_IN), dtype=jnp.float32)
        src = jax.random.randint(ks[1], (N_EDGES,), 0, N_NODES, dtype=jnp.int32)
        dst = jax.random.randint(ks[2], (N_EDGES,), 0, N_NODES, dtype=jnp.int32)
        s = 1.0 / np.sqrt(D_IN)
        W_s = jax.random.normal(ks[3], (D_OUT, D_IN), dtype=jnp.float32) * s
        W_t = jax.random.normal(ks[4], (D_OUT, D_IN), dtype=jnp.float32) * s
        W_attn = jax.random.normal(ks[5], (1, D_OUT), dtype=jnp.float32) * (1.0 / np.sqrt(D_OUT))
        W_fc = jax.random.normal(ks[6], (D_OUT, D_IN), dtype=jnp.float32) * s
        b_fc = jnp.zeros((D_OUT,), dtype=jnp.float32)
        return {'feature': feature, 'src': src, 'dst': dst, 'W_s': W_s, 'W_t': W_t, 'W_attn': W_attn, 'W_fc': W_fc, 'b_fc': b_fc}
    _L0_gnn_all = _L0_gnn_setup()
    _L0_gnn_in = {k: v for k, v in _L0_gnn_all.items() if k in ('W_s', 'W_t', 'W_attn', 'W_fc', 'b_fc')}
    del _L0_gnn_all

    def _L0_mix_setup():
        import jax, jax.numpy as jnp
        import numpy as np
        D_MODEL = 256
        NUM_HEADS = 8
        DEPTH = D_MODEL // NUM_HEADS
        B, L = (32, 512)

        def _feature_map(x):
            return jax.nn.elu(x) + 1.0
        key = jax.random.key(seed)
        ks = jax.random.split(key, 9)
        sc = 1.0 / np.sqrt(D_MODEL)
        return {'x': jax.random.normal(ks[0], (B, L, D_MODEL), dtype=jnp.float32), 'wq': jax.random.normal(ks[1], (D_MODEL, D_MODEL), dtype=jnp.float32) * sc, 'bq': jnp.zeros((D_MODEL,), dtype=jnp.float32), 'wk': jax.random.normal(ks[2], (D_MODEL, D_MODEL), dtype=jnp.float32) * sc, 'bk': jnp.zeros((D_MODEL,), dtype=jnp.float32), 'wv': jax.random.normal(ks[3], (D_MODEL, D_MODEL), dtype=jnp.float32) * sc, 'bv': jnp.zeros((D_MODEL,), dtype=jnp.float32), 'wo': jax.random.normal(ks[4], (D_MODEL, D_MODEL), dtype=jnp.float32) * sc, 'bo': jnp.zeros((D_MODEL,), dtype=jnp.float32)}
    _L0_mix_all = _L0_mix_setup()
    _L0_mix_in = {k: v for k, v in _L0_mix_all.items() if k in ('wq', 'bq', 'wk', 'bk', 'wv', 'bv', 'wo', 'bo')}
    del _L0_mix_all

    def _L0_ffn_setup():
        import jax, jax.numpy as jnp
        import numpy as np
        E = 8
        K = 2
        D = 256
        H = 512
        DOUT = 256
        EPS = 1e-05
        key = jax.random.key(seed)
        ks = jax.random.split(key, 9)
        s = 0.02
        return {'x': jax.random.normal(ks[0], (4, 1024, D), jnp.float32), 'gamma': 1.0 + 0.05 * jax.random.normal(ks[1], (D,), jnp.float32), 'beta': 0.05 * jax.random.normal(ks[2], (D,), jnp.float32), 'Wr': 0.01 * jax.random.normal(ks[3], (D, E), jnp.float32), 'br': jnp.zeros((E,), jnp.float32), 'W1': s * jax.random.normal(ks[4], (E, D, H), jnp.float32), 'b1': s * jax.random.normal(ks[5], (E, H), jnp.float32), 'W2': s * jax.random.normal(ks[6], (E, H, DOUT), jnp.float32), 'b2': s * jax.random.normal(ks[7], (E, DOUT), jnp.float32)}
    _L0_ffn_all = _L0_ffn_setup()
    _L0_ffn_in = {k: v for k, v in _L0_ffn_all.items() if k in ('gamma', 'beta', 'Wr', 'br', 'W1', 'b1', 'W2', 'b2')}
    del _L0_ffn_all
    return {'x': x, 'src': src, 'dst': dst, 'L0_gnn_W_s': _L0_gnn_in['W_s'], 'L0_gnn_W_t': _L0_gnn_in['W_t'], 'L0_gnn_W_attn': _L0_gnn_in['W_attn'], 'L0_gnn_W_fc': _L0_gnn_in['W_fc'], 'L0_gnn_b_fc': _L0_gnn_in['b_fc'], 'L0_mix_wq': _L0_mix_in['wq'], 'L0_mix_bq': _L0_mix_in['bq'], 'L0_mix_wk': _L0_mix_in['wk'], 'L0_mix_bk': _L0_mix_in['bk'], 'L0_mix_wv': _L0_mix_in['wv'], 'L0_mix_bv': _L0_mix_in['bv'], 'L0_mix_wo': _L0_mix_in['wo'], 'L0_mix_bo': _L0_mix_in['bo'], 'L0_ffn_gamma': _L0_ffn_in['gamma'], 'L0_ffn_beta': _L0_ffn_in['beta'], 'L0_ffn_Wr': _L0_ffn_in['Wr'], 'L0_ffn_br': _L0_ffn_in['br'], 'L0_ffn_W1': _L0_ffn_in['W1'], 'L0_ffn_b1': _L0_ffn_in['b1'], 'L0_ffn_W2': _L0_ffn_in['W2'], 'L0_ffn_b2': _L0_ffn_in['b2']}

def reference(x, src, dst, L0_gnn_W_s, L0_gnn_W_t, L0_gnn_W_attn, L0_gnn_W_fc, L0_gnn_b_fc, L0_mix_wq, L0_mix_bq, L0_mix_wk, L0_mix_bk, L0_mix_wv, L0_mix_bv, L0_mix_wo, L0_mix_bo, L0_ffn_gamma, L0_ffn_beta, L0_ffn_Wr, L0_ffn_br, L0_ffn_W1, L0_ffn_b1, L0_ffn_W2, L0_ffn_b2):
    import jax
    import jax.numpy as jnp

    def _L0_gnn_ref(feature, src, dst, W_s, W_t, W_attn, W_fc, b_fc):
        import jax, jax.numpy as jnp
        import numpy as np
        N_NODES = 1250
        N_EDGES = 40000
        D_IN = 256
        D_OUT = 256
        NEG_SLOPE = 0.2
        n = feature.shape[0]
        proj_s = feature @ W_s.T
        proj_t = feature @ W_t.T
        z = proj_s[src] + proj_t[dst]
        z = jnp.where(z >= 0, z, NEG_SLOPE * z)
        e = (z @ W_attn.T)[:, 0]
        m = jax.ops.segment_max(e, src, num_segments=n)
        m = jnp.where(jnp.isfinite(m), m, 0.0)
        e_exp = jnp.exp(e - m[src])
        denom = jax.ops.segment_sum(e_exp, src, num_segments=n)
        alpha = e_exp / denom[src]
        msg = feature[src] * alpha[:, None]
        agg = jax.ops.segment_sum(msg, dst, num_segments=n)
        return agg @ W_fc.T + b_fc

    def _L0_mix_ref(x, wq, bq, wk, bk, wv, bv, wo, bo):
        import jax, jax.numpy as jnp
        import numpy as np
        D_MODEL = 256
        NUM_HEADS = 8
        DEPTH = D_MODEL // NUM_HEADS
        B, L = (32, 512)

        def _feature_map(x):
            return jax.nn.elu(x) + 1.0
        b, l, _ = x.shape
        q = (x @ wq + bq).reshape(b, l, NUM_HEADS, DEPTH)
        k = (x @ wk + bk).reshape(b, l, NUM_HEADS, DEPTH)
        v = (x @ wv + bv).reshape(b, l, NUM_HEADS, DEPTH)
        q = _feature_map(q)
        k = _feature_map(k)
        kv = jnp.einsum('blhd,blhe->bhde', k, v)
        k_sum = jnp.sum(k, axis=1)
        qkv = jnp.einsum('blhd,bhde->blhe', q, kv)
        normalizer = jnp.einsum('blhd,bhd->blh', q, k_sum) + 1e-06
        out = qkv / normalizer[..., None]
        out = out.reshape(b, l, D_MODEL)
        return out @ wo + bo

    def _L0_ffn_ref(x, gamma, beta, Wr, br, W1, b1, W2, b2):
        import jax, jax.numpy as jnp
        import numpy as np
        E = 8
        K = 2
        D = 256
        H = 512
        DOUT = 256
        EPS = 1e-05
        mu = jnp.mean(x, axis=-1, keepdims=True)
        var = jnp.mean(jnp.square(x - mu), axis=-1, keepdims=True)
        xn = (x - mu) * jax.lax.rsqrt(var + EPS) * gamma + beta
        logits = jnp.einsum('bsd,de->bse', xn, Wr) + br
        top_vals, top_idx = jax.lax.top_k(logits, K)
        w = jax.nn.softmax(top_vals, axis=-1)
        w_full = jnp.einsum('bsk,bske->bse', w, jax.nn.one_hot(top_idx, E, dtype=w.dtype))
        y = jnp.zeros(x.shape[:-1] + (DOUT,), x.dtype)
        for e in range(E):
            h = jax.nn.gelu(jnp.einsum('bsd,dh->bsh', xn, W1[e]) + b1[e], approximate=False)
            y_e = jnp.einsum('bsh,hd->bsd', h, W2[e]) + b2[e]
            y = y + y_e * w_full[..., e, None]
        return y
    xn = _layernorm(x, axis=-1)
    x = x + _L0_gnn_ref(xn, src, dst, L0_gnn_W_s, L0_gnn_W_t, L0_gnn_W_attn, L0_gnn_W_fc, L0_gnn_b_fc) + _L0_mix_ref(xn[None], L0_mix_wq, L0_mix_bq, L0_mix_wk, L0_mix_bk, L0_mix_wv, L0_mix_bv, L0_mix_wo, L0_mix_bo)[0]
    x = x + _L0_ffn_ref(_layernorm(x, axis=-1)[None], L0_ffn_gamma, L0_ffn_beta, L0_ffn_Wr, L0_ffn_br, L0_ffn_W1, L0_ffn_b1, L0_ffn_W2, L0_ffn_b2)[0]
    return x

_drawn_inputs = setup_inputs


def setup_inputs(seed=0):
    import zlib

    import numpy as np

    out = dict(_drawn_inputs(seed))
    spreads = {'L0_gnn_b_fc': (0.0, 0.1),
     'L0_mix_bq': (0.0, 2.0),
     'L0_mix_bk': (0.0, 2.0),
     'L0_mix_bv': (0.0, 0.1),
     'L0_mix_bo': (0.0, 0.1),
     'L0_ffn_br': (0.0, 0.1)}
    factors = {'L0_mix_wq': 8.0,
     'L0_mix_wk': 6.168,
     'L0_mix_wv': 4.324,
     'L0_ffn_gamma': 6.255,
     'L0_ffn_beta': 5.102,
     'L0_ffn_b1': 8.0,
     'L0_ffn_b2': 4.522}
    for name, (base, spread) in spreads.items():
        noise = np.random.default_rng([zlib.crc32(name.encode()), seed]).standard_normal(out[name].shape)
        drawn = base * np.exp(spread * noise) if base else spread * noise
        out[name] = jnp.asarray(drawn.astype(out[name].dtype))
    for name, factor in factors.items():
        out[name] = (out[name] * factor).astype(out[name].dtype)
    return out
```

```python
from contextlib import ExitStack

import concourse.bass as bass
from concourse import mybir

ALU = mybir.AluOpType
ACT = mybir.ActivationFunctionType
AX = mybir.AxisListType
F32 = mybir.dt.float32
I32 = mybir.dt.int32
U32 = mybir.dt.uint32

P = 128
R = 125
S = 4
G = R * S
D = 256
K = D // P
HEADS = 8
HD = D // HEADS
J = 16
C = R * J
Q = 4
XW = D + 2
SLOPE = 0.2
SAFE = 60.0
FAR = 1.6e38
EPS = 1e-5


class Memory:

    def __init__(self, nc, ctx, prefix):
        self.nc, self.ctx, self.prefix = nc, ctx, prefix

    def sb(self, name, shape, dt=F32):
        return self.ctx.enter_context(self.nc.sbuf_tensor(f"{self.prefix}_{name}", shape, dt))

    def ps(self, name, shape, dt=F32):
        return self.ctx.enter_context(self.nc.psum_tensor(f"{self.prefix}_{name}", shape, dt))

    def sem(self, name):
        return self.ctx.enter_context(self.nc.semaphore(f"{self.prefix}_{name}"))


def project(nc, T):
    NG = T.x.shape[0] // G
    with ExitStack() as ctx:
        m = Memory(nc, ctx, "pj")
        sb, ps, sem = m.sb, m.ps, m.sem
        w_raw = sb("w_raw", [P, 3, K, D])
        w_st = sb("w_st", [P, K, 2, D])
        w_kv = sb("w_kv", [P, K, 2, D])
        w_q = sb("w_q", [P, K, D])
        b_kv = sb("b_kv", [P, 2, D])
        b_q = sb("b_q", [P, K])
        x = sb("x", [R, 2, S, D])
        xn = sb("xn", [R, 2, S, D])
        stats = sb("stats", [R, S, 6])
        mv = sb("mv", [R, S, 2])
        var = sb("var", [R, S])
        half = sb("half", [R, S])
        rstd = sb("rstd", [R, S])
        xnT = sb("xnT", [P, K, G])
        proj = sb("proj", [R, 2, S, 2, D])
        kb = sb("kb", [R, 2, D])
        kpos = sb("kpos", [R, 2, D])
        kexp = sb("kexp", [R, 2, D])
        kf = sb("kf", [R, 2, S, D])
        v1 = sb("v1", [R, 2, S, K, P + 1])
        qpos = sb("qpos", [P, K, G])
        qexp = sb("qexp", [P, K, G])
        qf = sb("qf", [P, 2, K, G])
        zero = sb("zero", [R, 2 * (P + 1)])

        tp = ps("tp", [P, K, 512])
        p1 = ps("p1", [P, 2, 512])
        p2 = ps("p2", [P, 2, 512])
        pq = ps("pq", [P, 512])
        pkv = ps("pkv", [P, 512])

        weights_in = sem("weights_in")
        ident_zeroed, ident_ready, consts_ready = sem("ident_zeroed"), sem("ident_ready"), sem("consts_ready")
        w_turned, w_copied = sem("w_turned"), sem("w_copied")
        x_in = [sem(f"x_in{b}") for b in range(2)]
        var_ready = sem("var_ready")
        stats_ready, mv_ready, rstd_ready, xn_ready = sem("stats_ready"), sem("mv_ready"), sem("rstd_ready"), sem("xn_ready")
        xn_stored = [sem(f"xn_stored{b}") for b in range(2)]
        xn_turned, xnT_ready = sem("xn_turned"), sem("xnT_ready")
        p1_ready, p1_copied, p2_ready, p2_copied = sem("p1_ready"), sem("p1_copied"), sem("p2_ready"), sem("p2_copied")
        proj_stored = [sem(f"proj_stored{b}") for b in range(2)]
        kexp_ready, kpos_ready, kf_ready, kv_added = sem("kexp_ready"), sem("kpos_ready"), sem("kf_ready"), sem("kv_added")
        pq_ready, pq_read, qf_ready = sem("pq_ready"), sem("pq_read"), sem("qf_ready")
        q_stored = [sem(f"q_stored{b}") for b in range(2)]
        kv_cleared, kv_out = sem("kv_cleared"), sem("kv_out")

        block = ctx.enter_context(nc.Block())
        x_rows = T.x.rearrange("(g s p) d -> g p s d", s=S, p=R)
        xn_rows = T.xn_table[0:NG * G, :].rearrange("(g s p) d -> g p s d", s=S, p=R)
        ps_rows = T.ps_table.rearrange("(g s p) d -> g p s d", s=S, p=R)
        pt_rows = T.pt_table.rearrange("(g s p) d -> g p s d", s=S, p=R)
        q_cols = T.q_table.rearrange("k p (g n) -> g p k n", n=G)

        def steps(eng, body):
            body(0, 0, 0)
            body(1, 1, 0)
            body(2, 0, 1)
            with eng.Fori(1, (NG - 1) // 2) as i:
                body(i * 2 + 1, 1, i)
                body(i * 2 + 2, 0, i + 1)

        @block.sync
        def _(sp):
            for n, w in enumerate((T.W_s, T.W_t, T.W_fc)):
                sp.dma_start(w_raw[:, n], w.rearrange("(c p) i -> p c i", p=P)).then_inc(weights_in, 16)
            for n, w in enumerate((T.wk, T.wv)):
                sp.dma_start(w_kv[:, :, n, :], w.rearrange("(c p) o -> p c o", p=P)).then_inc(weights_in, 16)
            sp.dma_start(w_q[:], T.wq.rearrange("(c p) o -> p c o", p=P)).then_inc(weights_in, 16)
            for n, b in enumerate((T.bk, T.bv)):
                sp.dma_start(b_kv[:, n, :], b.partition_broadcast(P)).then_inc(weights_in, 16)
            for k in range(K):
                sp.dma_start(b_q[:, k:k + 1], T.bq[k * P:(k + 1) * P].rearrange("(p a) -> p a", a=1)).then_inc(weights_in, 16)

            def step(g, b, u):
                if not (isinstance(g, int) and g < 2):
                    sp.wait_ge(xn_ready, g - 1)
                sp.dma_start(x[:, b], x_rows[g]).then_inc(x_in[b], 16)
                if not (isinstance(g, int) and g < 1):
                    c = 1 - b
                    sp.wait_ge(xn_ready, g)
                    sp.dma_start(xn_rows[g - 1, :, :, 0:D], xn[:, c]).then_inc(xn_stored[c], 16)

            steps(sp, step)
            sp.wait_ge(xn_ready, NG)
            sp.dma_start(xn_rows[NG - 1, :, :, 0:D], xn[:, (NG - 1) % 2]).then_inc(xn_stored[(NG - 1) % 2], 16)
            for b in range(2):
                n = (NG + 1 - b) // 2
                sp.wait_ge(xn_stored[b], 16 * n)
                sp.wait_ge(proj_stored[b], 32 * n)
                sp.wait_ge(q_stored[b], 16 * n)

        @block.gpsimd
        def _(pool):
            pool.memset(T.ident[:], 0.0).then_inc(ident_zeroed, 1)
            pool.wait_ge(ident_zeroed, 1)
            pool.affine_select(out=T.ident[:], in_=T.ident[:], compare_op=ALU.not_equal, fill=1.0, base=0,
                               pattern=[[-1, P]], channel_multiplier=1).then_inc(ident_ready, 1)
            pool.memset(v1[:], 1.0)
            pool.memset(half[:], -0.5)
            pool.memset(zero[:], 0.0).then_inc(consts_ready, 1)

            def step(g, b, u):
                pool.wait_ge(mv_ready, g + 1)
                pool.sem_inc(T.passed, 1)
                pool.tensor_scalar(var[:], mv[:, :, 1], EPS, None, ALU.add).then_inc(var_ready, 1)
                pool.wait_ge(var_ready, g + 1)
                pool.tensor_tensor(rstd[:], var[:], half[:], ALU.pow).then_inc(rstd_ready, 1)

            steps(pool, step)

        @block.tensor
        def _(pe):
            pe.wait_ge(consts_ready, 1)
            pe.wait_ge(ident_ready, 1)
            pe.matmul(pkv[:, 0:2 * (P + 1)], zero[:, 0:P], zero[:], start=True, stop=False,
                      skip_group_check=True).then_inc(kv_cleared, 1)
            pe.wait_ge(weights_in, 16 * 10)
            n = 0
            for w in range(3):
                for i in range(K):
                    for o in range(K):
                        if n >= 2:
                            pe.wait_ge(w_copied, n - 1)
                        pe.transpose(tp[:, n % 2, 0:P], w_raw[:, w, o, i * P:(i + 1) * P], T.ident[:]).then_inc(w_turned, 1)
                        n += 1
            pe.wait_ge(w_copied, n)

            def add_kv(g, b, s):
                pe.wait_ge(kf_ready, g * S + s + 1)
                for k in range(K):
                    mm = pe.matmul(pkv[:, k * (P + 1):(k + 1) * (P + 1)], kf[:, b, s, k * P:(k + 1) * P],
                                   v1[:, b, s, k, :], start=False, stop=False, skip_group_check=True)
                mm.then_inc(kv_added, 1)

            def step(g, b, u):
                first = isinstance(g, int) and g == 0
                pe.wait_ge(xn_ready, g + 1)
                for k in range(K):
                    if not first:
                        pe.wait_ge(xnT_ready, g * K)
                    for s in range(S):
                        t = pe.transpose(tp[:, k, s * R:(s + 1) * R], xn[:, b, s, k * P:(k + 1) * P], T.ident[0:R, 0:R])
                    t.then_inc(xn_turned, 1)
                pe.wait_ge(xnT_ready, g * K + K)
                for s in range(S):
                    for out, w, ready, copied in ((p1, w_st, p1_ready, p1_copied), (p2, w_kv, p2_ready, p2_copied)):
                        if not (first and s < 2):
                            pe.wait_ge(copied, g * S + s - 1)
                        for k in range(K):
                            mm = pe.matmul(out[0:R, s % 2, :], xnT[:, k, s * R:(s + 1) * R],
                                           w[:, k].rearrange("p a d -> p (a d)"), start=k == 0, stop=k == K - 1)
                        mm.then_inc(ready, 1)
                for h in range(K):
                    if not (first and h == 0):
                        pe.wait_ge(pq_read, (g * K + h) * 2)
                    for k in range(K):
                        mm = pe.matmul(pq[:, 0:G], w_q[:, k, h * P:(h + 1) * P], xnT[:, k, :], start=k == 0, stop=k == K - 1)
                    mm.then_inc(pq_ready, 1)
                if not first:
                    for s in range(S):
                        add_kv(g - 1, 1 - b, s)

            steps(pe, step)
            for s in range(S):
                add_kv(NG - 1, (NG - 1) % 2, s)

        @block.scalar
        def _(act):
            act.wait_ge(weights_in, 16 * 10)

            def step(g, b, u):
                first = isinstance(g, int) and g == 0
                for k in range(K):
                    act.wait_ge(xn_turned, g * K + k + 1)
                    act.copy(xnT[:, k, :], tp[:, k, 0:G]).then_inc(xnT_ready, 1)
                if not (isinstance(g, int) and g < 2):
                    act.wait_ge(proj_stored[b], 32 * u)
                for s in range(S):
                    act.wait_ge(p1_ready, g * S + s + 1)
                    act.copy(proj[:, b, s].rearrange("p a d -> p (a d)"), p1[0:R, s % 2, :]).then_inc(p1_copied, 1)
                    act.wait_ge(p2_copied, g * S + s + 1)
                    if not (first and s < 2):
                        act.wait_ge(kf_ready, g * S + s - 1)
                    act.activation(kexp[:, s % 2], kb[:, s % 2], ACT.Exp).then_inc(kexp_ready, 1)
                for h in range(K):
                    act.wait_ge(pq_ready, g * K + h + 1)
                    if not first:
                        act.wait_ge(qf_ready, g * K + h - K + 1)
                    act.activation(qexp[:, h, :], pq[:, 0:G], ACT.Exp, bias=b_q[:, h:h + 1]).then_inc(pq_read, 1)
                act.wait_ge(p1_copied, g * S + S)
                act.dma_start(ps_rows[g], proj[:, b, :, 0, :]).then_inc(proj_stored[b], 16)
                act.dma_start(pt_rows[g], proj[:, b, :, 1, :]).then_inc(proj_stored[b], 16)
                act.wait_ge(qf_ready, g * K + K)
                act.dma_start(q_cols[g], qf[:, b]).then_inc(q_stored[b], 16)

            steps(act, step)

        @block.vector
        def _(dve):
            n = 0
            for w in range(3):
                for i in range(K):
                    for o in range(K):
                        dve.wait_ge(w_turned, n + 1)
                        dst = T.w_fcT[:, i, o * P:(o + 1) * P] if w == 2 else w_st[:, i, w, o * P:(o + 1) * P]
                        dve.tensor_copy(dst, tp[:, n % 2, 0:P]).then_inc(w_copied, 1)
                        n += 1
            dve.wait_ge(weights_in, 16 * 10)
            dve.wait_ge(consts_ready, 1)

            def norm(g, b, u):
                dve.wait_ge(x_in[b], u * 16 + 16)
                if not (isinstance(g, int) and g == 0):
                    dve.wait_ge(mv_ready, g)
                for s in range(S):
                    last = dve.bn_stats(stats[:, s, :], x[:, b, s, :])
                last.then_inc(stats_ready, 1)
                dve.wait_ge(stats_ready, g + 1)
                if not (isinstance(g, int) and g == 0):
                    dve.wait_ge(xn_ready, g)
                dve.sem_inc(T.passed, 1)
                for s in range(S):
                    last = dve.bn_aggr(mv[:, s, :], stats[:, s, :])
                last.then_inc(mv_ready, 1)
                dve.wait_ge(rstd_ready, g + 1)
                if not (isinstance(g, int) and g < 2):
                    dve.wait_ge(xn_stored[b], 16 * u)
                    dve.wait_ge(xn_turned, (g - 1) * K)
                for s in range(S):
                    last = dve.tensor_scalar(xn[:, b, s, :], x[:, b, s, :], mv[:, s, 0:1], rstd[:, s:s + 1], ALU.subtract, ALU.mult)
                last.then_inc(xn_ready, 1)

            def keys(g, b, u):
                first = isinstance(g, int) and g == 0
                if not (isinstance(g, int) and g < 2):
                    dve.wait_ge(kv_added, (g - 1) * S)

                def feature(s):
                    dve.wait_ge(kexp_ready, g * S + s + 1)
                    dve.wait_ge(kpos_ready, g * S + s + 1)
                    dve.scalar_tensor_tensor(out=kf[:, b, s, :], in0=kexp[:, s % 2], scalar=1.0, in1=kpos[:, s % 2],
                                             op0=ALU.min, op1=ALU.add).then_inc(kf_ready, 1)

                for s in range(S):
                    dve.wait_ge(p2_ready, g * S + s + 1)
                    dve.tensor_tensor(v1[:, b, s, :, 0:P], p2[0:R, s % 2, D:2 * D].rearrange("p (k d) -> p k d", k=K),
                                      b_kv[0:R, 1, :].rearrange("p (k d) -> p k d", k=K), ALU.add)
                    if not (first and s < 2):
                        dve.wait_ge(kf_ready, g * S + s - 1)
                        dve.wait_ge(kpos_ready, g * S + s - 1)
                    dve.tensor_tensor(kb[:, s % 2], p2[0:R, s % 2, 0:D], b_kv[0:R, 0, :], ALU.add).then_inc(p2_copied, 1)
                    dve.wait_ge(p2_copied, g * S + s + 1)
                    dve.tensor_scalar(kpos[:, s % 2], kb[:, s % 2], 0.0, None, ALU.max).then_inc(kpos_ready, 1)
                    if s >= 1:
                        feature(s - 1)
                feature(S - 1)
                if not (isinstance(g, int) and g < 2):
                    dve.wait_ge(q_stored[b], 16 * u)
                for h in range(K):
                    dve.wait_ge(pq_read, (g * K + h) * 2 + 1)
                    if not first:
                        dve.wait_ge(qf_ready, g * K + h - K + 1)
                    dve.tensor_scalar(qpos[:, h, :], pq[:, 0:G], b_q[:, h:h + 1], 0.0, ALU.add, ALU.max).then_inc(pq_read, 1)
                    dve.wait_ge(pq_read, (g * K + h + 1) * 2)
                    dve.scalar_tensor_tensor(out=qf[:, b, h, :], in0=qexp[:, h, :], scalar=1.0, in1=qpos[:, h, :],
                                             op0=ALU.min, op1=ALU.add).then_inc(qf_ready, 1)

            norm(0, 0, 0)
            norm(1, 1, 0)
            keys(0, 0, 0)
            norm(2, 0, 1)
            keys(1, 1, 0)
            with dve.Fori(1, (NG - 1) // 2) as i:
                norm(i * 2 + 1, 1, i)
                keys(i * 2, 0, i)
                norm(i * 2 + 2, 0, i + 1)
                keys(i * 2 + 1, 1, i)
            keys(NG - 1, (NG - 1) % 2, (NG - 1) // 2)
            dve.memset(T.kv[:], 0.0)
            dve.memset(T.ksum[:], 0.0).then_inc(kv_out, 1)
            dve.wait_ge(kv_out, 1)
            dve.wait_ge(kv_added, NG * S)
            for k in range(K):
                for h in range(P // HD):
                    a, z = h * HD, (h + 1) * HD
                    dve.tensor_copy(T.kv[a:z, k, a:z], pkv[a:z, k * (P + 1) + a:k * (P + 1) + z])
                    dve.tensor_copy(T.ksum[a:z, k, a:z], pkv[a:z, k * (P + 1) + P:k * (P + 1) + P + 1].broadcast_to([HD, HD]))
            


def score(nc, T):
    E = T.src.shape[0]
    NC = E // C
    NQ = J // Q
    LO = P.bit_length() - 1
    with ExitStack() as ctx:
        m = Memory(nc, ctx, "sc")
        sb, ps, sem = m.sb, m.ps, m.sem
        src_i = sb("src_i", [R, 2, J], I32)
        dst_i = sb("dst_i", [R, 2, J], I32)
        w_attn = sb("w_attn", [P, D])
        rows_i = sb("rows_i", [R, P], I32)
        iota = sb("iota", [R, P])
        src_p = sb("src_p", [R, 2, Q, D])
        dst_p = sb("dst_p", [R, 2, Q, D])
        z = sb("z", [R, 2, Q, D])
        lk = sb("lk", [R, 2, Q, D])
        e = sb("e", [R, 2, J])
        cut = sb("cut", [R, 2, J])
        ex = sb("ex", [R, 2, J])
        low_i = sb("low_i", [R, 2, 2, J], I32)
        low = sb("low", [R, 2, 2, J])
        hot_row = sb("hot_row", [R, 2, J, P])
        hot_blk = sb("hot_blk", [R, 2, J, T.NB])
        zero = sb("zero", [R, P])
        sums = sb("sums", [P, T.NB])
        total = ps("total", [P, 512])

        consts_in, iota_made, iota_ready = sem("consts_in"), sem("iota_made"), sem("iota_ready")
        idx_in = [sem(f"idx_in{b}") for b in range(2)]
        rows_in = [sem(f"rows_in{b}") for b in range(2)]
        z_ready, leaky_ready, dots_ready = sem("z_ready"), sem("leaky_ready"), sem("dots_ready")
        scores_kept, exp_ready, low_ready, lowf_ready = sem("scores_kept"), sem("exp_ready"), sem("low_ready"), sem("lowf_ready")
        cut_ready = sem("cut_ready")
        shift_ready = sem("shift_ready")
        hot_ready, hot_used = sem("hot_ready"), sem("hot_used")

        block = ctx.enter_context(nc.Block())
        src_c = T.src.rearrange("(c p j) -> c p j", p=R, j=J)
        dst_c = T.dst.rearrange("(c p j) -> c p j", p=R, j=J)

        @block.sync
        def _(sp):
            sp.dma_start(w_attn[:], T.W_attn.rearrange("a d -> (a d)").partition_broadcast(P)).then_inc(consts_in, 16)

            def load(c, b):
                if not isinstance(c, int):
                    sp.wait_ge(z_ready, (c - 1) * NQ)
                    sp.wait_ge(low_ready, c - 1)
                sp.dma_start(src_i[:, b], src_c[c]).then_inc(idx_in[b], 16)
                sp.dma_start(dst_i[:, b], dst_c[c]).then_inc(idx_in[b], 16)

            load(0, 0)
            load(1, 1)
            with sp.Fori(1, NC // 2) as i:
                load(i * 2, 0)
                load(i * 2 + 1, 1)

        @block.gpsimd
        def _(pool):
            pool.iota(rows_i[:], [[1, P]], base=0, channel_multiplier=0).then_inc(iota_made, 1)
            pool.memset(zero[:], 0.0)
            pool.wait_ge(iota_made, 1)
            pool.tensor_copy(iota[:], rows_i[:]).then_inc(iota_ready, 1)

            def gather(c, b, i, first):
                pool.wait_ge(idx_in[b], i * 32 + 32)
                for q in range(NQ):
                    h = q % 2
                    if not (first and q < 2):
                        pool.wait_ge(z_ready, c * NQ + q - 1)
                    pool.sem_inc(T.passed, 1)
                    for t in range(Q):
                        j = q * Q + t
                        for rows, table, idx in ((src_p, T.ps_table, src_i), (dst_p, T.pt_table, dst_i)):
                            pool.indirect_dma_start(
                                out=rows[:, h, t, :], out_offset=None, in_=table,
                                in_offset=bass.IndirectOffsetOnAxis(ap=idx[:, b, j:j + 1], axis=0),
                            ).then_inc(rows_in[h], 16)

            gather(0, 0, 0, True)
            gather(1, 1, 0, False)
            with pool.Fori(1, NC // 2) as i:
                gather(i * 2, 0, i, False)
                gather(i * 2 + 1, 1, i, False)

        @block.vector
        def _(dve):
            dve.wait_ge(consts_in, 16)
            dve.wait_ge(iota_ready, 1)

            def leaky(c, q, first):
                n, h, b = c * NQ + q, q % 2, q % 2
                dve.wait_ge(z_ready, n + 1)
                if not (first and q < 2):
                    dve.wait_ge(dots_ready, n - 1)
                dve.scalar_tensor_tensor(out=lk[:, h], in0=z[:, h], scalar=SLOPE, in1=z[:, h],
                                         op0=ALU.mult, op1=ALU.max).then_inc(leaky_ready, 1)

            def dots(c, q, b, first):
                n, h = c * NQ + q, q % 2
                dve.wait_ge(leaky_ready, n + 1)
                if q == 0 and not first:
                    dve.wait_ge(scores_kept, c - 1)
                for t in range(Q):
                    j = q * Q + t
                    last = dve.tensor_tensor_reduce(out=lk[:, h, t], in0=lk[:, h, t], in1=w_attn[0:R], scale=1.0, scalar=0.0,
                                                    op0=ALU.mult, op1=ALU.add, accum_out=e[:, b, j:j + 1])
                last.then_inc(dots_ready, 1)

            def cap(c, b, first):
                dve.wait_ge(dots_ready, (c + 1) * NQ)
                if not first:
                    dve.wait_ge(exp_ready, c - 1)
                dve.tensor_scalar(cut[:, b], e[:, b], SAFE, None, ALU.min).then_inc(cut_ready, 1)

            def hots(c, b, first):
                dve.wait_ge(exp_ready, c + 1)
                dve.wait_ge(lowf_ready, c + 1)
                if not first:
                    dve.wait_ge(hot_used, c - 1)
                for j in range(J):
                    dve.tensor_scalar(hot_row[:, b, j], iota[:], low[:, b, 0, j:j + 1], None, ALU.is_equal)
                    last = dve.tensor_scalar(hot_blk[:, b, j], iota[:, 0:T.NB], low[:, b, 1, j:j + 1], ex[:, b, j:j + 1],
                                             ALU.is_equal, ALU.mult)
                last.then_inc(hot_ready, 1)

            def chunk(c, b, i, first, start):
                for q in range(NQ):
                    h = q % 2
                    n = c * NQ + q
                    dve.wait_ge(rows_in[h], (c * (NQ // 2) + q // 2 + 1) * (2 * Q * 16))
                    if not (start and q < 2):
                        dve.wait_ge(leaky_ready, n - 1)
                    dve.tensor_tensor(z[:, h], src_p[:, h], dst_p[:, h], ALU.add).then_inc(z_ready, 1)
                    leaky(c, q, start)
                    dots(c, q, b, first)
                cap(c, b, first)
                if not first:
                    dve.wait_ge(lowf_ready, c - 1)
                dve.tensor_scalar(low_i[:, b, 0], src_i[:, b], P - 1, None, ALU.bitwise_and)
                dve.tensor_scalar(low_i[:, b, 1], src_i[:, b], LO, None, ALU.arith_shift_right).then_inc(low_ready, 1)
                dve.wait_ge(low_ready, c + 1)
                if not first:
                    dve.wait_ge(hot_ready, c - 1)
                dve.tensor_copy(low[:, b], low_i[:, b]).then_inc(lowf_ready, 1)

            chunk(0, 0, 0, True, True)
            chunk(1, 1, 0, True, False)
            hots(0, 0, True)
            chunk(2, 0, 1, False, False)
            hots(1, 1, True)
            chunk(3, 1, 1, False, False)
            hots(2, 0, False)
            with dve.Fori(2, NC // 2) as i:
                chunk(i * 2, 0, i, False, False)
                hots(i * 2 - 1, 1, False)
                chunk(i * 2 + 1, 1, i, False, False)
                hots(i * 2, 0, False)
            hots(NC - 1, 1, False)
            dve.memset(T.shift[:], 0.0).then_inc(shift_ready, 1)
            dve.wait_ge(shift_ready, 1)
            dve.wait_ge(hot_used, NC)
            dve.tensor_scalar(sums[:], total[:, 0:T.NB], 1e-37, None, ALU.max).then_inc(shift_ready, 1)
            dve.wait_ge(shift_ready, 2)
            dve.reciprocal(T.shift[:, :, 1], sums[:])

        @block.scalar
        def _(act):
            def exps(c, b, first):
                act.wait_ge(dots_ready, (c + 1) * NQ)
                if not first:
                    act.wait_ge(hot_ready, c - 1)
                act.copy(T.e[:, bass.ds(c * J, J)], e[:, b]).then_inc(scores_kept, 1)
                act.wait_ge(cut_ready, c + 1)
                act.activation(ex[:, b], cut[:, b], ACT.Exp).then_inc(exp_ready, 1)

            exps(0, 0, True)
            exps(1, 1, True)
            with act.Fori(1, NC // 2) as i:
                exps(i * 2, 0, False)
                exps(i * 2 + 1, 1, False)

        @block.tensor
        def _(pe):
            pe.wait_ge(iota_ready, 1)
            pe.matmul(total[:, 0:T.NB], zero[:, 0:P], zero[:, 0:T.NB], start=True, stop=False, skip_group_check=True)

            def add(c, b):
                pe.wait_ge(hot_ready, c + 1)
                for j in range(J):
                    mm = pe.matmul(total[:, 0:T.NB], hot_row[:, b, j], hot_blk[:, b, j], start=False, stop=False,
                                   skip_group_check=True)
                mm.then_inc(hot_used, 1)

            with pe.Fori(0, NC // 2) as i:
                add(i * 2, 0)
                add(i * 2 + 1, 1)


def plan(nc, T):
    NC = T.src.shape[0] // C
    LO = P.bit_length() - 1
    with ExitStack() as ctx:
        m = Memory(nc, ctx, "pl")
        sb, ps, sem = m.sb, m.ps, m.sem
        dst_i = sb("dst_i", [R, NC, J], I32)
        dst_f = sb("dst_f", [R, NC, J])
        low = sb("low", [R, 2, NC])
        chunk = sb("chunk", [NC, 2])
        row = sb("row", [1, 2, NC])
        row_i = sb("row_i", [1, 2, NC], I32)
        blk_i = sb("blk_i", [1, 2, NC], I32)
        blk = sb("blk", [1, 2, NC])
        count = sb("count", [1, NC])
        ones = sb("ones", [1, NC])
        before = sb("before", [1, NC])
        ext = sb("ext", [R, 2])
        extT = sb("extT", [1, 1])
        span = sb("span", [R, 1])
        far = sb("far", [1, 2])
        tp = ps("tp", [P, 2, 512])
        tq = ps("tq", [P, 2, 512])
        dst_in, chain, turned = sem("dst_in"), sem("step_done"), sem("turned")
        block = ctx.enter_context(nc.Block())

        @block.sync
        def _(sp):
            sp.dma_start(dst_i[:], T.dst.rearrange("(c p j) -> p c j", p=R, j=J)).then_inc(dst_in, 16)

        @block.tensor
        def _(pe):
            pe.wait_ge(chain, 4)
            for k in range(2):
                mm = pe.transpose(tp[0:NC, k, 0:R], low[:, k, :], T.ident[0:R, 0:R])
            mm.then_inc(turned, 1)
            pe.wait_ge(chain, 8)
            pe.transpose(tq[0:1, 1, 0:R], span[:], T.ident[0:R, 0:R]).then_inc(turned, 1)
            pe.wait_ge(chain, 10)
            for k in range(2):
                mm = pe.transpose(tq[0:1, 0, k * P:k * P + NC], chunk[:, k:k + 1], T.ident[0:NC, 0:NC])
            mm.then_inc(turned, 1)

        @block.vector
        def _(dve):
            done = 0

            def then(ins):
                nonlocal done
                done += 1
                ins.then_inc(chain, 1)
                dve.wait_ge(chain, done)

            dve.wait_ge(dst_in, 16)
            then(dve.tensor_copy(dst_f[:], dst_i[:]))
            then(dve.tensor_reduce(low[:, 0, :], dst_f[:], AX.X, ALU.max))
            then(dve.tensor_scalar(dst_f[:], dst_f[:], -1.0, None, ALU.mult))
            then(dve.tensor_reduce(low[:, 1, :], dst_f[:], AX.X, ALU.max))
            then(dve.tensor_reduce(ext[:, 0:1], T.e[:], AX.X, ALU.max))
            then(dve.tensor_reduce(ext[:, 1:2], T.e[:], AX.X, ALU.min))
            then(dve.tensor_scalar(span[:], ext[:, 1:2], -1.0, None, ALU.mult))
            then(dve.tensor_tensor(span[:], span[:], ext[:, 0:1], ALU.max))
            dve.wait_ge(turned, 1)
            then(dve.tensor_reduce(chunk[:, 0:1], tp[0:NC, 0, 0:R], AX.X, ALU.max))
            then(dve.tensor_reduce(chunk[:, 1:2], tp[0:NC, 1, 0:R], AX.X, ALU.max))
            dve.wait_ge(turned, 3)
            then(dve.tensor_reduce(extT[:], tq[0:1, 1, 0:R], AX.X, ALU.max))
            then(dve.tensor_scalar(T.far_i[:], extT[:], SAFE, None, ALU.is_gt))
            then(dve.tensor_copy(row[:, 0, :], tq[0:1, 0, 0:NC]))
            then(dve.tensor_scalar(row[:, 1, :], tq[0:1, 0, P:P + NC], -1.0, None, ALU.mult))
            then(dve.tensor_copy(row_i[:], row[:]))
            then(dve.tensor_scalar(blk_i[:], row_i[:], LO, None, ALU.arith_shift_right))
            then(dve.tensor_copy(blk[:], blk_i[:]))
            then(dve.tensor_tensor(count[:], blk[:, 0, :], blk[:, 1, :], ALU.subtract))
            then(dve.tensor_scalar(count[:], count[:], 1.0, None, ALU.add))
            then(dve.memset(ones[:], 1.0))
            then(dve.tensor_tensor_scan(before[:], ones[:], count[:], 0.0, ALU.mult, ALU.add))
            then(dve.memset(T.plan[:], 0))
            then(dve.tensor_copy(T.plan[:, 0, 1:NC + 1], blk[:, 0, :]))
            then(dve.tensor_copy(T.plan[:, 1, 0:NC], blk[:, 1, :]))
            then(dve.tensor_copy(T.plan[:, 2, 1:NC + 1], before[:]))


def reshift(nc, T):
    NC = T.src.shape[0] // C
    NB = T.NB
    with ExitStack() as ctx:
        m = Memory(nc, ctx, "rs")
        sb, sem = m.sb, m.sem
        src_i = sb("src_i", [P, C], I32)
        src_f = sb("src_f", [P, C])
        e = sb("e", [P, C])
        t = sb("t", [P, C])
        part = sb("part", [P, 1])
        node_i = sb("node_i", [P, NB], I32)
        node = sb("node", [P, NB])
        top = sb("top", [P, NB])
        total = sb("total", [P, NB])
        kept, chunk_in, chunk_used = sem("kept"), sem("chunk_in"), sem("chunk_used")
        made, ready, chain = sem("made"), sem("ready"), sem("chain")
        shifted, ex_ready = sem("shifted"), sem("ex_ready")

        block = ctx.enter_context(nc.Block())

        @block.sync
        def _(sp):
            far = sp.value_load(T.far_i[0:1, 0:1], min_val=0, max_val=1)
            with sp.If(far > 0):
                sp.dma_start(T.e_flat.rearrange("(c p j) -> p c j", p=R, j=J),
                             T.e[:].rearrange("p (c j) -> p c j", j=J)).then_inc(kept, 16)
                sp.wait_ge(kept, 16)
                for sweep in range(2):
                    with sp.Fori(0, NC) as c:
                        sp.wait_ge(chunk_used, c + sweep * NC + 1)
                        sp.dma_start(src_i[:], T.src[bass.ds(c * C, C)].partition_broadcast(P)).then_inc(chunk_in, 16)
                        sp.dma_start(e[:], T.e_flat[bass.ds(c * C, C)].partition_broadcast(P)).then_inc(chunk_in, 16)

        @block.gpsimd
        def _(pool):
            pool.iota(node_i[:], [[P, NB]], base=0, channel_multiplier=1).then_inc(made, 1)
            pool.wait_ge(made, 1)
            pool.tensor_copy(node[:], node_i[:]).then_inc(ready, 1)

        @block.scalar
        def _(act):
            far = act.value_load(T.far_i[0:1, 0:1], min_val=0, max_val=1)
            with act.If(far > 0):
                with act.Fori(0, NC) as c:
                    with act.Fori(0, NB) as b:
                        act.wait_ge(shifted, c * NB + b + 1)
                        act.activation(t[:], t[:], ACT.Exp).then_inc(ex_ready, 1)

        @block.vector
        def _(dve):
            dve.wait_ge(ready, 1)
            far = dve.value_load(T.far_i[0:1, 0:1], min_val=0, max_val=1)
            with dve.If(far > 0):
                dve.sem_inc(chunk_used, 1)
                dve.memset(top[:], -FAR)
                dve.memset(total[:], 0.0)
                with dve.Fori(0, NC) as c:
                    dve.wait_ge(chunk_in, c * 32 + 32)
                    dve.tensor_copy(src_f[:], src_i[:]).then_inc(chain, 1)
                    with dve.Fori(0, NB) as b:
                        n = c * (NB * 4 + 1) + b * 4 + 1
                        dve.wait_ge(chain, n)
                        dve.tensor_scalar(t[:], src_f[:], node[:, bass.ds(b, 1)], -FAR, ALU.not_equal, ALU.mult).then_inc(chain, 1)
                        dve.wait_ge(chain, n + 1)
                        dve.tensor_tensor(t[:], t[:], e[:], ALU.add).then_inc(chain, 1)
                        dve.wait_ge(chain, n + 2)
                        dve.tensor_reduce(part[:], t[:], AX.X, ALU.max).then_inc(chain, 1)
                        dve.wait_ge(chain, n + 3)
                        dve.tensor_tensor(top[:, bass.ds(b, 1)], top[:, bass.ds(b, 1)], part[:], ALU.max).then_inc(chain, 1)
                    dve.wait_ge(chain, (c + 1) * (NB * 4 + 1))
                    dve.sem_inc(chunk_used, 1)
                base = NC * (NB * 4 + 1)
                with dve.Fori(0, NC) as c:
                    dve.wait_ge(chunk_in, c * 32 + 32 + NC * 32)
                    dve.tensor_copy(src_f[:], src_i[:]).then_inc(chain, 1)
                    with dve.Fori(0, NB) as b:
                        n = c * (NB * 3 + 1) + b * 3 + 1 + base
                        dve.wait_ge(chain, n)
                        dve.tensor_scalar(t[:], e[:], top[:, bass.ds(b, 1)], 0.0, ALU.subtract, ALU.min).then_inc(shifted, 1)
                        dve.wait_ge(ex_ready, c * NB + b + 1)
                        dve.scalar_tensor_tensor(out=t[:], in0=src_f[:], scalar=node[:, bass.ds(b, 1)], in1=t[:],
                                                 op0=ALU.is_equal, op1=ALU.mult).then_inc(chain, 1)
                        dve.wait_ge(chain, n + 1)
                        dve.tensor_reduce(part[:], t[:], AX.X, ALU.add).then_inc(chain, 1)
                        dve.wait_ge(chain, n + 2)
                        dve.tensor_tensor(total[:, bass.ds(b, 1)], total[:, bass.ds(b, 1)], part[:], ALU.add).then_inc(chain, 1)
                    dve.wait_ge(chain, (c + 1) * (NB * 3 + 1) + base)
                    dve.sem_inc(chunk_used, 1)
                end = base + NC * (NB * 3 + 1)
                dve.tensor_scalar(total[:], total[:], 1e-37, None, ALU.max).then_inc(chain, 1)
                dve.tensor_copy(T.shift[:, :, 0], top[:])
                dve.wait_ge(chain, end + 1)
                dve.reciprocal(T.shift[:, :, 1], total[:])


def aggregate(nc, T):
    NC = T.src.shape[0] // C
    HJ = J // 2
    with ExitStack() as ctx:
        m = Memory(nc, ctx, "ag")
        sb, ps, sem = m.sb, m.ps, m.sem
        acc = sb("acc", [P, T.NB, D])
        src_i = sb("src_i", [R, 2, J], I32)
        dst_i = sb("dst_i", [R, 2, J], I32)
        dst_f = sb("dst_f", [R, 2, J])
        rows = sb("rows", [R, 2, J, XW])
        e_s = sb("e_s", [R, 2, J])
        ex = sb("ex", [R, 2, J])
        att = sb("att", [R, 2, J])
        rel = sb("rel", [R, J])
        rows_i = sb("rows_i", [R, P], I32)
        iota = sb("iota", [R, P])
        first_i = sb("first_i", [R, T.NB], I32)
        first_row = sb("first_row", [R, T.NB])
        hot = [sb(f"hot{k}", [R, HJ, P]) for k in range(2)]
        part = ps("part", [P, 512])

        table_done = sem("table_done")
        iota_made, iota_ready = sem("iota_made"), sem("iota_ready")
        idx_in = [sem(f"idx_in{b}") for b in range(2)]
        rows_in = [sem(f"rows_in{b}") for b in range(2)]
        dst_ready, e_ready, ex_ready, att_ready, rel_ready = (sem("dst_ready"), sem("e_ready"), sem("ex_ready"),
                                                              sem("att_ready"), sem("rel_ready"))
        hot_ready = [sem(f"hot_ready{k}") for k in range(2)]
        hot_used = [sem(f"hot_used{k}") for k in range(2)]
        cleared, added, chunk_begun = sem("cleared"), sem("added"), sem("chunk_begun")
        agg_out = sem("agg_out")

        block = ctx.enter_context(nc.Block())
        src_c = T.src.rearrange("(c p j) -> c p j", p=R, j=J)
        dst_c = T.dst.rearrange("(c p j) -> c p j", p=R, j=J)

        def planned(eng, c, NBmax=T.NB - 1):
            prev = eng.value_load(T.plan[0:1, 0, bass.ds(c, 1)], min_val=0, max_val=NBmax)
            last = eng.value_load(T.plan[0:1, 0, bass.ds(c + 1, 1)], min_val=0, max_val=NBmax)
            first = eng.value_load(T.plan[0:1, 1, bass.ds(c, 1)], min_val=0, max_val=NBmax)
            pairs = eng.value_load(T.plan[0:1, 2, bass.ds(c, 1)], min_val=0, max_val=T.NB * NC)
            return prev, first, last, pairs

        @block.sync
        def _(sp):
            with nc.allow_non_contiguous_dma(reason="two words for each node"):
                sp.dma_start(T.xn_table[:, D:XW].rearrange("(b p) w -> p b w", p=P), T.shift[:]).then_inc(table_done, 16)

            def load(c, b):
                if not isinstance(c, int):
                    sp.wait_ge(att_ready, c - 1)
                    sp.wait_ge(dst_ready, c - 1)
                sp.dma_start(src_i[:, b], src_c[c]).then_inc(idx_in[b], 16)
                sp.dma_start(dst_i[:, b], dst_c[c]).then_inc(idx_in[b], 16)

            load(0, 0)
            load(1, 1)
            with sp.Fori(1, NC // 2) as i:
                load(i * 2, 0)
                load(i * 2 + 1, 1)
            total = sp.value_load(T.plan[0:1, 2, NC:NC + 1], min_val=0, max_val=T.NB * NC)
            sp.wait_ge(added, total + 2)
            sp.dma_start(T.agg.rearrange("(b p) d -> p b d", p=P), acc[:]).then_inc(agg_out, 16)
            sp.wait_ge(agg_out, 16)

        @block.gpsimd
        def _(pool):
            pool.iota(rows_i[:], [[1, P]], base=0, channel_multiplier=0)
            pool.iota(first_i[:], [[P, T.NB]], base=0, channel_multiplier=0).then_inc(iota_made, 1)
            pool.wait_ge(iota_made, 1)
            pool.tensor_copy(iota[:], rows_i[:])
            pool.tensor_copy(first_row[:], first_i[:]).then_inc(iota_ready, 1)
            pool.wait_ge(table_done, 16)

            def gather(c, b, i):
                pool.wait_ge(idx_in[b], i * 32 + 32)
                if not isinstance(c, int):
                    pool.wait_ge(chunk_begun, c)
                pool.sem_inc(T.passed, 1)
                for j in range(J):
                    pool.indirect_dma_start(
                        out=rows[:, b, j, :], out_offset=None, in_=T.xn_table[0:T.x.shape[0], :],
                        in_offset=bass.IndirectOffsetOnAxis(ap=src_i[:, b, j:j + 1], axis=0),
                    ).then_inc(rows_in[b], 16)

            gather(0, 0, 0)
            gather(1, 1, 0)
            with pool.Fori(1, NC // 2) as i:
                gather(i * 2, 0, i)
                gather(i * 2 + 1, 1, i)

        @block.vector
        def _(dve):
            dve.wait_ge(iota_ready, 1)
            dve.memset(part[:, 0:D], 0.0)
            for n in range(7):
                a, z = T.NB * n // 7, T.NB * (n + 1) // 7
                last = dve.memset(acc[:, a:z, :], 0.0)
            last.then_inc(cleared, 1)
            dve.wait_ge(cleared, 1)
            dve.sem_inc(hot_ready[0], 1)
            dve.sem_inc(hot_ready[1], 1)
            dve.sem_inc(added, 1)

            def one_hot(k, b, n):
                dve.wait_ge(hot_used[k], n + 1)
                for t in range(HJ):
                    j = k * HJ + t
                    last = dve.tensor_scalar(hot[k][:, t], iota[:], rel[:, j:j + 1], att[:, b, j:j + 1],
                                             ALU.is_equal, ALU.mult)
                last.then_inc(hot_ready[k], 1)

            def pair(b, n, blk, prev):
                dve.wait_ge(hot_ready[1], n + 1)
                dve.tensor_scalar(rel[:], dst_f[:, b], first_row[:, bass.ds(blk, 1)], None, ALU.subtract).then_inc(rel_ready, 1)
                dve.wait_ge(rel_ready, n + 1)
                one_hot(0, b, n)
                dve.wait_ge(hot_used[1], n + 1)
                dve.wait_ge(added, n + 1)
                row = acc[:, bass.ds(prev, 1), :].rearrange("p a d -> p (a d)")
                dve.tensor_tensor(row, row, part[:, 0:D], ALU.add).then_inc(added, 1)
                one_hot(1, b, n)

            def chunk(c, b, i):
                prev, first, last, pairs = planned(dve, c)
                dve.wait_ge(idx_in[b], i * 32 + 32)
                dve.tensor_copy(dst_f[:, b], dst_i[:, b]).then_inc(dst_ready, 1)
                dve.wait_ge(rows_in[b], i * (16 * J) + 16 * J)
                dve.tensor_tensor(e_s[:, b], T.e[:, bass.ds(c * J, J)], rows[:, b, :, D], ALU.subtract).then_inc(e_ready, 1)
                dve.wait_ge(ex_ready, c + 1)
                dve.tensor_tensor(att[:, b], ex[:, b], rows[:, b, :, D + 1], ALU.mult).then_inc(att_ready, 1)
                dve.wait_ge(att_ready, c + 1)
                dve.wait_ge(dst_ready, c + 1)
                dve.wait_ge(hot_used[1], pairs + 1)
                dve.sem_inc(chunk_begun, 1)
                pair(b, pairs, first, prev)
                with dve.If(first < last):
                    with dve.Fori(1, last - first + 1) as d:
                        blk = nc.s_assert_within(first + d, 1, T.NB - 1, skip_runtime_bounds_check_because="it is at most last")
                        pair(b, pairs + d, blk, blk - 1)

            with dve.Fori(0, NC // 2) as i:
                chunk(i * 2, 0, i)
                chunk(i * 2 + 1, 1, i)
            final = dve.value_load(T.plan[0:1, 0, NC:NC + 1], min_val=0, max_val=T.NB - 1)
            total = dve.value_load(T.plan[0:1, 2, NC:NC + 1], min_val=0, max_val=T.NB * NC)
            dve.wait_ge(hot_used[1], total + 1)
            dve.wait_ge(added, total + 1)
            row = acc[:, bass.ds(final, 1), :].rearrange("p a d -> p (a d)")
            dve.tensor_tensor(row, row, part[:, 0:D], ALU.add).then_inc(added, 1)

        @block.scalar
        def _(act):
            with act.Fori(0, NC // 2) as i:
                for b in range(2):
                    act.wait_ge(e_ready, i * 2 + b + 1)
                    act.activation(ex[:, b], e_s[:, b], ACT.Exp).then_inc(ex_ready, 1)

        @block.tensor
        def _(pe):
            pe.wait_ge(cleared, 1)
            for k in range(2):
                pe.sem_inc(hot_used[k], 1)

            def pair(b, n):
                pe.wait_ge(added, n + 2)
                for k in range(2):
                    pe.wait_ge(hot_ready[k], n + 2)
                    for t in range(HJ):
                        j = k * HJ + t
                        mm = pe.matmul(part[:, 0:D], hot[k][:, t], rows[:, b, j, 0:D], start=j == 0, stop=j == J - 1)
                    mm.then_inc(hot_used[k], 1)

            def chunk(c, b):
                prev, first, last, pairs = planned(pe, c)
                pair(b, pairs)
                with pe.If(first < last):
                    with pe.Fori(1, last - first + 1) as d:
                        pair(b, pairs + d)

            with pe.Fori(0, NC // 2) as i:
                chunk(i * 2, 0)
                chunk(i * 2 + 1, 1)


def finish(nc, T):
    NG = T.x.shape[0] // G
    E, _, H = T.W1.shape
    M = H // P
    NW = 2 * E + 6 + 3 * K
    with ExitStack() as ctx:
        m = Memory(nc, ctx, "fi")
        sb, ps, sem = m.sb, m.ps, m.sem
        w1 = sb("w1", [P, E, K, H])
        w2 = sb("w2", [P, E, M, D])
        w_o = sb("w_o", [P, K, D])
        w_r = sb("w_r", [P, K, E])
        b1 = sb("b1", [P, E, M])
        b1_rows = sb("b1_rows", [E * M, P])
        b2 = sb("b2", [E, D])
        b_r = sb("b_r", [P, E])
        gamma = sb("gamma", [P, K])
        beta = sb("beta", [P, K])
        b_out = sb("b_out", [P, 2, D])
        bias = sb("bias", [P, D])
        eight_i = sb("eight_i", [P, E], I32)
        eight = sb("eight", [P, E])
        half = sb("half", [R, S])
        x = sb("x", [R, S, D])
        agg = sb("agg", [R, S, D])
        qT = sb("qT", [P, K, G])
        aggT = sb("aggT", [P, K, G])
        den = sb("den", [P, K, G])
        oT = sb("oT", [P, K, G])
        x1 = sb("x1", [R, S, D])
        stats = sb("stats", [R, S, 6])
        mv = sb("mv", [R, S, 2])
        var = sb("var", [R, S])
        rstd = sb("rstd", [R, S])
        xn = sb("xn", [R, S, D])
        xhT = sb("xhT", [P, K, G])
        logit = sb("logit", [R, S, E])
        top = sb("top", [R, S, 8])
        top_i = sb("top_i", [R, S, 8], U32)
        top_f = sb("top_f", [R, S, 8])
        gap = sb("gap", [R, S])
        odds = sb("odds", [R, S])
        both = sb("both", [R, S])
        gate = sb("gate", [R, 2, S])
        pick = sb("pick", [R, 2, S, E])
        wgt = sb("wgt", [R, S, E])
        wgtT = sb("wgtT", [E, S, R])
        hid = sb("hid", [P, 2, M, G])
        y = sb("y", [R, S, D])

        bank = [ps(f"bank{n}", [P, 512]) for n in range(8)]
        weights_in, acts_in, out_done = sem("weights_in"), sem("acts_in"), sem("out_done")
        made, ready, b1_ready = sem("made"), sem("ready"), sem("b1_ready")
        agg_turned, aggT_ready = sem("agg_turned"), sem("aggT_ready")
        lin_ready, den_ready, oT_ready = sem("lin_ready"), sem("den_ready"), sem("oT_ready")
        bias_added, x1_mm, x1_ready = sem("bias_added"), sem("x1_mm"), sem("x1_ready")
        ln, mv_ready, var_ready, rstd_ready, xn_ready = sem("ln"), sem("mv_ready"), sem("var_ready"), sem("rstd_ready"), sem("xn_ready")
        xn_turned, xhT_ready = sem("xn_turned"), sem("xhT_ready")
        logit_mm, route, odds_ready, wgt_ready = sem("logit_mm"), sem("route"), sem("odds_ready"), sem("wgt_ready")
        y_free = sem("y_free")
        wgt_chain = sem("wgt_chain")
        wgt_turned, wgtT_ready, y0_mm = sem("wgt_turned"), sem("wgtT_ready"), sem("y0_mm")
        hid_mm, hid_ready, y_mm, y_added = sem("hid_mm"), sem("hid_ready"), sem("y_mm"), sem("y_added")

        block = ctx.enter_context(nc.Block())
        x_rows = T.x.rearrange("(g s p) d -> g p s d", s=S, p=R)
        out_rows = T.out.rearrange("(g s p) d -> g p s d", s=S, p=R)
        agg_rows = T.agg[0:NG * G, :].rearrange("(g s p) d -> g p s d", s=S, p=R)
        q_cols = T.q_table.rearrange("k p (g n) -> g p k n", n=G)
        NACT = 3 * 16

        @block.sync
        def _(sp):
            for e in range(E):
                sp.dma_start(w1[:, e], T.W1[e].rearrange("(c p) h -> p c h", p=P)).then_inc(weights_in, 16)
                sp.dma_start(w2[:, e], T.W2[e].rearrange("(c p) d -> p c d", p=P)).then_inc(weights_in, 16)
            sp.dma_start(w_o[:], T.wo.rearrange("(c p) o -> p c o", p=P)).then_inc(weights_in, 16)
            sp.dma_start(b1_rows[:], T.b1.rearrange("e (m p) -> (e m) p", p=P)).then_inc(weights_in, 16)
            sp.dma_start(b2[:], T.b2).then_inc(weights_in, 16)
            sp.dma_start(b_r[:], T.br.partition_broadcast(P)).then_inc(weights_in, 16)
            for k in range(K):
                for dst, vec in ((gamma, T.gamma), (beta, T.beta)):
                    sp.dma_start(dst[:, k:k + 1], vec[k * P:(k + 1) * P].rearrange("(p a) -> p a", a=1)).then_inc(weights_in, 16)
                sp.dma_start(w_r[:, k, :], T.Wr[k * P:(k + 1) * P, :]).then_inc(weights_in, 16)
            sp.dma_start(b_out[:, 0], T.b_fc.partition_broadcast(P)).then_inc(weights_in, 16)
            sp.dma_start(b_out[:, 1], T.bo.partition_broadcast(P)).then_inc(weights_in, 16)

            def load(g):
                sp.dma_start(x[:], x_rows[g]).then_inc(acts_in, 16)
                sp.dma_start(agg[:], agg_rows[g]).then_inc(acts_in, 16)
                sp.dma_start(qT[:], q_cols[g]).then_inc(acts_in, 16)

            load(0)
            sp.sem_inc(y_free, 1)
            with sp.Fori(1, NG) as g:
                sp.wait_ge(x1_ready, g * S)
                load(g)
                sp.wait_ge(y_added, g * (S * (E + 1)) + 1)
                sp.dma_start(out_rows[g - 1], y[:]).then_inc(out_done, 16)
                sp.wait_ge(out_done, g * 16)
                sp.sem_inc(y_free, 1)
            sp.wait_ge(y_added, NG * S * (E + 1) + 1)
            sp.dma_start(out_rows[NG - 1], y[:]).then_inc(out_done, 16)
            sp.wait_ge(out_done, 16 * NG)

        @block.gpsimd
        def _(pool):
            pool.iota(eight_i[:], [[1, E]], base=0, channel_multiplier=0)
            pool.memset(half[:], -0.5).then_inc(made, 1)
            pool.wait_ge(made, 1)
            pool.tensor_copy(eight[:], eight_i[:])
            pool.wait_ge(weights_in, 16 * NW)
            pool.tensor_tensor(bias[:], b_out[:, 0], b_out[:, 1], ALU.add).then_inc(ready, 1)
            pool.wait_ge(ready, 1)
            with pool.Fori(0, NG) as g:
                pool.wait_ge(acts_in, g * NACT + NACT)
                for s in range(S):
                    last = pool.tensor_tensor(x[:, s], x[:, s], bias[0:R], ALU.add)
                last.then_inc(bias_added, 1)
                for n in range(2):
                    pool.wait_ge(mv_ready, g * 2 + n + 1)
                    pool.sem_inc(T.passed, 1)
                    pool.tensor_scalar(var[:], mv[:, :, 1], EPS, None, ALU.add).then_inc(var_ready, 1)
                    pool.wait_ge(var_ready, g * 2 + n + 1)
                    pool.tensor_tensor(rstd[:], var[:], half[:], ALU.pow).then_inc(rstd_ready, 1)

        @block.tensor
        def _(pe):
            pe.wait_ge(weights_in, 16 * NW)
            pe.transpose(bank[0][:, 0:E * M], b1_rows[:], T.ident[0:E * M, 0:E * M]).then_inc(wgt_turned, 1)
            pe.wait_ge(b1_ready, 1)
            with pe.Fori(0, NG) as g:
                pe.wait_ge(acts_in, g * NACT + NACT)
                pe.wait_ge(y_added, g * (S * (E + 1)) + 1)
                for k in range(K):
                    for s in range(S):
                        mm = pe.transpose(bank[k][:, s * R:(s + 1) * R], agg[:, s, k * P:(k + 1) * P], T.ident[0:R, 0:R])
                    mm.then_inc(agg_turned, 1)
                for k in range(K):
                    pe.matmul(bank[2 + k][:, 0:G], T.kv[:, k], qT[:, k], start=True, stop=True)
                    pe.matmul(bank[4 + k][:, 0:G], T.ksum[:, k], qT[:, k], start=True, stop=True).then_inc(lin_ready, 1)
                pe.wait_ge(aggT_ready, g * K + K)
                pe.wait_ge(oT_ready, g * K + K)
                for s in range(S):
                    half_bank = bank[6 + s // 2][0:R, (s % 2) * D:(s % 2 + 1) * D]
                    for k in range(K):
                        pe.matmul(half_bank, aggT[:, k, s * R:(s + 1) * R], T.w_fcT[:, k], start=k == 0, stop=False)
                    for k in range(K):
                        mm = pe.matmul(half_bank, oT[:, k, s * R:(s + 1) * R], w_o[:, k], start=False, stop=k == K - 1)
                    if s % 2:
                        mm.then_inc(x1_mm, 1)
                pe.wait_ge(xn_ready, g * 2 + 2)
                for k in range(K):
                    for s in range(S):
                        mm = pe.transpose(bank[k][:, s * R:(s + 1) * R], xn[:, s, k * P:(k + 1) * P], T.ident[0:R, 0:R])
                    mm.then_inc(xn_turned, 1)
                pe.wait_ge(xhT_ready, g * K + K)
                for s in range(S):
                    for k in range(K):
                        mm = pe.matmul(bank[2][0:R, s * E:(s + 1) * E], xhT[:, k, s * R:(s + 1) * R], w_r[:, k],
                                       start=k == 0, stop=k == K - 1)
                mm.then_inc(logit_mm, 1)

                def hidden(e):
                    for i in range(M):
                        n = e * M + i
                        if n >= 2:
                            pe.wait_ge(hid_ready, g * (E * M) + n - 1)
                        for k in range(K):
                            mm = pe.matmul(bank[4 + n % 2][:, 0:G], w1[:, e, k, i * P:(i + 1) * P], xhT[:, k],
                                           start=k == 0, stop=k == K - 1)
                        mm.then_inc(hid_mm, 1)

                def project_out(e):
                    pe.wait_ge(hid_ready, g * (E * M) + (e + 1) * M)
                    for s in range(S):
                        if s % 2 == 0:
                            pe.wait_ge(y_added, g * (S * (E + 1)) + e * S + s + 3)
                        for i in range(M):
                            mm = pe.matmul(bank[6 + s // 2][0:R, (s % 2) * D:(s % 2 + 1) * D],
                                           hid[:, e % 2, i, s * R:(s + 1) * R], w2[:, e, i], start=i == 0, stop=i == M - 1)
                        if s % 2:
                            mm.then_inc(y_mm, 1)

                hidden(0)
                pe.wait_ge(wgt_ready, g + 1)
                for s in range(S):
                    mm = pe.transpose(bank[3][0:E, s * R:(s + 1) * R], wgt[:, s], T.ident[0:R, 0:R])
                mm.then_inc(wgt_turned, 1)
                pe.wait_ge(wgtT_ready, g + 1)
                for s in range(S):
                    mm = pe.matmul(bank[6 + s // 2][0:R, (s % 2) * D:(s % 2 + 1) * D], wgtT[:, s], b2[:], start=True, stop=True)
                    if s % 2:
                        mm.then_inc(y0_mm, 1)
                for e in range(1, E):
                    hidden(e)
                    project_out(e - 1)
                project_out(E - 1)

        @block.scalar
        def _(act):
            act.wait_ge(b1_ready, 1)
            with act.Fori(0, NG) as g:
                for k in range(K):
                    act.wait_ge(agg_turned, g * K + k + 1)
                    act.copy(aggT[:, k], bank[k][:, 0:G]).then_inc(aggT_ready, 1)
                act.wait_ge(route, g * 5 + 4)
                act.activation(odds[:], gap[:], ACT.Exp).then_inc(odds_ready, 1)
                for n in range(E * M):
                    e, i = n // M, n % M
                    act.wait_ge(hid_mm, g * (E * M) + n + 1)
                    if e >= 2 and i == 0:
                        act.wait_ge(y_mm, g * (E * S // 2) + (e - 1) * (S // 2))
                    act.activation(hid[:, e % 2, i], bank[4 + n % 2][:, 0:G], ACT.Gelu, bias=b1[:, e, i:i + 1]).then_inc(hid_ready, 1)

        @block.vector
        def _(dve):
            dve.wait_ge(wgt_turned, 1)
            dve.tensor_copy(b1[:].rearrange("p e m -> p (e m)"), bank[0][:, 0:E * M]).then_inc(b1_ready, 1)
            dve.wait_ge(weights_in, 16 * NW)
            dve.wait_ge(b1_ready, 1)
            dve.sem_inc(y_added, 1)

            with dve.Fori(0, NG) as g:
                for k in range(K):
                    dve.wait_ge(lin_ready, g * K + k + 1)
                    dve.tensor_scalar(den[:, k], bank[4 + k][:, 0:G], 1e-6, None, ALU.add).then_inc(den_ready, 1)
                    dve.wait_ge(den_ready, g * (2 * K) + 2 * k + 1)
                    dve.reciprocal(den[:, k], den[:, k]).then_inc(den_ready, 1)
                    dve.wait_ge(den_ready, g * (2 * K) + 2 * k + 2)
                    dve.tensor_tensor(oT[:, k], bank[2 + k][:, 0:G], den[:, k], ALU.mult).then_inc(oT_ready, 1)
                dve.wait_ge(bias_added, g + 1)
                for s in range(S):
                    if s % 2 == 0:
                        dve.wait_ge(x1_mm, g * 2 + s // 2 + 1)
                    dve.tensor_tensor(x1[:, s], x[:, s], bank[6 + s // 2][0:R, (s % 2) * D:(s % 2 + 1) * D], ALU.add).then_inc(x1_ready, 1)

                for n, rows in ((0, x1), (1, xn)):
                    dve.wait_ge(x1_ready, g * S + S)
                    for s in range(S):
                        last = dve.bn_stats(stats[:, s], rows[:, s])
                    last.then_inc(ln, 1)
                    dve.wait_ge(ln, g * 2 + n + 1)
                    dve.sem_inc(T.passed, 1)
                    for s in range(S):
                        last = dve.bn_aggr(mv[:, s], stats[:, s])
                    last.then_inc(mv_ready, 1)
                    dve.wait_ge(rstd_ready, g * 2 + n + 1)
                    for s in range(S):
                        last = dve.tensor_scalar(xn[:, s], rows[:, s], mv[:, s, 0:1], rstd[:, s:s + 1], ALU.subtract, ALU.mult)
                    last.then_inc(xn_ready, 1)
                    dve.wait_ge(xn_ready, g * 2 + n + 1)
                for k in range(K):
                    dve.wait_ge(xn_turned, g * K + k + 1)
                    dve.tensor_scalar(xhT[:, k], bank[k][:, 0:G], gamma[:, k:k + 1], beta[:, k:k + 1], ALU.mult, ALU.add).then_inc(xhT_ready, 1)

                dve.wait_ge(logit_mm, g + 1)
                dve.tensor_tensor(logit[:], bank[2][0:R, 0:S * E].rearrange("p (s e) -> p s e", e=E),
                                  b_r[0:R].unsqueeze(1).broadcast_to([R, S, E]), ALU.add).then_inc(route, 1)
                dve.wait_ge(route, g * 5 + 1)
                dve.sem_inc(T.passed, 1)
                for s in range(S):
                    last = dve.max(top[:, s], logit[:, s])
                last.then_inc(route, 1)
                dve.wait_ge(route, g * 5 + 2)
                dve.sem_inc(T.passed, 1)
                for s in range(S):
                    last = dve.max_index(top_i[:, s], top[:, s], logit[:, s])
                last.then_inc(route, 1)
                dve.tensor_tensor(gap[:], top[:, :, 1], top[:, :, 0], ALU.subtract).then_inc(route, 1)
                dve.wait_ge(route, g * 5 + 4)
                dve.tensor_copy(top_f[:], top_i[:]).then_inc(route, 1)
                dve.wait_ge(odds_ready, g + 1)
                dve.tensor_scalar(both[:], odds[:], 1.0, None, ALU.add).then_inc(wgt_chain, 1)
                dve.wait_ge(wgt_chain, g * 4 + 1)
                dve.reciprocal(gate[:, 0], both[:]).then_inc(wgt_chain, 1)
                dve.wait_ge(wgt_chain, g * 4 + 2)
                dve.tensor_tensor(gate[:, 1], gate[:, 0], odds[:], ALU.mult).then_inc(wgt_chain, 1)
                dve.wait_ge(wgt_chain, g * 4 + 3)
                dve.wait_ge(route, g * 5 + 5)
                for c in range(2):
                    for s in range(S):
                        last = dve.tensor_scalar(pick[:, c, s], eight[0:R], top_f[:, s, c:c + 1], gate[:, c, s:s + 1],
                                                 ALU.is_equal, ALU.mult)
                last.then_inc(wgt_chain, 1)
                dve.wait_ge(wgt_chain, g * 4 + 4)
                dve.tensor_tensor(wgt[:], pick[:, 0], pick[:, 1], ALU.add).then_inc(wgt_ready, 1)
                dve.wait_ge(wgt_turned, g + 2)
                dve.tensor_copy(wgtT[:].rearrange("e s r -> e (s r)"), bank[3][0:E, 0:G]).then_inc(wgtT_ready, 1)

                dve.wait_ge(y_free, g + 1)
                for s in range(S):
                    if s % 2 == 0:
                        dve.wait_ge(y0_mm, g * 2 + s // 2 + 1)
                    dve.tensor_tensor(y[:, s], x1[:, s], bank[6 + s // 2][0:R, (s % 2) * D:(s % 2 + 1) * D], ALU.add).then_inc(y_added, 1)
                for e in range(E):
                    for s in range(S):
                        if s % 2 == 0:
                            dve.wait_ge(y_mm, g * (E * S // 2) + e * (S // 2) + s // 2 + 1)
                        dve.wait_ge(y_added, g * (S * (E + 1)) + (e * S + s + 2))
                        dve.scalar_tensor_tensor(out=y[:, s], in0=bank[6 + s // 2][0:R, (s % 2) * D:(s % 2 + 1) * D],
                                                 scalar=wgt[:, s, e:e + 1], in1=y[:, s], op0=ALU.mult, op1=ALU.add).then_inc(y_added, 1)


class Tensors:

    def __init__(self, out, x, src, dst, W_s, W_t, W_attn, W_fc, b_fc, wq, bq, wk, bk, wv, bv, wo, bo,
                 gamma, beta, Wr, br, W1, b1, W2, b2):
        self.out, self.x, self.src, self.dst = out, x, src, dst
        self.W_s, self.W_t, self.W_attn, self.W_fc, self.b_fc = W_s, W_t, W_attn, W_fc, b_fc
        self.wq, self.bq, self.wk, self.bk, self.wv, self.bv, self.wo, self.bo = wq, bq, wk, bk, wv, bv, wo, bo
        self.gamma, self.beta, self.Wr, self.br = gamma, beta, Wr, br
        self.W1, self.b1, self.W2, self.b2 = W1, b1, W2, b2


def build(nc, out, **arrays):
    T = Tensors(out, **arrays)
    N = T.x.shape[0]
    T.NB = -(-N // P)
    T.xn_table = nc.dram_tensor("xn_table", [T.NB * P, XW], F32).ap()
    T.ps_table = nc.dram_tensor("ps_table", [N, D], F32).ap()
    T.pt_table = nc.dram_tensor("pt_table", [N, D], F32).ap()
    T.e_flat = nc.dram_tensor("e_flat", [T.src.shape[0]], F32).ap()
    T.agg = nc.dram_tensor("agg", [T.NB * P, D], F32).ap()
    T.q_table = nc.dram_tensor("q_table", [K, P, N], F32).ap()
    with ExitStack() as ctx:
        m = Memory(nc, ctx, "all")
        T.ident = m.sb("ident", [P, P])
        T.w_fcT = m.sb("w_fcT", [P, K, D])
        T.kv = m.sb("kv", [P, K, P])
        T.ksum = m.sb("ksum", [P, K, P])
        T.e = m.sb("e", [R, T.src.shape[0] // R])
        T.shift = m.sb("shift", [P, T.NB, 2])
        T.plan = m.sb("plan", [1, 3, T.src.shape[0] // C + 1], I32)
        T.far_i = m.sb("far_i", [1, 1], I32)
        T.passed = m.sem("passed")
        for step in STEPS:
            step(nc, T)


STEPS = [project, score, plan, reshift, aggregate, finish]


_INS = {
    "x": "x", "src": "src", "dst": "dst", "L0_gnn_W_s": "W_s", "L0_gnn_W_t": "W_t", "L0_gnn_W_attn": "W_attn",
    "L0_gnn_W_fc": "W_fc", "L0_gnn_b_fc": "b_fc", "L0_mix_wq": "wq", "L0_mix_bq": "bq", "L0_mix_wk": "wk",
    "L0_mix_bk": "bk", "L0_mix_wv": "wv", "L0_mix_bv": "bv", "L0_mix_wo": "wo", "L0_mix_bo": "bo",
    "L0_ffn_gamma": "gamma", "L0_ffn_beta": "beta", "L0_ffn_Wr": "Wr", "L0_ffn_br": "br", "L0_ffn_W1": "W1",
    "L0_ffn_b1": "b1", "L0_ffn_W2": "W2", "L0_ffn_b2": "b2",
}


def kernel(**inputs):
    import numpy as np
    import concourse.bacc as bacc
    from concourse.bass_utils import run_bass_kernel_spmd

    nc = bacc.Bacc("TRN2", target_bir_lowering=False, num_devices=1)
    arrays, args = {}, {}
    for name, short in _INS.items():
        a = np.ascontiguousarray(inputs[name])
        arrays[f"in_{short}"] = a
        args[short] = nc.dram_tensor(f"in_{short}", a.shape, mybir.dt.from_np(a.dtype), kind="ExternalInput").ap()
    out = nc.dram_tensor("out_x", inputs["x"].shape, F32, kind="ExternalOutput").ap()
    build(nc, out, **args)
    r = run_bass_kernel_spmd(nc, [arrays], core_ids=[0])
    return r.results[0]["out_x"]
```

```python
from contextlib import ExitStack

import concourse.bass as bass
from concourse import mybir

ALU = mybir.AluOpType
ACT = mybir.ActivationFunctionType
AX = mybir.AxisListType
F32 = mybir.dt.float32
I32 = mybir.dt.int32
U32 = mybir.dt.uint32

P = 128
R = 125
S = 4
G = R * S
D = 256
K = D // P
HEADS = 8
HD = D // HEADS
J = 16
C = R * J
Q = 4
XW = D + 2
BLK = 512
CAP = 26 * BLK
FULL, BLOCKS = 48, 56
SLOPE = 0.2
SAFE = 60.0
FAR = 1.6e38
EPS = 1e-5


class Memory:

    def __init__(self, nc, ctx, prefix):
        self.nc, self.ctx, self.prefix, self.sems = nc, ctx, prefix, []
        ctx.callback(self.clear)

    def clear(self):
        self.nc.clear_and_free_semaphores(self.sems)
        self.nc.all_engine_barrier()

    def sb(self, name, shape, dt=F32):
        return self.ctx.enter_context(self.nc.sbuf_tensor(f"{self.prefix}_{name}", shape, dt))

    def ps(self, name, shape, dt=F32):
        return self.ctx.enter_context(self.nc.psum_tensor(f"{self.prefix}_{name}", shape, dt))

    def sem(self, name):
        self.sems.append(self.nc.alloc_semaphore(f"{self.prefix}_{name}"))
        return self.sems[-1]


def project(nc, T):
    NG = T.x.shape[0] // G
    with ExitStack() as ctx:
        m = Memory(nc, ctx, "pj")
        sb, ps, sem = m.sb, m.ps, m.sem
        w_raw = sb("w_raw", [P, 3, K, D])
        w_st = sb("w_st", [P, K, 2, D])
        w_kv = sb("w_kv", [P, K, 2, D])
        w_q = sb("w_q", [P, K, D])
        b_kv = sb("b_kv", [P, 2, D])
        b_q = sb("b_q", [P, K])
        x = sb("x", [R, 2, S, D])
        xn = sb("xn", [R, 2, S, D])
        stats = sb("stats", [R, S, 6])
        mv = sb("mv", [R, S, 2])
        var = sb("var", [R, S])
        half = sb("half", [R, S])
        rstd = sb("rstd", [R, S])
        xnT = sb("xnT", [P, K, G])
        proj = sb("proj", [R, 2, S, 2, D])
        kb = sb("kb", [R, 2, D])
        kpos = sb("kpos", [R, 2, D])
        kexp = sb("kexp", [R, 2, D])
        kf = sb("kf", [R, 2, S, D])
        v1 = sb("v1", [R, 2, S, K, P + 1])
        qpos = sb("qpos", [P, K, G])
        qexp = sb("qexp", [P, K, G])
        qf = sb("qf", [P, 2, K, G])
        zero = sb("zero", [R, 2 * (P + 1)])

        tp = ps("tp", [P, K, 512])
        p1 = ps("p1", [P, 2, 512])
        p2 = ps("p2", [P, 2, 512])
        pq = ps("pq", [P, 512])
        pkv = ps("pkv", [P, 512])

        weights_in = sem("weights_in")
        ident_zeroed, ident_ready, consts_ready = sem("ident_zeroed"), sem("ident_ready"), sem("consts_ready")
        w_turned, w_copied = sem("w_turned"), sem("w_copied")
        x_in = [sem(f"x_in{b}") for b in range(2)]
        var_ready = sem("var_ready")
        stats_ready, mv_ready, rstd_ready, xn_ready = sem("stats_ready"), sem("mv_ready"), sem("rstd_ready"), sem("xn_ready")
        xn_stored = [sem(f"xn_stored{b}") for b in range(2)]
        xn_turned, xnT_ready = sem("xn_turned"), sem("xnT_ready")
        p1_ready, p1_copied, p2_ready, p2_copied = sem("p1_ready"), sem("p1_copied"), sem("p2_ready"), sem("p2_copied")
        proj_stored = [sem(f"proj_stored{b}") for b in range(2)]
        kexp_ready, kpos_ready, kf_ready, kv_added = sem("kexp_ready"), sem("kpos_ready"), sem("kf_ready"), sem("kv_added")
        pq_ready, pq_read, qf_ready = sem("pq_ready"), sem("pq_read"), sem("qf_ready")
        q_stored = [sem(f"q_stored{b}") for b in range(2)]
        kv_cleared, kv_out = sem("kv_cleared"), sem("kv_out")

        block = ctx.enter_context(nc.Block())
        x_rows = T.x.rearrange("(g s p) d -> g p s d", s=S, p=R)
        xn_rows = T.xn_table[0:NG * G, :].rearrange("(g s p) d -> g p s d", s=S, p=R)
        ps_rows = T.ps_table.rearrange("(g s p) d -> g p s d", s=S, p=R)
        pt_rows = T.pt_table.rearrange("(g s p) d -> g p s d", s=S, p=R)
        q_cols = T.q_table.rearrange("k p (g n) -> g p k n", n=G)

        def steps(eng, body):
            body(0, 0, 0)
            body(1, 1, 0)
            body(2, 0, 1)
            with eng.Fori(1, (NG - 1) // 2) as i:
                body(i * 2 + 1, 1, i)
                body(i * 2 + 2, 0, i + 1)

        @block.sync
        def _(sp):
            for n, w in enumerate((T.W_s, T.W_t, T.W_fc)):
                sp.dma_start(w_raw[:, n], w.rearrange("(c p) i -> p c i", p=P)).then_inc(weights_in, 16)
            for n, w in enumerate((T.wk, T.wv)):
                sp.dma_start(w_kv[:, :, n, :], w.rearrange("(c p) o -> p c o", p=P)).then_inc(weights_in, 16)
            sp.dma_start(w_q[:], T.wq.rearrange("(c p) o -> p c o", p=P)).then_inc(weights_in, 16)
            for n, b in enumerate((T.bk, T.bv)):
                sp.dma_start(b_kv[:, n, :], b.partition_broadcast(P)).then_inc(weights_in, 16)
            for k in range(K):
                sp.dma_start(b_q[:, k:k + 1], T.bq[k * P:(k + 1) * P].rearrange("(p a) -> p a", a=1)).then_inc(weights_in, 16)

            def step(g, b, u):
                if not (isinstance(g, int) and g < 2):
                    sp.wait_ge(xn_ready, g - 1)
                sp.dma_start(x[:, b], x_rows[g]).then_inc(x_in[b], 16)
                if not (isinstance(g, int) and g < 1):
                    c = 1 - b
                    sp.wait_ge(xn_ready, g)
                    sp.dma_start(xn_rows[g - 1, :, :, 0:D], xn[:, c]).then_inc(xn_stored[c], 16)

            steps(sp, step)
            sp.wait_ge(xn_ready, NG)
            sp.dma_start(xn_rows[NG - 1, :, :, 0:D], xn[:, (NG - 1) % 2]).then_inc(xn_stored[(NG - 1) % 2], 16)
            for b in range(2):
                n = (NG + 1 - b) // 2
                sp.wait_ge(xn_stored[b], 16 * n)
                sp.wait_ge(proj_stored[b], 32 * n)
                sp.wait_ge(q_stored[b], 16 * n)

        @block.gpsimd
        def _(pool):
            pool.memset(T.ident[:], 0.0).then_inc(ident_zeroed, 1)
            pool.wait_ge(ident_zeroed, 1)
            pool.affine_select(out=T.ident[:], in_=T.ident[:], compare_op=ALU.not_equal, fill=1.0, base=0,
                               pattern=[[-1, P]], channel_multiplier=1).then_inc(ident_ready, 1)
            pool.memset(v1[:], 1.0)
            pool.memset(half[:], -0.5)
            pool.memset(zero[:], 0.0).then_inc(consts_ready, 1)

            def step(g, b, u):
                pool.wait_ge(mv_ready, g + 1)
                pool.sem_inc(T.passed, 1)
                pool.tensor_scalar(var[:], mv[:, :, 1], EPS, None, ALU.add).then_inc(var_ready, 1)
                pool.wait_ge(var_ready, g + 1)
                pool.tensor_tensor(rstd[:], var[:], half[:], ALU.pow).then_inc(rstd_ready, 1)

            steps(pool, step)

        @block.tensor
        def _(pe):
            pe.wait_ge(consts_ready, 1)
            pe.wait_ge(ident_ready, 1)
            pe.matmul(pkv[:, 0:2 * (P + 1)], zero[:, 0:P], zero[:], start=True, stop=False,
                      skip_group_check=True).then_inc(kv_cleared, 1)
            pe.wait_ge(weights_in, 16 * 10)
            n = 0
            for w in range(3):
                for i in range(K):
                    for o in range(K):
                        if n >= 2:
                            pe.wait_ge(w_copied, n - 1)
                        pe.transpose(tp[:, n % 2, 0:P], w_raw[:, w, o, i * P:(i + 1) * P], T.ident[:]).then_inc(w_turned, 1)
                        n += 1
            pe.wait_ge(w_copied, n)

            def add_kv(g, b, s):
                pe.wait_ge(kf_ready, g * S + s + 1)
                for k in range(K):
                    mm = pe.matmul(pkv[:, k * (P + 1):(k + 1) * (P + 1)], kf[:, b, s, k * P:(k + 1) * P],
                                   v1[:, b, s, k, :], start=False, stop=False, skip_group_check=True)
                mm.then_inc(kv_added, 1)

            def step(g, b, u):
                first = isinstance(g, int) and g == 0
                pe.wait_ge(xn_ready, g + 1)
                for k in range(K):
                    if not first:
                        pe.wait_ge(xnT_ready, g * K)
                    for s in range(S):
                        t = pe.transpose(tp[:, k, s * R:(s + 1) * R], xn[:, b, s, k * P:(k + 1) * P], T.ident[0:R, 0:R])
                    t.then_inc(xn_turned, 1)
                pe.wait_ge(xnT_ready, g * K + K)
                for s in range(S):
                    for out, w, ready, copied in ((p1, w_st, p1_ready, p1_copied), (p2, w_kv, p2_ready, p2_copied)):
                        if not (first and s < 2):
                            pe.wait_ge(copied, g * S + s - 1)
                        for k in range(K):
                            mm = pe.matmul(out[0:R, s % 2, :], xnT[:, k, s * R:(s + 1) * R],
                                           w[:, k].rearrange("p a d -> p (a d)"), start=k == 0, stop=k == K - 1)
                        mm.then_inc(ready, 1)
                for h in range(K):
                    if not (first and h == 0):
                        pe.wait_ge(pq_read, (g * K + h) * 2)
                    for k in range(K):
                        mm = pe.matmul(pq[:, 0:G], w_q[:, k, h * P:(h + 1) * P], xnT[:, k, :], start=k == 0, stop=k == K - 1)
                    mm.then_inc(pq_ready, 1)
                if not first:
                    for s in range(S):
                        add_kv(g - 1, 1 - b, s)

            steps(pe, step)
            for s in range(S):
                add_kv(NG - 1, (NG - 1) % 2, s)

        @block.scalar
        def _(act):
            act.wait_ge(weights_in, 16 * 10)

            def step(g, b, u):
                first = isinstance(g, int) and g == 0
                for k in range(K):
                    act.wait_ge(xn_turned, g * K + k + 1)
                    act.copy(xnT[:, k, :], tp[:, k, 0:G]).then_inc(xnT_ready, 1)
                if not (isinstance(g, int) and g < 2):
                    act.wait_ge(proj_stored[b], 32 * u)
                for s in range(S):
                    act.wait_ge(p1_ready, g * S + s + 1)
                    act.copy(proj[:, b, s].rearrange("p a d -> p (a d)"), p1[0:R, s % 2, :]).then_inc(p1_copied, 1)
                    act.wait_ge(p2_copied, g * S + s + 1)
                    if not (first and s < 2):
                        act.wait_ge(kf_ready, g * S + s - 1)
                    act.activation(kexp[:, s % 2], kb[:, s % 2], ACT.Exp).then_inc(kexp_ready, 1)
                for h in range(K):
                    act.wait_ge(pq_ready, g * K + h + 1)
                    if not first:
                        act.wait_ge(qf_ready, g * K + h - K + 1)
                    act.activation(qexp[:, h, :], pq[:, 0:G], ACT.Exp, bias=b_q[:, h:h + 1]).then_inc(pq_read, 1)
                act.wait_ge(p1_copied, g * S + S)
                act.dma_start(ps_rows[g], proj[:, b, :, 0, :]).then_inc(proj_stored[b], 16)
                act.dma_start(pt_rows[g], proj[:, b, :, 1, :]).then_inc(proj_stored[b], 16)
                act.wait_ge(qf_ready, g * K + K)
                act.dma_start(q_cols[g], qf[:, b]).then_inc(q_stored[b], 16)

            steps(act, step)

        @block.vector
        def _(dve):
            n = 0
            for w in range(3):
                for i in range(K):
                    for o in range(K):
                        dve.wait_ge(w_turned, n + 1)
                        dst = T.w_fcT[:, i, o * P:(o + 1) * P] if w == 2 else w_st[:, i, w, o * P:(o + 1) * P]
                        dve.tensor_copy(dst, tp[:, n % 2, 0:P]).then_inc(w_copied, 1)
                        n += 1
            dve.wait_ge(weights_in, 16 * 10)
            dve.wait_ge(consts_ready, 1)

            def norm(g, b, u):
                dve.wait_ge(x_in[b], u * 16 + 16)
                if not (isinstance(g, int) and g == 0):
                    dve.wait_ge(mv_ready, g)
                for s in range(S):
                    last = dve.bn_stats(stats[:, s, :], x[:, b, s, :])
                last.then_inc(stats_ready, 1)
                dve.wait_ge(stats_ready, g + 1)
                if not (isinstance(g, int) and g == 0):
                    dve.wait_ge(xn_ready, g)
                dve.sem_inc(T.passed, 1)
                for s in range(S):
                    last = dve.bn_aggr(mv[:, s, :], stats[:, s, :])
                last.then_inc(mv_ready, 1)
                dve.wait_ge(rstd_ready, g + 1)
                if not (isinstance(g, int) and g < 2):
                    dve.wait_ge(xn_stored[b], 16 * u)
                    dve.wait_ge(xn_turned, (g - 1) * K)
                for s in range(S):
                    last = dve.tensor_scalar(xn[:, b, s, :], x[:, b, s, :], mv[:, s, 0:1], rstd[:, s:s + 1], ALU.subtract, ALU.mult)
                last.then_inc(xn_ready, 1)

            def keys(g, b, u):
                first = isinstance(g, int) and g == 0
                if not (isinstance(g, int) and g < 2):
                    dve.wait_ge(kv_added, (g - 1) * S)

                def feature(s):
                    dve.wait_ge(kexp_ready, g * S + s + 1)
                    dve.wait_ge(kpos_ready, g * S + s + 1)
                    dve.scalar_tensor_tensor(out=kf[:, b, s, :], in0=kexp[:, s % 2], scalar=1.0, in1=kpos[:, s % 2],
                                             op0=ALU.min, op1=ALU.add).then_inc(kf_ready, 1)

                for s in range(S):
                    dve.wait_ge(p2_ready, g * S + s + 1)
                    dve.tensor_tensor(v1[:, b, s, :, 0:P], p2[0:R, s % 2, D:2 * D].rearrange("p (k d) -> p k d", k=K),
                                      b_kv[0:R, 1, :].rearrange("p (k d) -> p k d", k=K), ALU.add)
                    if not (first and s < 2):
                        dve.wait_ge(kf_ready, g * S + s - 1)
                        dve.wait_ge(kpos_ready, g * S + s - 1)
                    dve.tensor_tensor(kb[:, s % 2], p2[0:R, s % 2, 0:D], b_kv[0:R, 0, :], ALU.add).then_inc(p2_copied, 1)
                    dve.wait_ge(p2_copied, g * S + s + 1)
                    dve.tensor_scalar(kpos[:, s % 2], kb[:, s % 2], 0.0, None, ALU.max).then_inc(kpos_ready, 1)
                    if s >= 1:
                        feature(s - 1)
                feature(S - 1)
                if not (isinstance(g, int) and g < 2):
                    dve.wait_ge(q_stored[b], 16 * u)
                for h in range(K):
                    dve.wait_ge(pq_read, (g * K + h) * 2 + 1)
                    if not first:
                        dve.wait_ge(qf_ready, g * K + h - K + 1)
                    dve.tensor_scalar(qpos[:, h, :], pq[:, 0:G], b_q[:, h:h + 1], 0.0, ALU.add, ALU.max).then_inc(pq_read, 1)
                    dve.wait_ge(pq_read, (g * K + h + 1) * 2)
                    dve.scalar_tensor_tensor(out=qf[:, b, h, :], in0=qexp[:, h, :], scalar=1.0, in1=qpos[:, h, :],
                                             op0=ALU.min, op1=ALU.add).then_inc(qf_ready, 1)

            norm(0, 0, 0)
            norm(1, 1, 0)
            keys(0, 0, 0)
            norm(2, 0, 1)
            keys(1, 1, 0)
            with dve.Fori(1, (NG - 1) // 2) as i:
                norm(i * 2 + 1, 1, i)
                keys(i * 2, 0, i)
                norm(i * 2 + 2, 0, i + 1)
                keys(i * 2 + 1, 1, i)
            keys(NG - 1, (NG - 1) % 2, (NG - 1) // 2)
            dve.memset(T.kv[:], 0.0)
            dve.memset(T.ksum[:], 0.0).then_inc(kv_out, 1)
            dve.wait_ge(kv_out, 1)
            dve.wait_ge(kv_added, NG * S)
            for k in range(K):
                for h in range(P // HD):
                    a, z = h * HD, (h + 1) * HD
                    dve.tensor_copy(T.kv[a:z, k, a:z], pkv[a:z, k * (P + 1) + a:k * (P + 1) + z])
                    dve.tensor_copy(T.ksum[a:z, k, a:z], pkv[a:z, k * (P + 1) + P:k * (P + 1) + P + 1].broadcast_to([HD, HD]))
            


def score(nc, T):
    E = T.src.shape[0]
    NC = E // C
    NQ = J // Q
    LO = P.bit_length() - 1
    with ExitStack() as ctx:
        m = Memory(nc, ctx, "sc")
        sb, ps, sem = m.sb, m.ps, m.sem
        src_i = sb("src_i", [R, 2, J], I32)
        dst_i = sb("dst_i", [R, 2, J], I32)
        w_attn = sb("w_attn", [P, D])
        rows_i = sb("rows_i", [R, P], I32)
        iota = sb("iota", [R, P])
        src_p = sb("src_p", [R, 2, Q, D])
        dst_p = sb("dst_p", [R, 2, Q, D])
        z = sb("z", [R, 2, Q, D])
        lk = sb("lk", [R, 2, Q, D])
        e = sb("e", [R, 2, J])
        cut = sb("cut", [R, 2, J])
        ex = sb("ex", [R, 2, J])
        low_i = sb("low_i", [R, 2, 2, J], I32)
        low = sb("low", [R, 2, 2, J])
        hot_row = sb("hot_row", [R, 2, J, P])
        hot_blk = sb("hot_blk", [R, 2, J, T.NB])
        zero = sb("zero", [R, P])
        sums = sb("sums", [P, T.NB])
        total = ps("total", [P, 512])

        consts_in, iota_made, iota_ready = sem("consts_in"), sem("iota_made"), sem("iota_ready")
        idx_in = [sem(f"idx_in{b}") for b in range(2)]
        rows_in = [sem(f"rows_in{b}") for b in range(2)]
        z_ready, leaky_ready, dots_ready = sem("z_ready"), sem("leaky_ready"), sem("dots_ready")
        scores_kept, exp_ready, low_ready, lowf_ready = sem("scores_kept"), sem("exp_ready"), sem("low_ready"), sem("lowf_ready")
        cut_ready = sem("cut_ready")
        shift_ready = sem("shift_ready")
        hot_ready, hot_used = sem("hot_ready"), sem("hot_used")

        block = ctx.enter_context(nc.Block())
        src_c = T.src.rearrange("(c p j) -> c p j", p=R, j=J)
        dst_c = T.dst.rearrange("(c p j) -> c p j", p=R, j=J)

        @block.sync
        def _(sp):
            sp.dma_start(w_attn[:], T.W_attn.rearrange("a d -> (a d)").partition_broadcast(P)).then_inc(consts_in, 16)

            def load(c, b):
                if not isinstance(c, int):
                    sp.wait_ge(z_ready, (c - 1) * NQ)
                    sp.wait_ge(low_ready, c - 1)
                sp.dma_start(src_i[:, b], src_c[c]).then_inc(idx_in[b], 16)
                sp.dma_start(dst_i[:, b], dst_c[c]).then_inc(idx_in[b], 16)

            load(0, 0)
            load(1, 1)
            with sp.Fori(1, NC // 2) as i:
                load(i * 2, 0)
                load(i * 2 + 1, 1)

        @block.gpsimd
        def _(pool):
            pool.iota(rows_i[:], [[1, P]], base=0, channel_multiplier=0).then_inc(iota_made, 1)
            pool.memset(zero[:], 0.0)
            pool.wait_ge(iota_made, 1)
            pool.tensor_copy(iota[:], rows_i[:]).then_inc(iota_ready, 1)

            def gather(c, b, i, first):
                pool.wait_ge(idx_in[b], i * 32 + 32)
                for q in range(NQ):
                    h = q % 2
                    if not (first and q < 2):
                        pool.wait_ge(z_ready, c * NQ + q - 1)
                    pool.sem_inc(T.passed, 1)
                    for t in range(Q):
                        j = q * Q + t
                        for rows, table, idx in ((src_p, T.ps_table, src_i), (dst_p, T.pt_table, dst_i)):
                            pool.indirect_dma_start(
                                out=rows[:, h, t, :], out_offset=None, in_=table,
                                in_offset=bass.IndirectOffsetOnAxis(ap=idx[:, b, j:j + 1], axis=0),
                            ).then_inc(rows_in[h], 16)

            gather(0, 0, 0, True)
            gather(1, 1, 0, False)
            with pool.Fori(1, NC // 2) as i:
                gather(i * 2, 0, i, False)
                gather(i * 2 + 1, 1, i, False)

        @block.vector
        def _(dve):
            dve.wait_ge(consts_in, 16)
            dve.wait_ge(iota_ready, 1)

            def leaky(c, q, first):
                n, h, b = c * NQ + q, q % 2, q % 2
                dve.wait_ge(z_ready, n + 1)
                if not (first and q < 2):
                    dve.wait_ge(dots_ready, n - 1)
                dve.scalar_tensor_tensor(out=lk[:, h], in0=z[:, h], scalar=SLOPE, in1=z[:, h],
                                         op0=ALU.mult, op1=ALU.max).then_inc(leaky_ready, 1)

            def dots(c, q, b, first):
                n, h = c * NQ + q, q % 2
                dve.wait_ge(leaky_ready, n + 1)
                if q == 0 and not first:
                    dve.wait_ge(scores_kept, c - 1)
                for t in range(Q):
                    j = q * Q + t
                    last = dve.tensor_tensor_reduce(out=lk[:, h, t], in0=lk[:, h, t], in1=w_attn[0:R], scale=1.0, scalar=0.0,
                                                    op0=ALU.mult, op1=ALU.add, accum_out=e[:, b, j:j + 1])
                last.then_inc(dots_ready, 1)

            def cap(c, b, first):
                dve.wait_ge(dots_ready, (c + 1) * NQ)
                if not first:
                    dve.wait_ge(exp_ready, c - 1)
                dve.tensor_scalar(cut[:, b], e[:, b], SAFE, None, ALU.min).then_inc(cut_ready, 1)

            def hots(c, b, first):
                dve.wait_ge(exp_ready, c + 1)
                dve.wait_ge(lowf_ready, c + 1)
                if not first:
                    dve.wait_ge(hot_used, c - 1)
                for j in range(J):
                    dve.tensor_scalar(hot_row[:, b, j], iota[:], low[:, b, 0, j:j + 1], None, ALU.is_equal)
                    last = dve.tensor_scalar(hot_blk[:, b, j], iota[:, 0:T.NB], low[:, b, 1, j:j + 1], ex[:, b, j:j + 1],
                                             ALU.is_equal, ALU.mult)
                last.then_inc(hot_ready, 1)

            def chunk(c, b, i, first, start):
                for q in range(NQ):
                    h = q % 2
                    n = c * NQ + q
                    dve.wait_ge(rows_in[h], (c * (NQ // 2) + q // 2 + 1) * (2 * Q * 16))
                    if not (start and q < 2):
                        dve.wait_ge(leaky_ready, n - 1)
                    dve.tensor_tensor(z[:, h], src_p[:, h], dst_p[:, h], ALU.add).then_inc(z_ready, 1)
                    leaky(c, q, start)
                    dots(c, q, b, first)
                cap(c, b, first)
                if not first:
                    dve.wait_ge(lowf_ready, c - 1)
                dve.tensor_scalar(low_i[:, b, 0], src_i[:, b], P - 1, None, ALU.bitwise_and)
                dve.tensor_scalar(low_i[:, b, 1], src_i[:, b], LO, None, ALU.arith_shift_right).then_inc(low_ready, 1)
                dve.wait_ge(low_ready, c + 1)
                if not first:
                    dve.wait_ge(hot_ready, c - 1)
                dve.tensor_copy(low[:, b], low_i[:, b]).then_inc(lowf_ready, 1)

            chunk(0, 0, 0, True, True)
            chunk(1, 1, 0, True, False)
            hots(0, 0, True)
            chunk(2, 0, 1, False, False)
            hots(1, 1, True)
            chunk(3, 1, 1, False, False)
            hots(2, 0, False)
            with dve.Fori(2, NC // 2) as i:
                chunk(i * 2, 0, i, False, False)
                hots(i * 2 - 1, 1, False)
                chunk(i * 2 + 1, 1, i, False, False)
                hots(i * 2, 0, False)
            hots(NC - 1, 1, False)
            dve.memset(T.shift[:], 0.0).then_inc(shift_ready, 1)
            dve.wait_ge(shift_ready, 1)
            dve.wait_ge(hot_used, NC)
            dve.tensor_scalar(sums[:], total[:, 0:T.NB], 1e-37, None, ALU.max).then_inc(shift_ready, 1)
            dve.wait_ge(shift_ready, 2)
            dve.reciprocal(T.shift[:, :, 1], sums[:])

        @block.scalar
        def _(act):
            def exps(c, b, first):
                act.wait_ge(dots_ready, (c + 1) * NQ)
                if not first:
                    act.wait_ge(hot_ready, c - 1)
                act.copy(T.e[:, bass.ds(c * J, J)], e[:, b]).then_inc(scores_kept, 1)
                act.wait_ge(cut_ready, c + 1)
                act.activation(ex[:, b], cut[:, b], ACT.Exp).then_inc(exp_ready, 1)

            exps(0, 0, True)
            exps(1, 1, True)
            with act.Fori(1, NC // 2) as i:
                exps(i * 2, 0, False)
                exps(i * 2 + 1, 1, False)

        @block.tensor
        def _(pe):
            pe.wait_ge(iota_ready, 1)
            pe.matmul(total[:, 0:T.NB], zero[:, 0:P], zero[:, 0:T.NB], start=True, stop=False, skip_group_check=True)

            def add(c, b):
                pe.wait_ge(hot_ready, c + 1)
                for j in range(J):
                    mm = pe.matmul(total[:, 0:T.NB], hot_row[:, b, j], hot_blk[:, b, j], start=False, stop=False,
                                   skip_group_check=True)
                mm.then_inc(hot_used, 1)

            with pe.Fori(0, NC // 2) as i:
                add(i * 2, 0)
                add(i * 2 + 1, 1)


def plan(nc, T):
    NC = T.src.shape[0] // C
    LO = P.bit_length() - 1
    with ExitStack() as ctx:
        m = Memory(nc, ctx, "pl")
        sb, ps, sem = m.sb, m.ps, m.sem
        dst_i = sb("dst_i", [R, NC, J], I32)
        dst_f = sb("dst_f", [R, NC, J])
        low = sb("low", [R, 2, NC])
        chunk = sb("chunk", [NC, 2])
        row = sb("row", [1, 2, NC])
        row_i = sb("row_i", [1, 2, NC], I32)
        blk_i = sb("blk_i", [1, 2, NC], I32)
        blk = sb("blk", [1, 2, NC])
        count = sb("count", [1, NC])
        ones = sb("ones", [1, NC])
        before = sb("before", [1, NC])
        ext = sb("ext", [R, 2])
        extT = sb("extT", [1, 1])
        span = sb("span", [R, 1])
        far = sb("far", [1, 2])
        tp = ps("tp", [P, 2, 512])
        tq = ps("tq", [P, 2, 512])
        dst_in, chain, turned = sem("dst_in"), sem("step_done"), sem("turned")
        block = ctx.enter_context(nc.Block())

        @block.sync
        def _(sp):
            sp.dma_start(dst_i[:], T.dst.rearrange("(c p j) -> p c j", p=R, j=J)).then_inc(dst_in, 16)

        @block.tensor
        def _(pe):
            pe.wait_ge(chain, 4)
            for k in range(2):
                mm = pe.transpose(tp[0:NC, k, 0:R], low[:, k, :], T.ident[0:R, 0:R])
            mm.then_inc(turned, 1)
            pe.wait_ge(chain, 8)
            pe.transpose(tq[0:1, 1, 0:R], span[:], T.ident[0:R, 0:R]).then_inc(turned, 1)
            pe.wait_ge(chain, 10)
            for k in range(2):
                mm = pe.transpose(tq[0:1, 0, k * P:k * P + NC], chunk[:, k:k + 1], T.ident[0:NC, 0:NC])
            mm.then_inc(turned, 1)

        @block.vector
        def _(dve):
            done = 0

            def then(ins):
                nonlocal done
                done += 1
                ins.then_inc(chain, 1)
                dve.wait_ge(chain, done)

            dve.wait_ge(dst_in, 16)
            then(dve.tensor_copy(dst_f[:], dst_i[:]))
            then(dve.tensor_reduce(low[:, 0, :], dst_f[:], AX.X, ALU.max))
            then(dve.tensor_scalar(dst_f[:], dst_f[:], -1.0, None, ALU.mult))
            then(dve.tensor_reduce(low[:, 1, :], dst_f[:], AX.X, ALU.max))
            then(dve.tensor_reduce(ext[:, 0:1], T.e[:], AX.X, ALU.max))
            then(dve.tensor_reduce(ext[:, 1:2], T.e[:], AX.X, ALU.min))
            then(dve.tensor_scalar(span[:], ext[:, 1:2], -1.0, None, ALU.mult))
            then(dve.tensor_tensor(span[:], span[:], ext[:, 0:1], ALU.max))
            dve.wait_ge(turned, 1)
            then(dve.tensor_reduce(chunk[:, 0:1], tp[0:NC, 0, 0:R], AX.X, ALU.max))
            then(dve.tensor_reduce(chunk[:, 1:2], tp[0:NC, 1, 0:R], AX.X, ALU.max))
            dve.wait_ge(turned, 3)
            then(dve.tensor_reduce(extT[:], tq[0:1, 1, 0:R], AX.X, ALU.max))
            then(dve.tensor_scalar(T.far_i[:], extT[:], SAFE, None, ALU.is_gt))
            then(dve.tensor_copy(row[:, 0, :], tq[0:1, 0, 0:NC]))
            then(dve.tensor_scalar(row[:, 1, :], tq[0:1, 0, P:P + NC], -1.0, None, ALU.mult))
            then(dve.tensor_copy(row_i[:], row[:]))
            then(dve.tensor_scalar(blk_i[:], row_i[:], LO, None, ALU.arith_shift_right))
            then(dve.tensor_copy(blk[:], blk_i[:]))
            then(dve.tensor_tensor(count[:], blk[:, 0, :], blk[:, 1, :], ALU.subtract))
            then(dve.tensor_scalar(count[:], count[:], 1.0, None, ALU.add))
            then(dve.memset(ones[:], 1.0))
            then(dve.tensor_tensor_scan(before[:], ones[:], count[:], 0.0, ALU.mult, ALU.add))
            then(dve.memset(T.plan[:], 0))
            then(dve.tensor_copy(T.plan[:, 0, 1:NC + 1], blk[:, 0, :]))
            then(dve.tensor_copy(T.plan[:, 1, 0:NC], blk[:, 1, :]))
            then(dve.tensor_copy(T.plan[:, 2, 1:NC + 1], before[:]))


def reshift(nc, T):
    NC = T.src.shape[0] // C
    NB = T.NB
    with ExitStack() as ctx:
        m = Memory(nc, ctx, "rs")
        sb, sem = m.sb, m.sem
        src_i = sb("src_i", [P, C], I32)
        src_f = sb("src_f", [P, C])
        e = sb("e", [P, C])
        t = sb("t", [P, C])
        part = sb("part", [P, 1])
        node_i = sb("node_i", [P, NB], I32)
        node = sb("node", [P, NB])
        top = sb("top", [P, NB])
        total = sb("total", [P, NB])
        kept, chunk_in, chunk_used = sem("kept"), sem("chunk_in"), sem("chunk_used")
        made, ready, chain = sem("made"), sem("ready"), sem("chain")
        shifted, ex_ready = sem("shifted"), sem("ex_ready")

        block = ctx.enter_context(nc.Block())

        @block.sync
        def _(sp):
            far = sp.value_load(T.far_i[0:1, 0:1], min_val=0, max_val=1)
            with sp.If(far > 0):
                sp.dma_start(T.e_flat.rearrange("(c p j) -> p c j", p=R, j=J),
                             T.e[:].rearrange("p (c j) -> p c j", j=J)).then_inc(kept, 16)
                sp.wait_ge(kept, 16)
                for sweep in range(2):
                    with sp.Fori(0, NC) as c:
                        sp.wait_ge(chunk_used, c + sweep * NC + 1)
                        sp.dma_start(src_i[:], T.src[bass.ds(c * C, C)].partition_broadcast(P)).then_inc(chunk_in, 16)
                        sp.dma_start(e[:], T.e_flat[bass.ds(c * C, C)].partition_broadcast(P)).then_inc(chunk_in, 16)

        @block.gpsimd
        def _(pool):
            pool.iota(node_i[:], [[P, NB]], base=0, channel_multiplier=1).then_inc(made, 1)
            pool.wait_ge(made, 1)
            pool.tensor_copy(node[:], node_i[:]).then_inc(ready, 1)

        @block.scalar
        def _(act):
            far = act.value_load(T.far_i[0:1, 0:1], min_val=0, max_val=1)
            with act.If(far > 0):
                with act.Fori(0, NC) as c:
                    with act.Fori(0, NB) as b:
                        act.wait_ge(shifted, c * NB + b + 1)
                        act.activation(t[:], t[:], ACT.Exp).then_inc(ex_ready, 1)

        @block.vector
        def _(dve):
            dve.wait_ge(ready, 1)
            far = dve.value_load(T.far_i[0:1, 0:1], min_val=0, max_val=1)
            with dve.If(far > 0):
                dve.sem_inc(chunk_used, 1)
                dve.memset(top[:], -FAR)
                dve.memset(total[:], 0.0)
                with dve.Fori(0, NC) as c:
                    dve.wait_ge(chunk_in, c * 32 + 32)
                    dve.tensor_copy(src_f[:], src_i[:]).then_inc(chain, 1)
                    with dve.Fori(0, NB) as b:
                        n = c * (NB * 4 + 1) + b * 4 + 1
                        dve.wait_ge(chain, n)
                        dve.tensor_scalar(t[:], src_f[:], node[:, bass.ds(b, 1)], -FAR, ALU.not_equal, ALU.mult).then_inc(chain, 1)
                        dve.wait_ge(chain, n + 1)
                        dve.tensor_tensor(t[:], t[:], e[:], ALU.add).then_inc(chain, 1)
                        dve.wait_ge(chain, n + 2)
                        dve.tensor_reduce(part[:], t[:], AX.X, ALU.max).then_inc(chain, 1)
                        dve.wait_ge(chain, n + 3)
                        dve.tensor_tensor(top[:, bass.ds(b, 1)], top[:, bass.ds(b, 1)], part[:], ALU.max).then_inc(chain, 1)
                    dve.wait_ge(chain, (c + 1) * (NB * 4 + 1))
                    dve.sem_inc(chunk_used, 1)
                base = NC * (NB * 4 + 1)
                with dve.Fori(0, NC) as c:
                    dve.wait_ge(chunk_in, c * 32 + 32 + NC * 32)
                    dve.tensor_copy(src_f[:], src_i[:]).then_inc(chain, 1)
                    with dve.Fori(0, NB) as b:
                        n = c * (NB * 3 + 1) + b * 3 + 1 + base
                        dve.wait_ge(chain, n)
                        dve.tensor_scalar(t[:], e[:], top[:, bass.ds(b, 1)], 0.0, ALU.subtract, ALU.min).then_inc(shifted, 1)
                        dve.wait_ge(ex_ready, c * NB + b + 1)
                        dve.scalar_tensor_tensor(out=t[:], in0=src_f[:], scalar=node[:, bass.ds(b, 1)], in1=t[:],
                                                 op0=ALU.is_equal, op1=ALU.mult).then_inc(chain, 1)
                        dve.wait_ge(chain, n + 1)
                        dve.tensor_reduce(part[:], t[:], AX.X, ALU.add).then_inc(chain, 1)
                        dve.wait_ge(chain, n + 2)
                        dve.tensor_tensor(total[:, bass.ds(b, 1)], total[:, bass.ds(b, 1)], part[:], ALU.add).then_inc(chain, 1)
                    dve.wait_ge(chain, (c + 1) * (NB * 3 + 1) + base)
                    dve.sem_inc(chunk_used, 1)
                end = base + NC * (NB * 3 + 1)
                dve.tensor_scalar(total[:], total[:], 1e-37, None, ALU.max).then_inc(chain, 1)
                dve.tensor_copy(T.shift[:, :, 0], top[:])
                dve.wait_ge(chain, end + 1)
                dve.reciprocal(T.shift[:, :, 1], total[:])


def aggregate(nc, T):
    NC = T.src.shape[0] // C
    HJ = J // 2
    with ExitStack() as ctx:
        m = Memory(nc, ctx, "ag")
        sb, ps, sem = m.sb, m.ps, m.sem
        acc = sb("acc", [P, T.NB, D])
        src_i = sb("src_i", [R, 2, J], I32)
        dst_i = sb("dst_i", [R, 2, J], I32)
        dst_f = sb("dst_f", [R, 2, J])
        rows = sb("rows", [R, 2, J, XW])
        e_s = sb("e_s", [R, 2, J])
        ex = sb("ex", [R, 2, J])
        att = sb("att", [R, 2, J])
        rel = sb("rel", [R, J])
        rows_i = sb("rows_i", [R, P], I32)
        iota = sb("iota", [R, P])
        first_i = sb("first_i", [R, T.NB], I32)
        first_row = sb("first_row", [R, T.NB])
        hot = [sb(f"hot{k}", [R, HJ, P]) for k in range(2)]
        part = ps("part", [P, 512])

        table_done = sem("table_done")
        iota_made, iota_ready = sem("iota_made"), sem("iota_ready")
        idx_in = [sem(f"idx_in{b}") for b in range(2)]
        rows_in = [sem(f"rows_in{b}") for b in range(2)]
        dst_ready, e_ready, ex_ready, att_ready, rel_ready = (sem("dst_ready"), sem("e_ready"), sem("ex_ready"),
                                                              sem("att_ready"), sem("rel_ready"))
        hot_ready = [sem(f"hot_ready{k}") for k in range(2)]
        hot_used = [sem(f"hot_used{k}") for k in range(2)]
        cleared, added, chunk_begun = sem("cleared"), sem("added"), sem("chunk_begun")
        agg_out = sem("agg_out")

        block = ctx.enter_context(nc.Block())
        src_c = T.src.rearrange("(c p j) -> c p j", p=R, j=J)
        dst_c = T.dst.rearrange("(c p j) -> c p j", p=R, j=J)

        def planned(eng, c, NBmax=T.NB - 1):
            prev = eng.value_load(T.plan[0:1, 0, bass.ds(c, 1)], min_val=0, max_val=NBmax)
            last = eng.value_load(T.plan[0:1, 0, bass.ds(c + 1, 1)], min_val=0, max_val=NBmax)
            first = eng.value_load(T.plan[0:1, 1, bass.ds(c, 1)], min_val=0, max_val=NBmax)
            pairs = eng.value_load(T.plan[0:1, 2, bass.ds(c, 1)], min_val=0, max_val=T.NB * NC)
            return prev, first, last, pairs

        @block.sync
        def _(sp):
            with nc.allow_non_contiguous_dma(reason="two words for each node"):
                sp.dma_start(T.xn_table[:, D:XW].rearrange("(b p) w -> p b w", p=P), T.shift[:]).then_inc(table_done, 16)

            def load(c, b):
                if not isinstance(c, int):
                    sp.wait_ge(att_ready, c - 1)
                    sp.wait_ge(dst_ready, c - 1)
                sp.dma_start(src_i[:, b], src_c[c]).then_inc(idx_in[b], 16)
                sp.dma_start(dst_i[:, b], dst_c[c]).then_inc(idx_in[b], 16)

            load(0, 0)
            load(1, 1)
            with sp.Fori(1, NC // 2) as i:
                load(i * 2, 0)
                load(i * 2 + 1, 1)
            total = sp.value_load(T.plan[0:1, 2, NC:NC + 1], min_val=0, max_val=T.NB * NC)
            sp.wait_ge(added, total + 2)
            sp.dma_start(T.agg.rearrange("(b p) d -> p b d", p=P), acc[:]).then_inc(agg_out, 16)
            sp.wait_ge(agg_out, 16)

        @block.gpsimd
        def _(pool):
            pool.iota(rows_i[:], [[1, P]], base=0, channel_multiplier=0)
            pool.iota(first_i[:], [[P, T.NB]], base=0, channel_multiplier=0).then_inc(iota_made, 1)
            pool.wait_ge(iota_made, 1)
            pool.tensor_copy(iota[:], rows_i[:])
            pool.tensor_copy(first_row[:], first_i[:]).then_inc(iota_ready, 1)
            pool.wait_ge(table_done, 16)

            def gather(c, b, i):
                pool.wait_ge(idx_in[b], i * 32 + 32)
                if not isinstance(c, int):
                    pool.wait_ge(chunk_begun, c)
                pool.sem_inc(T.passed, 1)
                for j in range(J):
                    pool.indirect_dma_start(
                        out=rows[:, b, j, :], out_offset=None, in_=T.xn_table[0:T.x.shape[0], :],
                        in_offset=bass.IndirectOffsetOnAxis(ap=src_i[:, b, j:j + 1], axis=0),
                    ).then_inc(rows_in[b], 16)

            gather(0, 0, 0)
            gather(1, 1, 0)
            with pool.Fori(1, NC // 2) as i:
                gather(i * 2, 0, i)
                gather(i * 2 + 1, 1, i)

        @block.vector
        def _(dve):
            dve.wait_ge(iota_ready, 1)
            dve.memset(part[:, 0:D], 0.0)
            for n in range(7):
                a, z = T.NB * n // 7, T.NB * (n + 1) // 7
                last = dve.memset(acc[:, a:z, :], 0.0)
            last.then_inc(cleared, 1)
            dve.wait_ge(cleared, 1)
            dve.sem_inc(hot_ready[0], 1)
            dve.sem_inc(hot_ready[1], 1)
            dve.sem_inc(added, 1)

            def one_hot(k, b, n):
                dve.wait_ge(hot_used[k], n + 1)
                for t in range(HJ):
                    j = k * HJ + t
                    last = dve.tensor_scalar(hot[k][:, t], iota[:], rel[:, j:j + 1], att[:, b, j:j + 1],
                                             ALU.is_equal, ALU.mult)
                last.then_inc(hot_ready[k], 1)

            def pair(b, n, blk, prev):
                dve.wait_ge(hot_ready[1], n + 1)
                dve.tensor_scalar(rel[:], dst_f[:, b], first_row[:, bass.ds(blk, 1)], None, ALU.subtract).then_inc(rel_ready, 1)
                dve.wait_ge(rel_ready, n + 1)
                one_hot(0, b, n)
                dve.wait_ge(hot_used[1], n + 1)
                dve.wait_ge(added, n + 1)
                row = acc[:, bass.ds(prev, 1), :].rearrange("p a d -> p (a d)")
                dve.tensor_tensor(row, row, part[:, 0:D], ALU.add).then_inc(added, 1)
                one_hot(1, b, n)

            def chunk(c, b, i):
                prev, first, last, pairs = planned(dve, c)
                dve.wait_ge(idx_in[b], i * 32 + 32)
                dve.tensor_copy(dst_f[:, b], dst_i[:, b]).then_inc(dst_ready, 1)
                dve.wait_ge(rows_in[b], i * (16 * J) + 16 * J)
                dve.tensor_tensor(e_s[:, b], T.e[:, bass.ds(c * J, J)], rows[:, b, :, D], ALU.subtract).then_inc(e_ready, 1)
                dve.wait_ge(ex_ready, c + 1)
                dve.tensor_tensor(att[:, b], ex[:, b], rows[:, b, :, D + 1], ALU.mult).then_inc(att_ready, 1)
                dve.wait_ge(att_ready, c + 1)
                dve.wait_ge(dst_ready, c + 1)
                dve.wait_ge(hot_used[1], pairs + 1)
                dve.sem_inc(chunk_begun, 1)
                pair(b, pairs, first, prev)
                with dve.If(first < last):
                    with dve.Fori(1, last - first + 1) as d:
                        blk = nc.s_assert_within(first + d, 1, T.NB - 1, skip_runtime_bounds_check_because="it is at most last")
                        pair(b, pairs + d, blk, blk - 1)

            with dve.Fori(0, NC // 2) as i:
                chunk(i * 2, 0, i)
                chunk(i * 2 + 1, 1, i)
            final = dve.value_load(T.plan[0:1, 0, NC:NC + 1], min_val=0, max_val=T.NB - 1)
            total = dve.value_load(T.plan[0:1, 2, NC:NC + 1], min_val=0, max_val=T.NB * NC)
            dve.wait_ge(hot_used[1], total + 1)
            dve.wait_ge(added, total + 1)
            row = acc[:, bass.ds(final, 1), :].rearrange("p a d -> p (a d)")
            dve.tensor_tensor(row, row, part[:, 0:D], ALU.add).then_inc(added, 1)

        @block.scalar
        def _(act):
            with act.Fori(0, NC // 2) as i:
                for b in range(2):
                    act.wait_ge(e_ready, i * 2 + b + 1)
                    act.activation(ex[:, b], e_s[:, b], ACT.Exp).then_inc(ex_ready, 1)

        @block.tensor
        def _(pe):
            pe.wait_ge(cleared, 1)
            for k in range(2):
                pe.sem_inc(hot_used[k], 1)

            def pair(b, n):
                pe.wait_ge(added, n + 2)
                for k in range(2):
                    pe.wait_ge(hot_ready[k], n + 2)
                    for t in range(HJ):
                        j = k * HJ + t
                        mm = pe.matmul(part[:, 0:D], hot[k][:, t], rows[:, b, j, 0:D], start=j == 0, stop=j == J - 1)
                    mm.then_inc(hot_used[k], 1)

            def chunk(c, b):
                prev, first, last, pairs = planned(pe, c)
                pair(b, pairs)
                with pe.If(first < last):
                    with pe.Fori(1, last - first + 1) as d:
                        pair(b, pairs + d)

            with pe.Fori(0, NC // 2) as i:
                chunk(i * 2, 0)
                chunk(i * 2 + 1, 1)


def mix(nc, T):
    NG = T.x.shape[0] // G
    E = T.W1.shape[0]
    NACT = 3 * 16
    with ExitStack() as ctx:
        m = Memory(nc, ctx, "mx")
        sb, ps, sem = m.sb, m.ps, m.sem
        w_o = sb("w_o", [P, K, D])
        w_r = sb("w_r", [P, K, E])
        b_r = sb("b_r", [P, E])
        gamma = sb("gamma", [P, K])
        beta = sb("beta", [P, K])
        b_out = sb("b_out", [1, 2, D])
        bias = sb("bias", [1, D])
        one_row = sb("one_row", [1, R])
        eight_i = sb("eight_i", [R, S, E], I32)
        eight = sb("eight", [R, S, E])
        start_i = sb("start_i", [R, S, E], I32)
        start = sb("start", [R, S, E])
        half = sb("half", [R, S])
        ones = sb("ones", [R, R])
        below = sb("below", [R, R])
        x = sb("x", [R, 2, S, D])
        agg = sb("agg", [R, 2, S, D])
        qT = sb("qT", [P, 2, K, G])
        aggT = sb("aggT", [P, K, G])
        den = sb("den", [P, K, G])
        rec = sb("rec", [P, K, G])
        oT = sb("oT", [P, K, G])
        x1 = sb("x1", [R, 2, S, D])
        stats = sb("stats", [R, 2, S, 6])
        mv = sb("mv", [R, 2, S, 2])
        var = sb("var", [R, 2, S])
        rstd = sb("rstd", [R, 2, S])
        xn1 = sb("xn1", [R, S, D])
        xn = sb("xn", [R, 4, S, D])
        xhT = sb("xhT", [P, K, G])
        raw = sb("raw", [R, 2, S * E])
        logit = sb("logit", [R, S, E])
        top = sb("top", [R, S, 8])
        top_i = sb("top_i", [R, S, 8], U32)
        top_f = sb("top_f", [R, S, 8])
        gap = sb("gap", [R, S])
        odds = sb("odds", [R, S])
        both = sb("both", [R, S])
        pick = sb("pick", [R, 2, S, E])
        mask = sb("mask", [R, S, E])
        seen = sb("seen", [R, E])
        new = sb("new", [R, E])
        place = sb("place", [R, S, E])
        picked = sb("picked", [R, 2, S, E])
        slot = sb("slot", [R, 2, S])
        slot_i = sb("slot_i", [R, 4, 2, S], I32)
        slots = sb("slots", [R, 2, NG * S])
        slot_all = sb("slot_all", [R, 2, NG * S])
        moved = sb("moved", [R, 2, NG * S])
        delta = sb("delta", [R, E])
        count = sb("count", [R, E])
        steps_f = sb("steps_f", [R, E])
        count_i = sb("count_i", [R, E], I32)
        steps_i = sb("steps_i", [R, E], I32)
        one8 = sb("one8", [R, E])
        before = sb("before", [R, E])

        bank = [ps(f"bank{n}", [P, 512]) for n in range(8)]
        weights_in, consts_made, consts_ready, bias_ready = (sem("weights_in"), sem("consts_made"), sem("consts_ready"),
                                                             sem("bias_ready"))
        acts_in = [sem(f"acts_in{b}") for b in range(2)]
        x1_stored = [sem(f"x1_stored{b}") for b in range(2)]
        rows_sent = [sem(f"rows_sent{b}") for b in range(4)]
        agg_turned, aggT_ready = sem("agg_turned"), sem("aggT_ready")
        lin_ready, den_ready, rec_ready, oT_ready = sem("lin_ready"), sem("den_ready"), sem("rec_ready"), sem("oT_ready")
        x1_mm, x1_ready = sem("x1_mm"), sem("x1_ready")
        stats_ready, mv_ready, var_ready, rstd_ready = sem("stats_ready"), sem("mv_ready"), sem("var_ready"), sem("rstd_ready")
        xn1_ready, xn_ready = sem("xn1_ready"), sem("xn_ready")
        xn_turned, xhT_ready, logit_mm, raw_ready = sem("xn_turned"), sem("xhT_ready"), sem("logit_mm"), sem("raw_ready")
        logit_ready, top_ready, found, gap_ready = sem("logit_ready"), sem("top_ready"), sem("found"), sem("gap_ready")
        topf_ready, pick_ready, mask_ready, rank_mm = sem("topf_ready"), sem("pick_ready"), sem("mask_ready"), sem("rank_mm")
        odds_ready, both_ready, gate_ready = sem("odds_ready"), sem("both_ready"), sem("gate_ready")
        new_ready, seen_ready, place_ready = sem("new_ready"), sem("seen_ready"), sem("place_ready")
        picked_ready, slot_ready, sloti_ready = sem("picked_ready"), sem("slot_ready"), sem("sloti_ready")
        final, rows_gone = sem("final"), sem("rows_gone")

        block = ctx.enter_context(nc.Block())
        x_rows = T.x.rearrange("(g s p) d -> g p s d", s=S, p=R)
        x1_rows = T.x1_table.rearrange("(g s p) d -> g p s d", s=S, p=R)
        agg_rows = T.agg[0:NG * G, :].rearrange("(g s p) d -> g p s d", s=S, p=R)
        q_cols = T.q_table.rearrange("k p (g n) -> g p k n", n=G)

        def pipeline(eng, step, last):
            for g in range(4):
                step(g, g, 0)
            with eng.Fori(1, (NG - 1) // 4) as i:
                for b in range(4):
                    step(i * 4 + b, b, i)
            for g in range(NG - 1, last + 1):
                step(g, g % 4, g // 4)

        def has(g, lag):
            return not isinstance(g, int) or 0 <= g - lag < NG

        def after(eng, semaphore, value):
            if not isinstance(value, int) or value > 0:
                eng.wait_ge(semaphore, value)

        @block.sync
        def _(sp):
            sp.dma_start(w_o[:], T.wo.rearrange("(c p) o -> p c o", p=P)).then_inc(weights_in, 16)
            sp.dma_start(b_r[:], T.br.partition_broadcast(P)).then_inc(weights_in, 16)
            for k in range(K):
                for dst, vec in ((gamma, T.gamma), (beta, T.beta)):
                    sp.dma_start(dst[:, k:k + 1], vec[k * P:(k + 1) * P].rearrange("(p a) -> p a", a=1)).then_inc(weights_in, 16)
                sp.dma_start(w_r[:, k, :], T.Wr[k * P:(k + 1) * P, :]).then_inc(weights_in, 16)
            sp.dma_start(b_out[:, 0], T.b_fc.rearrange("(a d) -> a d", a=1)).then_inc(weights_in, 16)
            sp.dma_start(b_out[:, 1], T.bo.rearrange("(a d) -> a d", a=1)).then_inc(weights_in, 16)

            def step(g, b, u):
                c = b % 2
                if has(g, 0):
                    after(sp, x1_ready, g - 1)
                    sp.dma_start(x[:, c], x_rows[g]).then_inc(acts_in[c], 16)
                    sp.dma_start(agg[:, c], agg_rows[g]).then_inc(acts_in[c], 16)
                    sp.dma_start(qT[:, c], q_cols[g]).then_inc(acts_in[c], 16)
                if has(g, 1):
                    sp.wait_ge(x1_ready, g)
                    sp.dma_start(x1_rows[g - 1], x1[:, 1 - c]).then_inc(x1_stored[1 - c], 16)

            pipeline(sp, step, NG)
            for c in range(2):
                sp.wait_ge(x1_stored[c], 16 * ((NG + 1 - c) // 2))

        @block.gpsimd
        def _(pool):
            pool.iota(eight_i[:], [[0, S], [1, E]], base=0, channel_multiplier=0)
            pool.iota(start_i[:], [[0, S], [CAP, E]], base=0, channel_multiplier=0)
            pool.memset(half[:], -0.5)
            pool.memset(one_row[:], 1.0)
            pool.memset(seen[:], 0.0)
            pool.memset(ones[:], 1.0).then_inc(consts_made, 1)
            pool.wait_ge(consts_made, 1)
            pool.tensor_copy(eight[:], eight_i[:])
            pool.tensor_copy(start[:], start_i[:])
            pool.affine_select(out=below[:], in_=ones[:], compare_op=ALU.is_gt, fill=0.0, base=0,
                               pattern=[[1, R]], channel_multiplier=-1).then_inc(consts_ready, 1)

            def inverse_root(g, n):
                pool.wait_ge(mv_ready, g * 2 + n + 1)
                pool.sem_inc(T.passed, 1)
                pool.tensor_scalar(var[:, n], mv[:, n, :, 1], EPS, None, ALU.add).then_inc(var_ready, 1)
                pool.wait_ge(var_ready, g * 2 + n + 1)
                pool.tensor_tensor(rstd[:, n], var[:, n], half[:], ALU.pow).then_inc(rstd_ready, 1)

            def send(g, b, c):
                pool.wait_ge(sloti_ready, g + 1)
                pool.sem_inc(T.passed, 1)
                for s in range(S):
                    pool.indirect_dma_start(
                        out=T.lists, out_offset=bass.IndirectOffsetOnAxis(ap=slot_i[:, b, c, s:s + 1], axis=0),
                        in_=xn[:, b, s, :], in_offset=None,
                    ).then_inc(rows_sent[b], 16)

            def step(g, b, u):
                for n in range(2):
                    if has(g, 1):
                        inverse_root(g - 1, n)
                    if has(g, 3):
                        send(g - 3, (b + 1) % 4, n)
                if has(g, 4):
                    pool.wait_ge(rows_sent[b], u * (16 * 2 * S))
                    pool.sem_inc(rows_gone, 1)

            pool.sem_inc(rows_gone, 1)
            pipeline(pool, step, NG + 2)
            for b in range(4):
                pool.wait_ge(rows_sent[b], 16 * 2 * S * ((NG + 3 - b) // 4))

        @block.tensor
        def _(pe):
            pe.wait_ge(weights_in, 16 * (4 + 3 * K))
            pe.wait_ge(consts_ready, 1)
            pe.wait_ge(bias_ready, 1)

            def residual(g, b, u):
                c = b % 2
                pe.wait_ge(acts_in[c], (g - c) * (NACT // 2) + NACT)
                after(pe, xhT_ready, (g - 1) * K)
                for k in range(K):
                    for s in range(S):
                        mm = pe.transpose(bank[k][:, s * R:(s + 1) * R], agg[:, c, s, k * P:(k + 1) * P], T.ident[0:R, 0:R])
                    mm.then_inc(agg_turned, 1)
                after(pe, raw_ready, g - 1)
                after(pe, place_ready, g - 2)
                after(pe, oT_ready, g * K)
                for k in range(K):
                    pe.matmul(bank[4 + k][:, 0:G], T.ksum[:, k], qT[:, c, k], start=True, stop=True).then_inc(lin_ready, 1)
                    pe.matmul(bank[2 + k][:, 0:G], T.kv[:, k], qT[:, c, k], start=True, stop=True).then_inc(lin_ready, 1)
                pe.wait_ge(aggT_ready, g * K + K)
                after(pe, x1_ready, g)
                for s in range(S):
                    out = bank[6 + s // 2][0:R, (s % 2) * D:(s % 2 + 1) * D]
                    pe.matmul(out, one_row[:], bias[:], start=True, stop=False)
                    for k in range(K):
                        pe.matmul(out, aggT[:, k, s * R:(s + 1) * R], T.w_fcT[:, k], start=False, stop=False)
                    if s == 0:
                        pe.wait_ge(oT_ready, g * K + K)
                    for k in range(K):
                        mm = pe.matmul(out, oT[:, k, s * R:(s + 1) * R], w_o[:, k], start=False, stop=k == K - 1)
                    if s % 2:
                        mm.then_inc(x1_mm, 1)

            def ranks(g):
                pe.wait_ge(mask_ready, g + 1)
                after(pe, seen_ready, g)
                out = bank[3][0:R, 0:S * E].rearrange("p (s e) -> p s e", e=E)
                pe.matmul(out, below[:], mask[:], start=True, stop=False)
                for n in range(1, S):
                    pe.matmul(out[:, n:S], ones[:], mask[:, 0:S - n], start=False, stop=False)
                pe.matmul(out, ones[:], seen[:].unsqueeze(1).broadcast_to([R, S, E]), start=False, stop=True).then_inc(rank_mm, 1)

            def logits(g, b, there):
                pe.wait_ge(xn_ready, g + 1)
                if there:
                    pe.wait_ge(aggT_ready, (g + 1) * K + K)
                for k in range(K):
                    for s in range(S):
                        mm = pe.transpose(bank[k][:, s * R:(s + 1) * R], xn[:, b, s, k * P:(k + 1) * P], T.ident[0:R, 0:R])
                    mm.then_inc(xn_turned, 1)
                pe.wait_ge(xhT_ready, g * K + K)
                for s in range(S):
                    for k in range(K):
                        mm = pe.matmul(bank[2][0:R, s * E:(s + 1) * E], xhT[:, k, s * R:(s + 1) * R], w_r[:, k],
                                       start=k == 0, stop=k == K - 1)
                mm.then_inc(logit_mm, 1)

            def step(g, b, u):
                if has(g, 0):
                    residual(g, b, u)
                if has(g, 2):
                    ranks(g - 2)
                if has(g, 1):
                    logits(g - 1, (b + 3) % 4, has(g, 0))

            pipeline(pe, step, NG + 1)
            pe.wait_ge(seen_ready, NG)
            pe.wait_ge(place_ready, NG)
            pe.matmul(bank[3][0:R, 0:E], ones[:], seen[:], start=True, stop=True).then_inc(rank_mm, 1)

        @block.scalar
        def _(act):
            act.wait_ge(weights_in, 16 * (4 + 3 * K))

            def step(g, b, u):
                c = b % 2
                if has(g, 0):
                    after(act, x1_mm, g * 2)
                    for k in range(K):
                        act.wait_ge(agg_turned, g * K + k + 1)
                        act.copy(aggT[:, k], bank[k][:, 0:G]).then_inc(aggT_ready, 1)
                if has(g, 2):
                    act.wait_ge(gap_ready, g - 1)
                    after(act, gate_ready, (g - 2) * 2)
                    act.activation(odds[:], gap[:], ACT.Exp).then_inc(odds_ready, 1)
                if has(g, 1):
                    after(act, logit_mm, g - 1)
                    for k in range(K):
                        act.wait_ge(xn_turned, (g - 1) * K + k + 1)
                        act.activation(xhT[:, k], bank[k][:, 0:G], ACT.Identity, bias=beta[:, k:k + 1],
                                       scale=gamma[:, k:k + 1]).then_inc(xhT_ready, 1)
                    act.wait_ge(logit_mm, g)
                    after(act, logit_ready, g - 2)
                    act.copy(raw[:, 1 - c], bank[2][0:R, 0:S * E]).then_inc(raw_ready, 1)

            pipeline(act, step, NG + 1)

        @block.vector
        def _(dve):
            dve.wait_ge(weights_in, 16 * (4 + 3 * K))
            dve.wait_ge(consts_ready, 1)
            dve.tensor_tensor(bias[:], b_out[:, 0], b_out[:, 1], ALU.add).then_inc(bias_ready, 1)

            def moments(g, n, rows):
                for s in range(S):
                    last = dve.bn_stats(stats[:, n, s], rows[:, s])
                last.then_inc(stats_ready, 1)
                dve.wait_ge(stats_ready, g * 2 + n + 1)
                dve.sem_inc(T.passed, 1)
                for s in range(S):
                    last = dve.bn_aggr(mv[:, n, s], stats[:, n, s])
                last.then_inc(mv_ready, 1)

            def normalize(g, n, out, rows, ready):
                dve.wait_ge(rstd_ready, g * 2 + n + 1)
                for s in range(S):
                    last = dve.tensor_scalar(out[:, s], rows[:, s], mv[:, n, s, 0:1], rstd[:, n, s:s + 1], ALU.subtract, ALU.mult)
                last.then_inc(ready, 1)

            def attention(g, k):
                dve.wait_ge(lin_ready, g * (2 * K) + 2 * k + 1)
                dve.tensor_scalar(den[:, k], bank[4 + k][:, 0:G], 1e-6, None, ALU.add).then_inc(den_ready, 1)
                dve.wait_ge(den_ready, g * K + k + 1)
                dve.reciprocal(rec[:, k], den[:, k]).then_inc(rec_ready, 1)
                dve.wait_ge(rec_ready, g * K + k + 1)
                dve.wait_ge(lin_ready, g * (2 * K) + 2 * k + 2)
                dve.tensor_tensor(oT[:, k], bank[2 + k][:, 0:G], rec[:, k], ALU.mult).then_inc(oT_ready, 1)

            def pick_experts(g, c):
                dve.wait_ge(raw_ready, g + 1)
                dve.tensor_tensor(logit[:], raw[:, c].rearrange("p (s e) -> p s e", e=E),
                                  b_r[0:R].unsqueeze(1).broadcast_to([R, S, E]), ALU.add).then_inc(logit_ready, 1)
                dve.wait_ge(logit_ready, g + 1)
                dve.sem_inc(T.passed, 1)
                for s in range(S):
                    last = dve.max(top[:, s], logit[:, s])
                last.then_inc(top_ready, 1)
                dve.wait_ge(top_ready, g + 1)
                dve.sem_inc(T.passed, 1)
                for s in range(S):
                    last = dve.max_index(top_i[:, s], top[:, s], logit[:, s])
                last.then_inc(found, 1)
                dve.tensor_tensor(gap[:], top[:, :, 1], top[:, :, 0], ALU.subtract).then_inc(gap_ready, 1)
                dve.wait_ge(found, g + 1)
                dve.tensor_copy(top_f[:, :, 0:2], top_i[:, :, 0:2]).then_inc(topf_ready, 1)
                dve.wait_ge(topf_ready, g + 1)
                for n in range(2):
                    last = dve.tensor_tensor(pick[:, n], eight[:], top_f[:, :, n:n + 1].broadcast_to([R, S, E]), ALU.is_equal)
                last.then_inc(pick_ready, 1)
                dve.wait_ge(pick_ready, g + 1)
                dve.tensor_tensor(mask[:], pick[:, 0], pick[:, 1], ALU.add).then_inc(mask_ready, 1)

            def places(g, b):
                dve.wait_ge(odds_ready, g + 1)
                dve.tensor_scalar(both[:], odds[:], 1.0, None, ALU.add).then_inc(both_ready, 1)
                dve.wait_ge(mask_ready, g + 1)
                dve.tensor_reduce(new[:], mask[:].rearrange("p s e -> p e s"), AX.X, ALU.add).then_inc(new_ready, 1)
                dve.wait_ge(both_ready, g + 1)
                dve.reciprocal(T.gate[:, 0, bass.ds(g * S, S)], both[:]).then_inc(gate_ready, 1)
                dve.wait_ge(rank_mm, g + 1)
                dve.tensor_tensor(place[:], bank[3][0:R, 0:S * E].rearrange("p (s e) -> p s e", e=E), start[:], ALU.add).then_inc(place_ready, 1)
                dve.wait_ge(gate_ready, g * 2 + 1)
                dve.tensor_tensor(T.gate[:, 1, bass.ds(g * S, S)], T.gate[:, 0, bass.ds(g * S, S)], odds[:], ALU.mult).then_inc(gate_ready, 1)
                dve.wait_ge(place_ready, g + 1)
                for n in range(2):
                    last = dve.tensor_tensor(picked[:, n], pick[:, n], place[:], ALU.mult)
                last.then_inc(picked_ready, 1)
                dve.wait_ge(new_ready, g + 1)
                dve.tensor_tensor(seen[:], seen[:], new[:], ALU.add).then_inc(seen_ready, 1)
                dve.wait_ge(picked_ready, g + 1)
                dve.tensor_reduce(slot[:], picked[:], AX.X, ALU.add).then_inc(slot_ready, 1)
                dve.wait_ge(slot_ready, g + 1)
                dve.tensor_copy(slots[:, :, bass.ds(g * S, S)], slot[:])
                dve.tensor_copy(slot_i[:, b], slot[:]).then_inc(sloti_ready, 1)

            def step(g, b, u):
                c = b % 2
                if has(g, 1):
                    after(dve, x1_ready, g)
                    moments(g - 1, 0, x1[:, 1 - c])
                if has(g, 0):
                    after(dve, x1_mm, g * 2)
                    attention(g, 0)
                    attention(g, 1)
                if has(g, 1):
                    after(dve, mv_ready, (g - 1) * 2)
                    normalize(g - 1, 0, xn1, x1[:, 1 - c], xn1_ready)
                    dve.wait_ge(xn1_ready, g)
                    moments(g - 1, 1, xn1)
                if has(g, 2):
                    pick_experts(g - 2, c)
                if has(g, 1):
                    b1 = (b + 3) % 4
                    after(dve, rows_gone, g - 3)
                    normalize(g - 1, 1, xn[:, b1], xn1, xn_ready)
                if has(g, 0):
                    after(dve, x1_stored[c], (g - c) * 8)
                    for s in range(S):
                        if s % 2 == 0:
                            dve.wait_ge(x1_mm, g * 2 + s // 2 + 1)
                        last = dve.tensor_tensor(x1[:, c, s], x[:, c, s], bank[6 + s // 2][0:R, (s % 2) * D:(s % 2 + 1) * D], ALU.add)
                    last.then_inc(x1_ready, 1)
                if has(g, 2):
                    places(g - 2, (b + 2) % 4)

            pipeline(dve, step, NG + 1)
            dve.wait_ge(rank_mm, NG + 1)
            done = 0
            for make in (
                lambda: dve.tensor_copy(count[:], bank[3][0:R, 0:E]),
                lambda: dve.tensor_copy(T.moe[:, 0, 0:E], count[0:1]),
                lambda: dve.tensor_scalar(steps_f[:], count[:], BLK - 1.0, None, ALU.add),
                lambda: dve.tensor_copy(count_i[:], steps_f[:]),
                lambda: dve.tensor_scalar(steps_i[:], count_i[:], BLK.bit_length() - 1, None, ALU.arith_shift_right),
                lambda: dve.tensor_copy(T.moe[:, 1, 0:E], steps_i[0:1]),
                lambda: dve.tensor_copy(steps_f[:], steps_i[:]),
                lambda: dve.memset(one8[:], 1.0),
                lambda: dve.memset(T.moe[:, 2, 0:1], 0),
                lambda: dve.tensor_tensor_scan(before[:], one8[:], steps_f[:], 0.0, ALU.mult, ALU.add),
                lambda: dve.tensor_copy(T.moe[:, 2, 1:E + 1], before[0:1]),
                lambda: dve.tensor_scalar(delta[:], steps_f[:], float(BLK), -float(CAP), ALU.mult, ALU.add),
                lambda: dve.tensor_copy(slot_all[:], slots[:]),
            ):
                done += 1
                make().then_inc(final, 1)
                dve.wait_ge(final, done)
            for e in range(1, E):
                for make in (
                    lambda: dve.tensor_scalar(moved[:], slots[:], e * CAP - 0.5, delta[:, e - 1:e], ALU.is_gt, ALU.mult),
                    lambda: dve.tensor_tensor(slot_all[:], slot_all[:], moved[:], ALU.add),
                ):
                    done += 1
                    make().then_inc(final, 1)
                    dve.wait_ge(final, done)
            dve.tensor_copy(T.slot[:], slot_all[:])


def experts(nc, T):
    E, _, H = T.W1.shape
    M = H // P
    A = BLK // P
    MAX = CAP // BLK
    with ExitStack() as ctx:
        m = Memory(nc, ctx, "ex")
        sb, ps, sem = m.sb, m.ps, m.sem
        w1 = sb("w1", [P, 2, K, H])
        w2 = sb("w2", [P, 2, M, D])
        b2 = sb("b2", [P, 2, D])
        b1_rows = sb("b1_rows", [E * M, P])
        b1 = sb("b1", [P, E * M])
        gamma = sb("gamma", [P, K])
        beta = sb("beta", [P, K])
        zeros = sb("zeros", [P, A, D])
        x = sb("x", [P, A, D])
        xT = sb("xT", [P, K, BLK])
        hid = sb("hid", [P, M, BLK])
        y = sb("y", [P, A, D])
        tp = [ps(f"tp{k}", [P, 512]) for k in range(K)]
        hp = [ps(f"hp{k}", [P, 512]) for k in range(M)]
        yp = [ps(f"yp{k}", [P, 512]) for k in range(2)]

        zeroed, tails_in, consts_in, b1_turned, b1_ready = (sem("zeroed"), sem("tails_in"), sem("consts_in"),
                                                            sem("b1_turned"), sem("b1_ready"))
        weights_in = [sem(f"weights_in{b}") for b in range(2)]
        b1_copied, expert_done = sem("b1_copied"), sem("expert_done")
        x_in, x_turned, xT_ready = sem("x_in"), sem("x_turned"), sem("xT_ready")
        hid_mm, hid_ready, y_mm, y_ready, y_out = sem("hid_mm"), sem("hid_ready"), sem("y_mm"), sem("y_ready"), sem("y_out")
        y_free, spare_out = sem("y_free"), sem("spare_out")

        block = ctx.enter_context(nc.Block())

        def planned(eng, e):
            n = eng.value_load(T.moe[0:1, 1, bass.ds(e, 1)], min_val=0, max_val=MAX)
            base = eng.value_load(T.moe[0:1, 2, bass.ds(e, 1)], min_val=0, max_val=2 * MAX)
            return n, base

        def blocks(eng, body, before=None):
            with eng.Fori(0, E // 2) as i:
                for b in range(2):
                    e = i * 2 + b
                    n, base = planned(eng, e)
                    if before is not None:
                        before(e, b, i)
                    with eng.If(n > 0):
                        with eng.Fori(0, n) as k:
                            body(e, b, base + k, k)

        @block.sync
        def _(sp):
            sp.dma_start(b1_rows[:], T.b1.rearrange("e (m p) -> (e m) p", p=P)).then_inc(consts_in, 16)
            for k in range(K):
                for dst, vec in ((gamma, T.gamma), (beta, T.beta)):
                    sp.dma_start(dst[:, k:k + 1], vec[k * P:(k + 1) * P].rearrange("(p a) -> p a", a=1)).then_inc(consts_in, 16)
            sp.wait_ge(zeroed, 1)
            with sp.Fori(0, E) as e:
                n = sp.value_load(T.moe[0:1, 0, bass.ds(e, 1)], min_val=0, max_val=CAP - BLK)
                sp.dma_start(T.lists[bass.ds(e * CAP + n, BLK), :].rearrange("(p a) d -> p a d", p=P), zeros[:]).then_inc(tails_in, 16)
            sp.wait_ge(tails_in, 16 * E)
            for t in range(FULL, BLOCKS):
                sp.dma_start(T.results[t * BLK:(t + 1) * BLK, :].rearrange("(p a) d -> p a d", p=P), zeros[:]).then_inc(spare_out, 16)

            def load(row):
                sp.dma_start(x[:], T.lists[bass.ds(row, BLK), :].rearrange("(a p) d -> p a d", p=P)).then_inc(x_in, 16)

            def body(e, b, t, k):
                sp.wait_ge(x_turned, t * K + 1)
                load(e * CAP + k * BLK)

            blocks(sp, body)
            total = sp.value_load(T.moe[0:1, 2, E:E + 1], min_val=0, max_val=BLOCKS)
            sp.wait_ge(x_turned, total * K + 1)
            load(0)

        @block.gpsimd
        def _(pool):
            pool.memset(zeros[:], 0.0).then_inc(zeroed, 1)
            pool.sem_inc(y_free, 1)
            pool.wait_ge(spare_out, 16 * (BLOCKS - FULL))

            def body(e, b, t, k):
                pool.wait_ge(y_ready, t * 2 + 4)
                pool.sem_inc(T.passed, 1)
                row = nc.s_assert_within(t * BLK, 0, (BLOCKS - 1) * BLK, skip_runtime_bounds_check_because="the lists have at most BLOCKS blocks")
                pool.dma_start(T.results[bass.ds(row, BLK), :].rearrange("(a p) d -> p a d", p=P), y[:]).then_inc(y_out, 16)
                pool.wait_ge(y_out, t * 16 + 16)
                pool.sem_inc(y_free, 1)

            blocks(pool, body)

        @block.tensor
        def _(pe):
            pe.sem_inc(x_turned, 1)
            pe.sem_inc(y_mm, 1)
            pe.wait_ge(consts_in, 16 * (1 + 2 * K))
            pe.transpose(yp[0][:, 0:E * M], b1_rows[:], T.ident[0:E * M, 0:E * M]).then_inc(b1_turned, 1)

            def turn():
                for k in range(K):
                    for a in range(A):
                        mm = pe.transpose(tp[k][:, a * P:(a + 1) * P], x[:, a, k * P:(k + 1) * P], T.ident[:])
                    mm.then_inc(x_turned, 1)

            pe.wait_ge(x_in, 16)
            turn()
            pe.wait_ge(b1_ready, 1)

            def before(e, b, i):
                pe.wait_ge(weights_in[b], i * 48 + 48)

            def body(e, b, t, k_):
                pe.wait_ge(xT_ready, t * K + K)
                for n in range(M):
                    for k in range(K):
                        mm = pe.matmul(hp[n][:, 0:BLK], w1[:, b, k, n * P:(n + 1) * P], xT[:, k], start=k == 0, stop=k == K - 1)
                    mm.then_inc(hid_mm, 1)
                pe.wait_ge(x_in, t * 16 + 32)
                turn()
                pe.wait_ge(hid_ready, t * M + M)
                for a in range(A):
                    if a % 2 == 0:
                        pe.wait_ge(y_ready, t * 2 + a // 2 + 1)
                    for n in range(M):
                        mm = pe.matmul(yp[a // 2][:, (a % 2) * D:(a % 2 + 1) * D], hid[:, n, a * P:(a + 1) * P], w2[:, b, n],
                                       start=n == 0, stop=n == M - 1)
                    if a % 2:
                        mm.then_inc(y_mm, 1)

            blocks(pe, body, before)

        @block.scalar
        def _(act):
            def weights(e, b):
                one = bass.ds(e, 1)
                act.dma_start(w1[:, b], T.W1[one].rearrange("a (c p) h -> p (a c) h", p=P)).then_inc(weights_in[b], 16)
                act.dma_start(w2[:, b], T.W2[one].rearrange("a (c p) d -> p (a c) d", p=P)).then_inc(weights_in[b], 16)
                act.dma_start(b2[:, b], T.b2[one].rearrange("a d -> (a d)").partition_broadcast(P)).then_inc(weights_in[b], 16)

            weights(0, 0)
            act.wait_ge(b1_ready, 1)
            with act.Fori(0, E // 2) as i:
                for b in range(2):
                    e = i * 2 + b
                    n, base = planned(act, e)
                    act.wait_ge(y_mm, base * 2 + 1)
                    act.wait_ge(y_ready, base * 2 + 2)
                    act.sem_inc(T.passed, 1)
                    if b == 0:
                        weights(e + 1, 1)
                    else:
                        with act.If(i < E // 2 - 1):
                            weights(nc.s_assert_within(e + 1, 2, E - 1, skip_runtime_bounds_check_because="i is below its last"), 0)
                    with act.If(n > 0):
                        with act.Fori(0, n) as k:
                            t = base + k
                            act.wait_ge(y_mm, t * 2 + 1)
                            for j in range(M):
                                act.wait_ge(hid_mm, t * M + j + 1)
                                act.activation(hid[:, j], hp[j][:, 0:BLK], ACT.Gelu,
                                               bias=b1[:, bass.ds(e * M + j, 1)]).then_inc(hid_ready, 1)

        @block.vector
        def _(dve):
            dve.sem_inc(y_ready, 2)
            dve.wait_ge(b1_turned, 1)
            dve.tensor_copy(b1[:], yp[0][:, 0:E * M]).then_inc(b1_ready, 1)
            dve.wait_ge(consts_in, 16 * (1 + 2 * K))

            def body(e, b, t, k_):
                dve.wait_ge(hid_mm, t * M + M)
                for k in range(K):
                    dve.wait_ge(x_turned, t * K + K + k + 2)
                    dve.tensor_scalar(xT[:, k], tp[k][:, 0:BLK], gamma[:, k:k + 1], beta[:, k:k + 1], ALU.mult, ALU.add).then_inc(xT_ready, 1)
                dve.wait_ge(y_free, t + 1)
                for j in range(2):
                    dve.wait_ge(y_mm, t * 2 + j + 2)
                    dve.tensor_tensor(y[:, 2 * j:2 * j + 2], yp[j][:].rearrange("p (a d) -> p a d", d=D),
                                      b2[:, b].unsqueeze(1).broadcast_to([P, 2, D]), ALU.add).then_inc(y_ready, 1)

            for k in range(K):
                dve.wait_ge(x_turned, k + 2)
                dve.tensor_scalar(xT[:, k], tp[k][:, 0:BLK], gamma[:, k:k + 1], beta[:, k:k + 1], ALU.mult, ALU.add).then_inc(xT_ready, 1)

            def before(e, b, i):
                dve.wait_ge(weights_in[b], i * 48 + 48)
                dve.sem_inc(T.passed, 1)

            blocks(dve, body, before)


def combine(nc, T):
    NG = T.x.shape[0] // G
    with ExitStack() as ctx:
        m = Memory(nc, ctx, "co")
        sb, sem = m.sb, m.sem
        slot_i = sb("slot_i", [R, 2, 2, S], I32)
        x1 = sb("x1", [R, 2, S, D])
        res = sb("res", [R, 2, 2, S, D])
        first = sb("first", [R, 2, S, D])
        out = sb("out", [R, 2, S, D])
        slot_ready, rows_in = sem("slot_ready"), [sem(f"rows_in{b}") for b in range(2)]
        x1_in = [sem(f"x1_in{b}") for b in range(2)]
        first_ready, out_ready = sem("first_ready"), sem("out_ready")
        out_stored = [sem(f"out_stored{b}") for b in range(2)]
        block = ctx.enter_context(nc.Block())
        x1_rows = T.x1_table.rearrange("(g s p) d -> g p s d", s=S, p=R)
        out_rows = T.out.rearrange("(g s p) d -> g p s d", s=S, p=R)

        def run(eng, step):
            for g in range(3):
                step(g, g % 2, g // 2)
            with eng.Fori(1, (NG - 1) // 2) as i:
                step(i * 2 + 1, 1, i)
                step(i * 2 + 2, 0, i + 1)

        @block.sync
        def _(sp):
            def step(g, b, u):
                if not (isinstance(g, int) and g < 2):
                    sp.wait_ge(first_ready, g - 1)
                sp.dma_start(x1[:, b], x1_rows[g]).then_inc(x1_in[b], 16)
                if not (isinstance(g, int) and g < 1):
                    sp.wait_ge(out_ready, g)
                    sp.dma_start(out_rows[g - 1], out[:, 1 - b]).then_inc(out_stored[1 - b], 16)

            run(sp, step)
            sp.wait_ge(out_ready, NG)
            sp.dma_start(out_rows[NG - 1], out[:, (NG - 1) % 2]).then_inc(out_stored[(NG - 1) % 2], 16)
            for b in range(2):
                sp.wait_ge(out_stored[b], 16 * ((NG + 1 - b) // 2))

        @block.gpsimd
        def _(pool):
            def step(g, b, u):
                pool.wait_ge(slot_ready, g + 1)
                pool.sem_inc(T.passed, 1)
                for s in range(S):
                    for n in range(2):
                        pool.indirect_dma_start(
                            out=res[:, b, n, s, :], out_offset=None, in_=T.results,
                            in_offset=bass.IndirectOffsetOnAxis(ap=slot_i[:, b, n, s:s + 1], axis=0),
                        ).then_inc(rows_in[b], 16)

            run(pool, step)

        @block.vector
        def _(dve):
            def places(g, b):
                dve.tensor_copy(slot_i[:, b], T.slot[:, :, bass.ds(g * S, S)]).then_inc(slot_ready, 1)

            def add(g, b, u):
                dve.wait_ge(x1_in[b], u * 16 + 16)
                dve.wait_ge(rows_in[b], u * (16 * 2 * S) + 16 * 2 * S)
                for n, into, base, ready in ((0, first, x1, first_ready), (1, out, first, out_ready)):
                    if n:
                        dve.wait_ge(first_ready, g + 1)
                        if not (isinstance(g, int) and g < 2):
                            dve.wait_ge(out_stored[b], u * 16)
                    for s in range(S):
                        last = dve.scalar_tensor_tensor(out=into[:, b, s], in0=res[:, b, n, s], scalar=T.gate[:, n, bass.ds(g * S + s, 1)],
                                                        in1=base[:, b, s], op0=ALU.mult, op1=ALU.add)
                    last.then_inc(ready, 1)

            places(0, 0)
            places(1, 1)
            for g in range(2):
                add(g, g % 2, 0)
                dve.wait_ge(out_ready, g + 1)
                places(g + 2, g % 2)
            with dve.Fori(1, (NG - 3) // 2) as i:
                for b in range(2):
                    add(i * 2 + b, b, i)
                    dve.wait_ge(out_ready, i * 2 + b + 1)
                    places(i * 2 + b + 2, b)
            for g in range(NG - 3, NG):
                add(g, g % 2, g // 2)
                if g + 2 < NG:
                    dve.wait_ge(out_ready, g + 1)
                    places(g + 2, g % 2)


class Tensors:

    def __init__(self, out, x, src, dst, W_s, W_t, W_attn, W_fc, b_fc, wq, bq, wk, bk, wv, bv, wo, bo,
                 gamma, beta, Wr, br, W1, b1, W2, b2):
        self.out, self.x, self.src, self.dst = out, x, src, dst
        self.W_s, self.W_t, self.W_attn, self.W_fc, self.b_fc = W_s, W_t, W_attn, W_fc, b_fc
        self.wq, self.bq, self.wk, self.bk, self.wv, self.bv, self.wo, self.bo = wq, bq, wk, bk, wv, bv, wo, bo
        self.gamma, self.beta, self.Wr, self.br = gamma, beta, Wr, br
        self.W1, self.b1, self.W2, self.b2 = W1, b1, W2, b2


def build(nc, out, **arrays):
    T = Tensors(out, **arrays)
    N = T.x.shape[0]
    T.NB = -(-N // P)
    T.xn_table = nc.dram_tensor("xn_table", [T.NB * P, XW], F32).ap()
    T.ps_table = nc.dram_tensor("ps_table", [N, D], F32).ap()
    T.pt_table = nc.dram_tensor("pt_table", [N, D], F32).ap()
    T.e_flat = nc.dram_tensor("e_flat", [T.src.shape[0]], F32).ap()
    T.x1_table = nc.dram_tensor("x1_table", [N, D], F32).ap()
    T.lists = nc.dram_tensor("lists", [T.W1.shape[0] * CAP, D], F32).ap()
    T.results = nc.dram_tensor("results", [BLOCKS * BLK, D], F32).ap()
    T.agg = nc.dram_tensor("agg", [T.NB * P, D], F32).ap()
    T.q_table = nc.dram_tensor("q_table", [K, P, N], F32).ap()
    with ExitStack() as ctx:
        m = Memory(nc, ctx, "all")
        T.ident = m.sb("ident", [P, P])
        T.w_fcT = m.sb("w_fcT", [P, K, D])
        T.kv = m.sb("kv", [P, K, P])
        T.ksum = m.sb("ksum", [P, K, P])
        T.e = m.sb("e", [R, T.src.shape[0] // R])
        T.shift = m.sb("shift", [P, T.NB, 2])
        T.plan = m.sb("plan", [1, 3, T.src.shape[0] // C + 1], I32)
        T.gate = m.sb("gate", [R, 2, N // R])
        T.slot = m.sb("slot", [R, 2, N // R], I32)
        T.moe = m.sb("moe", [1, 3, T.W1.shape[0] + 1], I32)
        T.far_i = m.sb("far_i", [1, 1], I32)
        T.passed = m.sem("passed")
        for step in STEPS:
            step(nc, T)


STEPS = [project, score, plan, reshift, aggregate, mix, experts, combine]


_INS = {
    "x": "x", "src": "src", "dst": "dst", "L0_gnn_W_s": "W_s", "L0_gnn_W_t": "W_t", "L0_gnn_W_attn": "W_attn",
    "L0_gnn_W_fc": "W_fc", "L0_gnn_b_fc": "b_fc", "L0_mix_wq": "wq", "L0_mix_bq": "bq", "L0_mix_wk": "wk",
    "L0_mix_bk": "bk", "L0_mix_wv": "wv", "L0_mix_bv": "bv", "L0_mix_wo": "wo", "L0_mix_bo": "bo",
    "L0_ffn_gamma": "gamma", "L0_ffn_beta": "beta", "L0_ffn_Wr": "Wr", "L0_ffn_br": "br", "L0_ffn_W1": "W1",
    "L0_ffn_b1": "b1", "L0_ffn_W2": "W2", "L0_ffn_b2": "b2",
}


def kernel(**inputs):
    import numpy as np
    import concourse.bacc as bacc
    from concourse.bass_utils import run_bass_kernel_spmd

    nc = bacc.Bacc("TRN2", target_bir_lowering=False, num_devices=1)
    arrays, args = {}, {}
    for name, short in _INS.items():
        a = np.ascontiguousarray(inputs[name])
        arrays[f"in_{short}"] = a
        args[short] = nc.dram_tensor(f"in_{short}", a.shape, mybir.dt.from_np(a.dtype), kind="ExternalInput").ap()
    out = nc.dram_tensor("out_x", inputs["x"].shape, F32, kind="ExternalOutput").ap()
    build(nc, out, **args)
    r = run_bass_kernel_spmd(nc, [arrays], core_ids=[0])
    return r.results[0]["out_x"]
```

```python
from contextlib import ExitStack

import concourse.bass as bass
from concourse import mybir

ALU = mybir.AluOpType
ACT = mybir.ActivationFunctionType
AX = mybir.AxisListType
F32 = mybir.dt.float32
I32 = mybir.dt.int32
U32 = mybir.dt.uint32

P = 128
R = 125
S = 4
G = R * S
D = 256
K = D // P
HEADS = 8
HD = D // HEADS
J = 4
C = R * J
H = 4
CR = C * H
JA, HA = 2 * J, H // 2
CA = R * JA
XW = D + 2
BLK = 512
CAP = 26 * BLK
FULL, BLOCKS = 48, 56
SLOPE = 0.2
SAFE = 60.0
FAR = 1.6e38
EPS = 1e-5


class Memory:

    def __init__(self, nc, ctx, prefix):
        self.nc, self.ctx, self.prefix, self.sems = nc, ctx, prefix, []
        ctx.callback(self.clear)

    def clear(self):
        self.nc.clear_and_free_semaphores(self.sems)
        self.nc.all_engine_barrier()

    def sb(self, name, shape, dt=F32):
        return self.ctx.enter_context(self.nc.sbuf_tensor(f"{self.prefix}_{name}", shape, dt))

    def ps(self, name, shape, dt=F32):
        return self.ctx.enter_context(self.nc.psum_tensor(f"{self.prefix}_{name}", shape, dt))

    def sem(self, name):
        self.sems.append(self.nc.alloc_semaphore(f"{self.prefix}_{name}"))
        return self.sems[-1]


def project(nc, T):
    NG = T.x.shape[0] // G
    with ExitStack() as ctx:
        m = Memory(nc, ctx, "pj")
        sb, ps, sem = m.sb, m.ps, m.sem
        w_raw = sb("w_raw", [P, 3, K, D])
        w_st = sb("w_st", [P, K, 2, D])
        w_kv = sb("w_kv", [P, K, 2, D])
        w_q = sb("w_q", [P, K, D])
        b_kv = sb("b_kv", [P, 2, D])
        b_q = sb("b_q", [P, K])
        x = sb("x", [R, 2, S, D])
        xn = sb("xn", [R, 2, S, D])
        stats = sb("stats", [R, S, 6])
        mv = sb("mv", [R, S, 2])
        var = sb("var", [R, S])
        half = sb("half", [R, S])
        rstd = sb("rstd", [R, S])
        xnT = sb("xnT", [P, K, G])
        proj = sb("proj", [R, 2, S, 2, D])
        kb = sb("kb", [R, 2, D])
        kpos = sb("kpos", [R, 2, D])
        kexp = sb("kexp", [R, 2, D])
        kf = sb("kf", [R, 2, S, D])
        v1 = sb("v1", [R, 2, S, K, P + 1])
        qpos = sb("qpos", [P, K, G])
        qexp = sb("qexp", [P, K, G])
        qf = sb("qf", [P, 2, K, G])
        zero = sb("zero", [R, 2 * (P + 1)])

        tp = ps("tp", [P, K, 512])
        p1 = ps("p1", [P, 2, 512])
        p2 = ps("p2", [P, 2, 512])
        pq = ps("pq", [P, 512])
        pkv = ps("pkv", [P, 512])

        weights_in = sem("weights_in")
        ident_zeroed, ident_ready, consts_ready = sem("ident_zeroed"), sem("ident_ready"), sem("consts_ready")
        w_turned, w_copied = sem("w_turned"), sem("w_copied")
        x_in = [sem(f"x_in{b}") for b in range(2)]
        var_ready = sem("var_ready")
        stats_ready, mv_ready, rstd_ready, xn_ready = sem("stats_ready"), sem("mv_ready"), sem("rstd_ready"), sem("xn_ready")
        xn_stored = [sem(f"xn_stored{b}") for b in range(2)]
        xn_turned, xnT_ready = sem("xn_turned"), sem("xnT_ready")
        p1_ready, p1_copied, p2_ready, p2_copied = sem("p1_ready"), sem("p1_copied"), sem("p2_ready"), sem("p2_copied")
        proj_stored = [sem(f"proj_stored{b}") for b in range(2)]
        kexp_ready, kpos_ready, kf_ready, kv_added = sem("kexp_ready"), sem("kpos_ready"), sem("kf_ready"), sem("kv_added")
        pq_ready, pq_read, qf_ready = sem("pq_ready"), sem("pq_read"), sem("qf_ready")
        q_stored = [sem(f"q_stored{b}") for b in range(2)]
        kv_cleared, kv_out = sem("kv_cleared"), sem("kv_out")

        block = ctx.enter_context(nc.Block())
        x_rows = T.x.rearrange("(g s p) d -> g p s d", s=S, p=R)
        xn_rows = T.xn_table[0:NG * G, :].rearrange("(g s p) d -> g p s d", s=S, p=R)
        ps_rows = T.ps_table.rearrange("(g s p) d -> g p s d", s=S, p=R)
        pt_rows = T.pt_table.rearrange("(g s p) d -> g p s d", s=S, p=R)
        q_cols = T.q_table.rearrange("k p (g n) -> g p k n", n=G)

        def steps(eng, body):
            body(0, 0, 0)
            body(1, 1, 0)
            body(2, 0, 1)
            with eng.Fori(1, (NG - 1) // 2) as i:
                body(i * 2 + 1, 1, i)
                body(i * 2 + 2, 0, i + 1)

        @block.sync
        def _(sp):
            for n, w in enumerate((T.W_s, T.W_t, T.W_fc)):
                sp.dma_start(w_raw[:, n], w.rearrange("(c p) i -> p c i", p=P)).then_inc(weights_in, 16)
            for n, w in enumerate((T.wk, T.wv)):
                sp.dma_start(w_kv[:, :, n, :], w.rearrange("(c p) o -> p c o", p=P)).then_inc(weights_in, 16)
            sp.dma_start(w_q[:], T.wq.rearrange("(c p) o -> p c o", p=P)).then_inc(weights_in, 16)
            for n, b in enumerate((T.bk, T.bv)):
                sp.dma_start(b_kv[:, n, :], b.partition_broadcast(P)).then_inc(weights_in, 16)
            for k in range(K):
                sp.dma_start(b_q[:, k:k + 1], T.bq[k * P:(k + 1) * P].rearrange("(p a) -> p a", a=1)).then_inc(weights_in, 16)

            def step(g, b, u):
                if not (isinstance(g, int) and g < 2):
                    sp.wait_ge(xn_ready, g - 1)
                sp.dma_start(x[:, b], x_rows[g]).then_inc(x_in[b], 16)
                if not (isinstance(g, int) and g < 1):
                    c = 1 - b
                    sp.wait_ge(xn_ready, g)
                    sp.dma_start(xn_rows[g - 1, :, :, 0:D], xn[:, c]).then_inc(xn_stored[c], 16)

            steps(sp, step)
            sp.wait_ge(xn_ready, NG)
            sp.dma_start(xn_rows[NG - 1, :, :, 0:D], xn[:, (NG - 1) % 2]).then_inc(xn_stored[(NG - 1) % 2], 16)
            for b in range(2):
                n = (NG + 1 - b) // 2
                sp.wait_ge(xn_stored[b], 16 * n)
                sp.wait_ge(proj_stored[b], 32 * n)
                sp.wait_ge(q_stored[b], 16 * n)

        @block.gpsimd
        def _(pool):
            pool.memset(T.ident[:], 0.0).then_inc(ident_zeroed, 1)
            pool.wait_ge(ident_zeroed, 1)
            pool.affine_select(out=T.ident[:], in_=T.ident[:], compare_op=ALU.not_equal, fill=1.0, base=0,
                               pattern=[[-1, P]], channel_multiplier=1).then_inc(ident_ready, 1)
            pool.memset(v1[:], 1.0)
            pool.memset(half[:], -0.5)
            pool.memset(zero[:], 0.0).then_inc(consts_ready, 1)

            def step(g, b, u):
                pool.wait_ge(mv_ready, g + 1)
                pool.sem_inc(T.passed, 1)
                pool.tensor_scalar(var[:], mv[:, :, 1], EPS, None, ALU.add).then_inc(var_ready, 1)
                pool.wait_ge(var_ready, g + 1)
                pool.tensor_tensor(rstd[:], var[:], half[:], ALU.pow).then_inc(rstd_ready, 1)

            steps(pool, step)

        @block.tensor
        def _(pe):
            pe.wait_ge(consts_ready, 1)
            pe.wait_ge(ident_ready, 1)
            pe.matmul(pkv[:, 0:2 * (P + 1)], zero[:, 0:P], zero[:], start=True, stop=False,
                      skip_group_check=True).then_inc(kv_cleared, 1)
            pe.wait_ge(weights_in, 16 * 10)
            n = 0
            for w in range(3):
                for i in range(K):
                    for o in range(K):
                        if n >= 2:
                            pe.wait_ge(w_copied, n - 1)
                        pe.transpose(tp[:, n % 2, 0:P], w_raw[:, w, o, i * P:(i + 1) * P], T.ident[:]).then_inc(w_turned, 1)
                        n += 1
            pe.wait_ge(w_copied, n)

            def add_kv(g, b, s):
                pe.wait_ge(kf_ready, g * S + s + 1)
                for k in range(K):
                    mm = pe.matmul(pkv[:, k * (P + 1):(k + 1) * (P + 1)], kf[:, b, s, k * P:(k + 1) * P],
                                   v1[:, b, s, k, :], start=False, stop=False, skip_group_check=True)
                mm.then_inc(kv_added, 1)

            def step(g, b, u):
                first = isinstance(g, int) and g == 0
                pe.wait_ge(xn_ready, g + 1)
                for k in range(K):
                    if not first:
                        pe.wait_ge(xnT_ready, g * K)
                    for s in range(S):
                        t = pe.transpose(tp[:, k, s * R:(s + 1) * R], xn[:, b, s, k * P:(k + 1) * P], T.ident[0:R, 0:R])
                    t.then_inc(xn_turned, 1)
                pe.wait_ge(xnT_ready, g * K + K)
                for s in range(S):
                    for out, w, ready, copied in ((p1, w_st, p1_ready, p1_copied), (p2, w_kv, p2_ready, p2_copied)):
                        if not (first and s < 2):
                            pe.wait_ge(copied, g * S + s - 1)
                        for k in range(K):
                            mm = pe.matmul(out[0:R, s % 2, :], xnT[:, k, s * R:(s + 1) * R],
                                           w[:, k].rearrange("p a d -> p (a d)"), start=k == 0, stop=k == K - 1)
                        mm.then_inc(ready, 1)
                for h in range(K):
                    if not (first and h == 0):
                        pe.wait_ge(pq_read, (g * K + h) * 2)
                    for k in range(K):
                        mm = pe.matmul(pq[:, 0:G], w_q[:, k, h * P:(h + 1) * P], xnT[:, k, :], start=k == 0, stop=k == K - 1)
                    mm.then_inc(pq_ready, 1)
                if not first:
                    for s in range(S):
                        add_kv(g - 1, 1 - b, s)

            steps(pe, step)
            for s in range(S):
                add_kv(NG - 1, (NG - 1) % 2, s)

        @block.scalar
        def _(act):
            act.wait_ge(weights_in, 16 * 10)

            def step(g, b, u):
                first = isinstance(g, int) and g == 0
                for k in range(K):
                    act.wait_ge(xn_turned, g * K + k + 1)
                    act.copy(xnT[:, k, :], tp[:, k, 0:G]).then_inc(xnT_ready, 1)
                if not (isinstance(g, int) and g < 2):
                    act.wait_ge(proj_stored[b], 32 * u)
                for s in range(S):
                    act.wait_ge(p1_ready, g * S + s + 1)
                    act.copy(proj[:, b, s].rearrange("p a d -> p (a d)"), p1[0:R, s % 2, :]).then_inc(p1_copied, 1)
                    act.wait_ge(p2_copied, g * S + s + 1)
                    if not (first and s < 2):
                        act.wait_ge(kf_ready, g * S + s - 1)
                    act.activation(kexp[:, s % 2], kb[:, s % 2], ACT.Exp).then_inc(kexp_ready, 1)
                for h in range(K):
                    act.wait_ge(pq_ready, g * K + h + 1)
                    if not first:
                        act.wait_ge(qf_ready, g * K + h - K + 1)
                    act.activation(qexp[:, h, :], pq[:, 0:G], ACT.Exp, bias=b_q[:, h:h + 1]).then_inc(pq_read, 1)
                act.wait_ge(p1_copied, g * S + S)
                act.dma_start(ps_rows[g], proj[:, b, :, 0, :]).then_inc(proj_stored[b], 16)
                act.dma_start(pt_rows[g], proj[:, b, :, 1, :]).then_inc(proj_stored[b], 16)
                act.wait_ge(qf_ready, g * K + K)
                act.dma_start(q_cols[g], qf[:, b]).then_inc(q_stored[b], 16)

            steps(act, step)

        @block.vector
        def _(dve):
            n = 0
            for w in range(3):
                for i in range(K):
                    for o in range(K):
                        dve.wait_ge(w_turned, n + 1)
                        dst = T.w_fcT[:, i, o * P:(o + 1) * P] if w == 2 else w_st[:, i, w, o * P:(o + 1) * P]
                        dve.tensor_copy(dst, tp[:, n % 2, 0:P]).then_inc(w_copied, 1)
                        n += 1
            dve.wait_ge(weights_in, 16 * 10)
            dve.wait_ge(consts_ready, 1)

            def norm(g, b, u):
                dve.wait_ge(x_in[b], u * 16 + 16)
                if not (isinstance(g, int) and g == 0):
                    dve.wait_ge(mv_ready, g)
                for s in range(S):
                    last = dve.bn_stats(stats[:, s, :], x[:, b, s, :])
                last.then_inc(stats_ready, 1)
                dve.wait_ge(stats_ready, g + 1)
                if not (isinstance(g, int) and g == 0):
                    dve.wait_ge(xn_ready, g)
                dve.sem_inc(T.passed, 1)
                for s in range(S):
                    last = dve.bn_aggr(mv[:, s, :], stats[:, s, :])
                last.then_inc(mv_ready, 1)
                dve.wait_ge(rstd_ready, g + 1)
                if not (isinstance(g, int) and g < 2):
                    dve.wait_ge(xn_stored[b], 16 * u)
                    dve.wait_ge(xn_turned, (g - 1) * K)
                for s in range(S):
                    last = dve.tensor_scalar(xn[:, b, s, :], x[:, b, s, :], mv[:, s, 0:1], rstd[:, s:s + 1], ALU.subtract, ALU.mult)
                last.then_inc(xn_ready, 1)

            def keys(g, b, u):
                first = isinstance(g, int) and g == 0
                if not (isinstance(g, int) and g < 2):
                    dve.wait_ge(kv_added, (g - 1) * S)

                def feature(s):
                    dve.wait_ge(kexp_ready, g * S + s + 1)
                    dve.wait_ge(kpos_ready, g * S + s + 1)
                    dve.scalar_tensor_tensor(out=kf[:, b, s, :], in0=kexp[:, s % 2], scalar=1.0, in1=kpos[:, s % 2],
                                             op0=ALU.min, op1=ALU.add).then_inc(kf_ready, 1)

                for s in range(S):
                    dve.wait_ge(p2_ready, g * S + s + 1)
                    dve.tensor_tensor(v1[:, b, s, :, 0:P], p2[0:R, s % 2, D:2 * D].rearrange("p (k d) -> p k d", k=K),
                                      b_kv[0:R, 1, :].rearrange("p (k d) -> p k d", k=K), ALU.add)
                    if not (first and s < 2):
                        dve.wait_ge(kf_ready, g * S + s - 1)
                        dve.wait_ge(kpos_ready, g * S + s - 1)
                    dve.tensor_tensor(kb[:, s % 2], p2[0:R, s % 2, 0:D], b_kv[0:R, 0, :], ALU.add).then_inc(p2_copied, 1)
                    dve.wait_ge(p2_copied, g * S + s + 1)
                    dve.tensor_scalar(kpos[:, s % 2], kb[:, s % 2], 0.0, None, ALU.max).then_inc(kpos_ready, 1)
                    if s >= 1:
                        feature(s - 1)
                feature(S - 1)
                if not (isinstance(g, int) and g < 2):
                    dve.wait_ge(q_stored[b], 16 * u)
                for h in range(K):
                    dve.wait_ge(pq_read, (g * K + h) * 2 + 1)
                    if not first:
                        dve.wait_ge(qf_ready, g * K + h - K + 1)
                    dve.tensor_scalar(qpos[:, h, :], pq[:, 0:G], b_q[:, h:h + 1], 0.0, ALU.add, ALU.max).then_inc(pq_read, 1)
                    dve.wait_ge(pq_read, (g * K + h + 1) * 2)
                    dve.scalar_tensor_tensor(out=qf[:, b, h, :], in0=qexp[:, h, :], scalar=1.0, in1=qpos[:, h, :],
                                             op0=ALU.min, op1=ALU.add).then_inc(qf_ready, 1)

            norm(0, 0, 0)
            norm(1, 1, 0)
            keys(0, 0, 0)
            norm(2, 0, 1)
            keys(1, 1, 0)
            with dve.Fori(1, (NG - 1) // 2) as i:
                norm(i * 2 + 1, 1, i)
                keys(i * 2, 0, i)
                norm(i * 2 + 2, 0, i + 1)
                keys(i * 2 + 1, 1, i)
            keys(NG - 1, (NG - 1) % 2, (NG - 1) // 2)
            dve.memset(T.kv[:], 0.0)
            dve.memset(T.ksum[:], 0.0).then_inc(kv_out, 1)
            dve.wait_ge(kv_out, 1)
            dve.wait_ge(kv_added, NG * S)
            for k in range(K):
                for h in range(P // HD):
                    a, z = h * HD, (h + 1) * HD
                    dve.tensor_copy(T.kv[a:z, k, a:z], pkv[a:z, k * (P + 1) + a:k * (P + 1) + z])
                    dve.tensor_copy(T.ksum[a:z, k, a:z], pkv[a:z, k * (P + 1) + P:k * (P + 1) + P + 1].broadcast_to([HD, HD]))
            


def index(nc, T):
    E = T.src.shape[0]
    NC = E // C
    A = NC // H
    W = E // A
    LO = P.bit_length() - 1
    B4 = 4
    with ExitStack() as ctx:
        m = Memory(nc, ctx, "ix")
        sb, ps, sem = m.sb, m.ps, m.sem
        raw = sb("raw", [A, 2, W], I32)
        flat = sb("flat", [A, 2, W])
        low_i = sb("low_i", [R, E // R], I32)
        src_i = sb("src_i", [R, E // R], I32)
        ext = sb("ext", [A, 2, H])
        row = sb("row", [1, 2, H, A])
        row_i = sb("row_i", [1, 2, H, A], I32)
        blk = sb("blk", [1, 2, H, A])
        count = sb("count", [1, NC])
        ones = sb("ones", [1, NC])
        before = sb("before", [1, NC])
        tp = ps("tp", [P, 2, 512])
        te = ps("te", [P, 2 * H * P])
        raw_in, flat_ready, flat_out = sem("raw_in"), sem("flat_ready"), sem("flat_out")
        pad_ready, pt_in = sem("pad_ready"), sem("pt_in")
        N = T.x.shape[0]
        full = N // P
        turned, copied, ext_ready, ext_turned, chain = (sem("turned"), sem("copied"), sem("ext_ready"),
                                                        sem("ext_turned"), sem("step_done"))
        block = ctx.enter_context(nc.Block())
        tiles = W // R
        turns = 2 * tiles // B4

        @block.sync
        def _(sp):
            for n, a in enumerate((T.src, T.dst)):
                sp.dma_start(raw[:, n], a.rearrange("(a w) -> a w", w=W)).then_inc(raw_in, 16)
            sp.dma_start(T.pt[:, 0:full, :], T.pt_table[0:full * P, :].rearrange("(b p) d -> p b d", p=P)).then_inc(pt_in, 16)
            sp.wait_ge(pad_ready, 1)
            sp.dma_start(T.pt[0:N - full * P, full, :], T.pt_table[full * P:N, :]).then_inc(pt_in, 16)
            sp.wait_ge(flat_ready, 2)
            sp.dma_start(T.dst_flat.rearrange("(a w) -> a w", w=W), flat[:, 1]).then_inc(flat_out, 16)
            sp.wait_ge(flat_out, 16)
            sp.wait_ge(pt_in, 32)

        @block.tensor
        def _(pe):
            n = 0
            for w in range(2):
                pe.wait_ge(flat_ready, w + 1)
                for q in range(tiles // B4):
                    if n >= 2:
                        pe.wait_ge(copied, n - 1)
                    for t in range(B4):
                        at = (q * B4 + t) * R
                        mm = pe.transpose(tp[0:R, n % 2, t * P:t * P + A], flat[:, w, at:at + R], T.ident[0:A, 0:A])
                    mm.then_inc(turned, 1)
                    n += 1
            pe.wait_ge(ext_ready, 1)
            for k in range(2):
                for h in range(H):
                    at = (k * H + h) * P
                    mm = pe.transpose(te[0:1, at:at + A], ext[:, k, h:h + 1], T.ident[0:A, 0:A])
            mm.then_inc(ext_turned, 1)

        @block.scalar
        def _(act):
            for n in range(turns):
                to = (T.src_t, T.dst_t)[n // (turns // 2)]
                q = n % (turns // 2)
                act.wait_ge(turned, n + 1)
                act.copy(to[:].rearrange("p (a t) -> p t a", t=tiles)[:, q * B4:(q + 1) * B4, :],
                         tp[0:R, n % 2].rearrange("p (t a) -> p t a", a=P)[:, :, 0:A]).then_inc(copied, 1)

        @block.vector
        def _(dve):
            done = 0

            def then(ins):
                nonlocal done
                done += 1
                ins.then_inc(chain, 1)
                dve.wait_ge(chain, done)

            dve.memset(T.pt[:, full, :], 0.0).then_inc(pad_ready, 1)
            dve.wait_ge(raw_in, 32)
            for w in range(2):
                dve.tensor_copy(flat[:, w], raw[:, w]).then_inc(flat_ready, 1)
            dve.wait_ge(flat_ready, 2)
            chunks = flat[:, 1].rearrange("a (h c) -> a h c", h=H)
            dve.tensor_reduce(ext[:, 0], chunks, AX.X, ALU.max)
            dve.tensor_reduce(ext[:, 1], chunks, AX.X, ALU.min).then_inc(ext_ready, 1)
            dve.wait_ge(ext_turned, 1)
            then(dve.tensor_copy(row[:].rearrange("o k h a -> o (k h) a"),
                                 te[0:1].rearrange("o (n a) -> o n a", a=P)[:, :, 0:A]))
            then(dve.tensor_copy(row_i[:], row[:]))
            then(dve.tensor_scalar(row_i[:], row_i[:], LO, None, ALU.arith_shift_right))
            then(dve.tensor_copy(blk[:], row_i[:]))
            then(dve.memset(ones[:], 1.0))
            for plan, n in ((T.plan, H), (T.plan_a, HA)):
                if n == HA:
                    for h in range(HA):
                        then(dve.tensor_tensor(blk[:, 0, h, :], blk[:, 0, 2 * h, :], blk[:, 0, 2 * h + 1, :], ALU.max))
                        then(dve.tensor_tensor(blk[:, 1, h, :], blk[:, 1, 2 * h, :], blk[:, 1, 2 * h + 1, :], ALU.min))
                NCn = A * n
                then(dve.memset(plan[:], 0))
                then(dve.tensor_copy(plan[:, 0, 1:NCn + 1].rearrange("o (a h) -> o h a", h=n), blk[:, 0, 0:n]))
                then(dve.tensor_copy(plan[:, 1, 0:NCn].rearrange("o (a h) -> o h a", h=n), blk[:, 1, 0:n]))
                then(dve.tensor_tensor(count[:, 0:NCn].rearrange("o (a h) -> o h a", h=n), blk[:, 0, 0:n], blk[:, 1, 0:n], ALU.subtract))
                then(dve.tensor_tensor_scan(before[:, 0:NCn], ones[:, 0:NCn], count[:, 0:NCn], 0.0, ALU.mult, ALU.add))
                then(dve.tensor_copy(plan[:, 2, 1:NCn + 1], before[:, 0:NCn]))
            dve.wait_ge(copied, turns // 2)
            then(dve.tensor_copy(src_i[:], T.src_t[:]))
            then(dve.tensor_scalar(low_i[:], src_i[:], P - 1, None, ALU.bitwise_and))
            then(dve.tensor_copy(T.src_low[:, 0, :], low_i[:]))
            then(dve.tensor_scalar(src_i[:], src_i[:], LO, None, ALU.arith_shift_right))
            then(dve.tensor_copy(T.src_low[:, 1, :], src_i[:]))


def spans(eng, T, c):
    top = T.NB - 1
    last = eng.value_load(T.plan[0:1, 0, bass.ds(c + 1, 1)], min_val=0, max_val=top)
    first = eng.value_load(T.plan[0:1, 1, bass.ds(c, 1)], min_val=0, max_val=top)
    before = eng.value_load(T.plan[0:1, 2, bass.ds(c, 1)], min_val=0, max_val=top * (T.src.shape[0] // C))
    return first, last - first, before


def planned(eng, T, c, with_prev=True):
    top = T.NB - 1
    prev = eng.value_load(T.plan_a[0:1, 0, bass.ds(c, 1)], min_val=0, max_val=top) if with_prev else None
    last = eng.value_load(T.plan_a[0:1, 0, bass.ds(c + 1, 1)], min_val=0, max_val=top)
    first = eng.value_load(T.plan_a[0:1, 1, bass.ds(c, 1)], min_val=0, max_val=top)
    more = eng.value_load(T.plan_a[0:1, 2, bass.ds(c, 1)], min_val=0, max_val=top * (T.src.shape[0] // CA))
    return prev, first, last, more + c


def by_four(eng, body, NC, tail):
    for c in range(4):
        body(c, c, 0)
    with eng.Fori(1, NC // 4 - tail) as i:
        for b in range(4):
            body(i * 4 + b, b, i)
    if tail:
        for b in range(4):
            body(NC - 4 + b, b, NC // 4 - 1)


def by_four_ahead(eng, load, body, NC, tail):
    U = 8

    def turn(c0, i):
        regs = [load(c0)]
        for n in range(U):
            body(c0 + n, n % 4, i + n // 4, regs[n], lambda n=n: regs.append(load(c0 + n + 1) if n + 1 < U else None))

    turn(0, 0)
    with eng.Fori(1, NC // U - tail) as i:
        turn(i * U, i * (U // 4))
    if tail:
        turn(NC - U, (NC - U) // 4)


def from_(c, n):
    return not isinstance(c, int) or c >= n


def score(nc, T):
    E = T.src.shape[0]
    NC = E // C
    with ExitStack() as ctx:
        m = Memory(nc, ctx, "sc")
        sb, ps, sem = m.sb, m.ps, m.sem
        pt = T.pt
        src_i = sb("src_i", [R, 4, J], I32)
        w_attn = sb("w_attn", [P, D])
        rows_i = sb("rows_i", [R, P], I32)
        iota = sb("iota", [R, P])
        node_i = sb("node_i", [P, T.NB], I32)
        node = sb("node", [P, T.NB])
        minus_node = sb("minus_node", [P, T.NB])
        dst_b = sb("dst_b", [P, 4, C])
        off_first = [sb(f"off_first{b}", [P, C]) for b in range(4)]
        off_more = sb("off_more", [P, C])
        hot_first = [sb(f"hot_first{b}", [P, C]) for b in range(4)]
        hot_more = sb("hot_more", [P, C])
        src_p = sb("src_p", [R, 4, J, D])
        z = sb("z", [R, 2, J, D])
        dot = sb("dot", [R, 2, J])
        cut = sb("cut", [R, 2, J])
        ex = sb("ex", [R, 2, J])
        low = sb("low", [R, 2, 2, J])
        hot_row = sb("hot_row", [R, 2, J, P])
        hot_blk = sb("hot_blk", [R, 2, J, T.NB])
        zero = sb("zero", [R, P])
        sums = sb("sums", [P, T.NB])
        zt = ps("zt", [P, 2, J, D])
        total = ps("total", [P, 512])

        w_in = sem("w_in")
        iota_made, iota_ready, node_ready = sem("iota_made"), sem("iota_ready"), sem("node_ready")
        src_ready = sem("src_ready")
        dst_in = [sem(f"dst_in{b}") for b in range(4)]
        dst_used = sem("dst_used")
        first_off, first_ready, first_used = sem("first_off"), sem("first_ready"), sem("first_used")
        more_off, more_ready, more_used = sem("more_off"), sem("more_ready"), sem("more_used")
        rows_in = [sem(f"rows_in{b}") for b in range(4)]
        z_made, up_ready, z_ready, dots_ready, scores_ready, cut_ready, exp_ready = (sem("z_made"), sem("up_ready"), sem("z_ready"), sem("dots_ready"), sem("scores_ready"),
                                                                   sem("cut_ready"), sem("exp_ready"))
        low_ready, hot_ready, hot_used, shift_ready = sem("low_ready"), sem("hot_ready"), sem("hot_used"), sem("shift_ready")

        block = ctx.enter_context(nc.Block())

        @block.sync
        def _(sp):
            sp.dma_start(w_attn[:], T.W_attn.rearrange("a d -> (a d)").partition_broadcast(P)).then_inc(w_in, 16)

            def load(c, b):
                if from_(c, 4):
                    sp.wait_ge(dst_used, c - 3)
                sp.dma_start(dst_b[:, b], T.dst_flat[bass.ds(c * C, C)].partition_broadcast(P)).then_inc(dst_in[b], 16)

            load(0, 0)
            load(1, 1)
            load(2, 2)
            load(3, 3)
            with sp.Fori(1, NC // 4) as i:
                for b in range(4):
                    load(i * 4 + b, b)

        @block.gpsimd
        def _(pool):
            pool.iota(rows_i[:], [[1, P]], base=0, channel_multiplier=0)
            pool.iota(node_i[:], [[P, T.NB]], base=0, channel_multiplier=1).then_inc(iota_made, 1)
            pool.memset(zero[:], 0.0)
            pool.wait_ge(iota_made, 1)
            pool.tensor_copy(node[:], node_i[:])
            pool.tensor_copy(iota[:], rows_i[:]).then_inc(iota_ready, 1)

            def gather(c, b, i):
                pool.wait_ge(src_ready, c + 1)
                if from_(c, 4):
                    pool.wait_ge(z_made, c - 3)
                pool.sem_inc(T.passed, 1)
                for j in range(J):
                    pool.indirect_dma_start(
                        out=src_p[:, b, j, :], out_offset=None, in_=T.ps_table,
                        in_offset=bass.IndirectOffsetOnAxis(ap=src_i[:, b, j:j + 1], axis=0),
                    ).then_inc(rows_in[b], 16)

            by_four(pool, gather, NC, 0)

        @block.scalar
        def _(act):
            def indices(c, b):
                act.copy(src_i[:, b], T.src_t[:, bass.ds(c * J, J)]).then_inc(src_ready, 1)

            def hot_of_first(c, b, i, regs):
                first, more, before = regs
                act.wait_ge(dst_in[b], i * 16 + 16)
                if from_(c, 4):
                    act.wait_ge(first_ready, c - 2)
                act.sem_inc(T.passed, 1)
                act.activation(off_first[b][:], dst_b[:, b, :], ACT.Abs, bias=minus_node[:, bass.ds(first, 1)]).then_inc(first_off, 1)
                act.wait_ge(first_off, c + 1)
                if from_(c, 4):
                    act.wait_ge(first_used, c - 2)
                act.activation(hot_first[b][:], off_first[b][:], ACT.Relu, bias=1.0, scale=-1.0).then_inc(first_ready, 1)

            def hots_of_more(b, regs):
                first, more, before = regs
                with act.If(more > 0):
                    with act.Fori(0, more) as d:
                        blk = nc.s_assert_within(first + d + 1, 1, T.NB - 1, skip_runtime_bounds_check_because="it is at most last")
                        act.wait_ge(more_ready, before + d + 1)
                        act.sem_inc(T.passed, 1)
                        act.activation(off_more[:], dst_b[:, b, :], ACT.Abs, bias=minus_node[:, bass.ds(blk, 1)]).then_inc(more_off, 1)
                        act.wait_ge(more_off, before + d + 1)
                        act.wait_ge(more_used, before + d + 1)
                        act.activation(hot_more[:], off_more[:], ACT.Relu, bias=1.0, scale=-1.0).then_inc(more_ready, 1)
                act.sem_inc(dst_used, 1)

            def relu(c, b):
                act.wait_ge(z_made, c + 1)
                if from_(c, 2):
                    act.wait_ge(dots_ready, c - 1)
                act.activation(z[:, b % 2], zt[0:R, b % 2], ACT.Relu, scale=1.0 - SLOPE).then_inc(up_ready, 1)

            def exps(c, b):
                act.wait_ge(cut_ready, c + 1)
                if from_(c, 2):
                    act.wait_ge(hot_ready, c - 1)
                act.activation(ex[:, b % 2], cut[:, b % 2], ACT.Exp).then_inc(exp_ready, 1)

            for c in range(4):
                indices(c, c)
            act.sem_inc(first_ready, 1)
            act.sem_inc(more_ready, 1)
            act.wait_ge(node_ready, 1)
            for c in range(2):
                regs = spans(act, T, c)
                hot_of_first(c, c, 0, regs)
                hots_of_more(c, regs)

            def body(c, b, i, regs, ahead):
                if not isinstance(c, int) or c + 2 < NC:
                    hot_of_first(c + 2, (b + 2) % 4, i + (b + 2) // 4, regs)
                ahead()
                relu(c, b)
                if from_(c, 1):
                    exps(c - 1, b - 1)
                if not isinstance(c, int) or c + 4 < NC:
                    indices(c + 4, b)
                if not isinstance(c, int) or c + 2 < NC:
                    hots_of_more((b + 2) % 4, regs)

            by_four_ahead(act, lambda c: spans(act, T, c + 2) if not isinstance(c, int) or c + 2 < NC else None, body, NC, 1)
            exps(NC - 1, 1)

        @block.tensor
        def _(pe):
            pe.wait_ge(iota_ready, 1)
            pe.matmul(total[:, 0:T.NB], zero[:, 0:P], zero[:, 0:T.NB], start=True, stop=False, skip_group_check=True)
            pe.sem_inc(first_used, 1)
            pe.sem_inc(more_used, 1)

            def products(b, blk, hots, start):
                for j in range(J):
                    hot = hots[:, j * R:(j + 1) * R]
                    mm = pe.matmul(zt[0:R, b % 2, j, :], hot, pt[:, bass.ds(blk, 1), :].rearrange("p a d -> p (a d)"),
                                   start=start and j % 2 == 0, stop=False, skip_group_check=True)
                return mm

            def add(c, b):
                pe.wait_ge(hot_ready, c + 1)
                for j in range(J):
                    mm = pe.matmul(total[:, 0:T.NB], hot_row[:, b % 2, j], hot_blk[:, b % 2, j], start=False, stop=False,
                                   skip_group_check=True)
                mm.then_inc(hot_used, 1)

            def body(c, b, i, regs, ahead):
                first, more, before = regs
                if from_(c, 2):
                    pe.wait_ge(z_ready, c - 1)
                pe.wait_ge(first_ready, c + 2)
                products(b, first, hot_first[b], True).then_inc(first_used, 1)
                with pe.If(more > 0):
                    with pe.Fori(0, more) as d:
                        blk = nc.s_assert_within(first + d + 1, 1, T.NB - 1, skip_runtime_bounds_check_because="it is at most last")
                        pe.wait_ge(more_ready, before + d + 2)
                        products(b, blk, hot_more, False).then_inc(more_used, 1)
                pe.wait_ge(rows_in[b], i * (J * 16) + J * 16)
                for j in range(J):
                    mm = pe.matmul(zt[0:R, b % 2, j, :], T.ident[0:R, 0:R], src_p[:, b, j, :], start=False, stop=False,
                                   skip_group_check=True)
                mm.then_inc(z_made, 1)
                ahead()
                if from_(c, 3):
                    add(c - 3, b + 1)

            by_four_ahead(pe, lambda c: spans(pe, T, c), body, NC, 0)
            add(NC - 3, 1)
            add(NC - 2, 0)
            add(NC - 1, 1)

        @block.vector
        def _(dve):
            dve.wait_ge(iota_ready, 1)
            dve.tensor_scalar(minus_node[:], node[:], -1.0, None, ALU.mult).then_inc(node_ready, 1)
            dve.wait_ge(w_in, 16)

            def hots(c, b):
                b = b % 2
                dve.wait_ge(exp_ready, c + 1)
                dve.wait_ge(low_ready, c + 1)
                if from_(c, 2):
                    dve.wait_ge(hot_used, c - 1)
                dve.tensor_tensor(hot_row[:, b], iota[:].unsqueeze(1).broadcast_to([R, J, P]),
                                  low[:, b, 0, :].unsqueeze(2).broadcast_to([R, J, P]), ALU.is_equal)
                for j in range(J):
                    last = dve.tensor_scalar(hot_blk[:, b, j], iota[:, 0:T.NB], low[:, b, 1, j:j + 1], ex[:, b, j:j + 1],
                                             ALU.is_equal, ALU.mult)
                last.then_inc(hot_ready, 1)

            def body(c, b, i):
                b2 = b % 2
                dve.wait_ge(up_ready, c + 1)
                dve.scalar_tensor_tensor(out=z[:, b2], in0=zt[0:R, b2], scalar=SLOPE, in1=z[:, b2],
                                         op0=ALU.mult, op1=ALU.add).then_inc(z_ready, 1)
                if from_(c, 2):
                    dve.wait_ge(hot_ready, c - 1)
                dve.tensor_copy(low[:, b2], T.src_low[:, :, bass.ds(c * J, J)]).then_inc(low_ready, 1)
                dve.wait_ge(z_ready, c + 1)
                if from_(c, 2):
                    dve.wait_ge(scores_ready, c - 1)
                for j in range(J):
                    last = dve.scalar_tensor_tensor(out=z[:, b2, j], in0=z[:, b2, j], scalar=1.0, in1=w_attn[0:R],
                                                    op0=ALU.mult, op1=ALU.mult, accum_out=dot[:, b2, j:j + 1])
                last.then_inc(dots_ready, 1)
                if from_(c, 1):
                    hots(c - 1, b - 1)
                dve.wait_ge(dots_ready, c + 1)
                score = T.e[:, bass.ds(c * J, J)]
                dve.tensor_copy(score, dot[:, b2]).then_inc(scores_ready, 1)
                if from_(c, 2):
                    dve.wait_ge(exp_ready, c - 1)
                dve.tensor_scalar(cut[:, b2], dot[:, b2], SAFE, None, ALU.min).then_inc(cut_ready, 1)

            by_four(dve, body, NC, 0)
            hots(NC - 1, 1)
            dve.memset(T.shift[:], 0.0).then_inc(shift_ready, 1)
            dve.wait_ge(shift_ready, 1)
            dve.wait_ge(hot_used, NC)
            dve.tensor_scalar(sums[:], total[:, 0:T.NB], 1e-37, None, ALU.max).then_inc(shift_ready, 1)
            dve.wait_ge(shift_ready, 2)
            dve.reciprocal(T.shift[:, :, 1], sums[:])


def edges(nc, T):
    with ExitStack() as ctx:
        T.pt = Memory(nc, ctx, "ed").sb("pt", [P, T.NB, D])
        index(nc, T)
        score(nc, T)


def extent(nc, T):
    with ExitStack() as ctx:
        m = Memory(nc, ctx, "xt")
        sb, ps, sem = m.sb, m.ps, m.sem
        ext = sb("ext", [R, 2])
        extT = sb("extT", [1, 1])
        span = sb("span", [R, 1])
        tp = ps("tp", [P, 512])
        chain, turned = sem("step_done"), sem("turned")
        block = ctx.enter_context(nc.Block())

        @block.tensor
        def _(pe):
            pe.wait_ge(chain, 4)
            pe.transpose(tp[0:1, 0:R], span[:], T.ident[0:R, 0:R]).then_inc(turned, 1)

        @block.vector
        def _(dve):
            done = 0

            def then(ins):
                nonlocal done
                done += 1
                ins.then_inc(chain, 1)
                dve.wait_ge(chain, done)

            then(dve.tensor_reduce(ext[:, 0:1], T.e[:], AX.X, ALU.max))
            then(dve.tensor_reduce(ext[:, 1:2], T.e[:], AX.X, ALU.min))
            then(dve.tensor_scalar(span[:], ext[:, 1:2], -1.0, None, ALU.mult))
            then(dve.tensor_tensor(span[:], span[:], ext[:, 0:1], ALU.max))
            dve.wait_ge(turned, 1)
            then(dve.tensor_reduce(extT[:], tp[0:1, 0:R], AX.X, ALU.max))
            then(dve.tensor_scalar(T.far_i[:], extT[:], SAFE, None, ALU.is_gt))


def reshift(nc, T):
    NC = T.src.shape[0] // CR
    NB = T.NB
    with ExitStack() as ctx:
        m = Memory(nc, ctx, "rs")
        sb, sem = m.sb, m.sem
        src_in = sb("src_in", [P, CR])
        src_f = sb("src_f", [P, CR])
        e = sb("e", [P, CR])
        t = sb("t", [P, CR])
        part = sb("part", [P, 1])
        node_i = sb("node_i", [P, NB], I32)
        node = sb("node", [P, NB])
        top = sb("top", [P, NB])
        total = sb("total", [P, NB])
        kept, chunk_in, chunk_used = sem("kept"), sem("chunk_in"), sem("chunk_used")
        made, ready, chain = sem("made"), sem("ready"), sem("chain")
        shifted, ex_ready = sem("shifted"), sem("ex_ready")

        block = ctx.enter_context(nc.Block())

        @block.sync
        def _(sp):
            far = sp.value_load(T.far_i[0:1, 0:1], min_val=0, max_val=1)
            with sp.If(far > 0):
                sp.dma_start(T.e_flat.rearrange("(c p j) -> p c j", p=R, j=H * J),
                             T.e[:].rearrange("p (c j) -> p c j", j=H * J)).then_inc(kept, 16)
                sp.dma_start(T.src_flat.rearrange("(c p j) -> p c j", p=R, j=H * J),
                             T.src_t[:].rearrange("p (c j) -> p c j", j=H * J)).then_inc(kept, 16)
                sp.wait_ge(kept, 32)
                for sweep in range(2):
                    with sp.Fori(0, NC) as c:
                        sp.wait_ge(chunk_used, c + sweep * NC + 1)
                        sp.dma_start(src_in[:], T.src_flat[bass.ds(c * CR, CR)].partition_broadcast(P)).then_inc(chunk_in, 16)
                        sp.dma_start(e[:], T.e_flat[bass.ds(c * CR, CR)].partition_broadcast(P)).then_inc(chunk_in, 16)

        @block.gpsimd
        def _(pool):
            pool.iota(node_i[:], [[P, NB]], base=0, channel_multiplier=1).then_inc(made, 1)
            pool.wait_ge(made, 1)
            pool.tensor_copy(node[:], node_i[:]).then_inc(ready, 1)

        @block.scalar
        def _(act):
            far = act.value_load(T.far_i[0:1, 0:1], min_val=0, max_val=1)
            with act.If(far > 0):
                with act.Fori(0, NC) as c:
                    with act.Fori(0, NB) as b:
                        act.wait_ge(shifted, c * NB + b + 1)
                        act.activation(t[:], t[:], ACT.Exp).then_inc(ex_ready, 1)

        @block.vector
        def _(dve):
            dve.wait_ge(ready, 1)
            far = dve.value_load(T.far_i[0:1, 0:1], min_val=0, max_val=1)
            with dve.If(far > 0):
                dve.sem_inc(chunk_used, 1)
                dve.memset(top[:], -FAR)
                dve.memset(total[:], 0.0)
                with dve.Fori(0, NC) as c:
                    dve.wait_ge(chunk_in, c * 32 + 32)
                    dve.tensor_copy(src_f[:], src_in[:]).then_inc(chain, 1)
                    with dve.Fori(0, NB) as b:
                        n = c * (NB * 4 + 1) + b * 4 + 1
                        dve.wait_ge(chain, n)
                        dve.tensor_scalar(t[:], src_f[:], node[:, bass.ds(b, 1)], -FAR, ALU.not_equal, ALU.mult).then_inc(chain, 1)
                        dve.wait_ge(chain, n + 1)
                        dve.tensor_tensor(t[:], t[:], e[:], ALU.add).then_inc(chain, 1)
                        dve.wait_ge(chain, n + 2)
                        dve.tensor_reduce(part[:], t[:], AX.X, ALU.max).then_inc(chain, 1)
                        dve.wait_ge(chain, n + 3)
                        dve.tensor_tensor(top[:, bass.ds(b, 1)], top[:, bass.ds(b, 1)], part[:], ALU.max).then_inc(chain, 1)
                    dve.wait_ge(chain, (c + 1) * (NB * 4 + 1))
                    dve.sem_inc(chunk_used, 1)
                base = NC * (NB * 4 + 1)
                with dve.Fori(0, NC) as c:
                    dve.wait_ge(chunk_in, c * 32 + 32 + NC * 32)
                    dve.tensor_copy(src_f[:], src_in[:]).then_inc(chain, 1)
                    with dve.Fori(0, NB) as b:
                        n = c * (NB * 3 + 1) + b * 3 + 1 + base
                        dve.wait_ge(chain, n)
                        dve.tensor_scalar(t[:], e[:], top[:, bass.ds(b, 1)], 0.0, ALU.subtract, ALU.min).then_inc(shifted, 1)
                        dve.wait_ge(ex_ready, c * NB + b + 1)
                        dve.scalar_tensor_tensor(out=t[:], in0=src_f[:], scalar=node[:, bass.ds(b, 1)], in1=t[:],
                                                 op0=ALU.is_equal, op1=ALU.mult).then_inc(chain, 1)
                        dve.wait_ge(chain, n + 1)
                        dve.tensor_reduce(part[:], t[:], AX.X, ALU.add).then_inc(chain, 1)
                        dve.wait_ge(chain, n + 2)
                        dve.tensor_tensor(total[:, bass.ds(b, 1)], total[:, bass.ds(b, 1)], part[:], ALU.add).then_inc(chain, 1)
                    dve.wait_ge(chain, (c + 1) * (NB * 3 + 1) + base)
                    dve.sem_inc(chunk_used, 1)
                end = base + NC * (NB * 3 + 1)
                dve.tensor_scalar(total[:], total[:], 1e-37, None, ALU.max).then_inc(chain, 1)
                dve.tensor_copy(T.shift[:, :, 0], top[:])
                dve.wait_ge(chain, end + 1)
                dve.reciprocal(T.shift[:, :, 1], total[:])


def aggregate(nc, T):
    NC = T.src.shape[0] // CA
    HJ = JA // 2
    with ExitStack() as ctx:
        m = Memory(nc, ctx, "ag")
        sb, ps, sem = m.sb, m.ps, m.sem
        acc = sb("acc", [P, T.NB, D])
        src_i = sb("src_i", [R, 4, JA], I32)
        rows = sb("rows", [R, 4, JA, XW])
        e_s = sb("e_s", [R, 2, JA])
        ex = sb("ex", [R, 2, JA])
        att = sb("att", [R, 2, JA])
        rel = sb("rel", [R, JA])
        rows_i = sb("rows_i", [R, P], I32)
        iota = sb("iota", [R, P])
        first_i = sb("first_i", [R, T.NB], I32)
        first_row = sb("first_row", [R, T.NB])
        hot = [sb(f"hot{k}", [R, HJ, P]) for k in range(2)]
        part = ps("part", [P, 512])

        table_done = sem("table_done")
        iota_made, iota_ready = sem("iota_made"), sem("iota_ready")
        src_ready = sem("src_ready")
        rows_in = [sem(f"rows_in{b}") for b in range(4)]
        e_ready, ex_ready, att_ready, rel_ready = sem("e_ready"), sem("ex_ready"), sem("att_ready"), sem("rel_ready")
        hot_ready = [sem(f"hot_ready{k}") for k in range(2)]
        hot_used = [sem(f"hot_used{k}") for k in range(2)]
        cleared, added, chunk_done = sem("cleared"), sem("added"), sem("chunk_done")
        agg_out = sem("agg_out")

        block = ctx.enter_context(nc.Block())

        @block.sync
        def _(sp):
            with nc.allow_non_contiguous_dma(reason="two words for each node"):
                sp.dma_start(T.xn_table[:, D:XW].rearrange("(b p) w -> p b w", p=P), T.shift[:]).then_inc(table_done, 16)

            total = sp.value_load(T.plan_a[0:1, 2, NC:NC + 1], min_val=0, max_val=T.NB * NC) + NC
            sp.wait_ge(added, total + 2)
            sp.dma_start(T.agg.rearrange("(b p) d -> p b d", p=P), acc[:]).then_inc(agg_out, 16)
            sp.wait_ge(agg_out, 16)

        @block.gpsimd
        def _(pool):
            pool.iota(rows_i[:], [[1, P]], base=0, channel_multiplier=0)
            pool.iota(first_i[:], [[P, T.NB]], base=0, channel_multiplier=0).then_inc(iota_made, 1)
            pool.wait_ge(iota_made, 1)
            pool.tensor_copy(iota[:], rows_i[:])
            pool.tensor_copy(first_row[:], first_i[:]).then_inc(iota_ready, 1)
            pool.wait_ge(table_done, 16)

            def gather(c, b, i):
                pool.wait_ge(src_ready, c + 1)
                if from_(c, 4):
                    pool.wait_ge(chunk_done, c - 3)
                pool.sem_inc(T.passed, 1)
                for j in range(JA):
                    pool.indirect_dma_start(
                        out=rows[:, b, j, :], out_offset=None, in_=T.xn_table[0:T.x.shape[0], :],
                        in_offset=bass.IndirectOffsetOnAxis(ap=src_i[:, b, j:j + 1], axis=0),
                    ).then_inc(rows_in[b], 16)

            by_four(pool, gather, NC, 0)

        @block.vector
        def _(dve):
            dve.wait_ge(iota_ready, 1)
            dve.memset(part[:, 0:D], 0.0)
            for n in range(7):
                a, z = T.NB * n // 7, T.NB * (n + 1) // 7
                last = dve.memset(acc[:, a:z, :], 0.0)
            last.then_inc(cleared, 1)
            dve.wait_ge(cleared, 1)
            dve.sem_inc(hot_ready[0], 1)
            dve.sem_inc(hot_ready[1], 1)
            dve.sem_inc(added, 1)

            def one_hot(k, b, n):
                dve.wait_ge(hot_used[k], n + 1)
                for t in range(HJ):
                    j = k * HJ + t
                    last = dve.tensor_scalar(hot[k][:, t], iota[:], rel[:, j:j + 1], att[:, b % 2, j:j + 1],
                                             ALU.is_equal, ALU.mult)
                last.then_inc(hot_ready[k], 1)

            def pair(c, b, n, blk, prev):
                dve.wait_ge(hot_ready[1], n + 1)
                dve.tensor_scalar(rel[:], T.dst_t[:, bass.ds(c * JA, JA)], first_row[:, bass.ds(blk, 1)], None, ALU.subtract).then_inc(rel_ready, 1)
                dve.wait_ge(rel_ready, n + 1)
                one_hot(0, b, n)
                dve.wait_ge(hot_used[1], n + 1)
                dve.wait_ge(added, n + 1)
                row = acc[:, bass.ds(prev, 1), :].rearrange("p a d -> p (a d)")
                dve.tensor_tensor(row, row, part[:, 0:D], ALU.add).then_inc(added, 1)
                one_hot(1, b, n)

            def chunk(c, b, i, regs, ahead):
                prev, first, last, pairs = regs
                dve.wait_ge(rows_in[b], i * (16 * JA) + 16 * JA)
                if from_(c, 2):
                    dve.wait_ge(ex_ready, c - 1)
                dve.tensor_tensor(e_s[:, b % 2], T.e[:, bass.ds(c * JA, JA)], rows[:, b, :, D], ALU.subtract).then_inc(e_ready, 1)
                dve.wait_ge(ex_ready, c + 1)
                dve.tensor_tensor(att[:, b % 2], ex[:, b % 2], rows[:, b, :, D + 1], ALU.mult).then_inc(att_ready, 1)
                dve.wait_ge(att_ready, c + 1)
                pair(c, b, pairs, first, prev)
                with dve.If(first < last):
                    with dve.Fori(1, last - first + 1) as d:
                        blk = nc.s_assert_within(first + d, 1, T.NB - 1, skip_runtime_bounds_check_because="it is at most last")
                        pair(c, b, pairs + d, blk, blk - 1)
                ahead()

            by_four_ahead(dve, lambda c: planned(dve, T, c), chunk, NC, 0)
            final = dve.value_load(T.plan_a[0:1, 0, NC:NC + 1], min_val=0, max_val=T.NB - 1)
            total = dve.value_load(T.plan_a[0:1, 2, NC:NC + 1], min_val=0, max_val=T.NB * NC) + NC
            dve.wait_ge(hot_used[1], total + 1)
            dve.wait_ge(added, total + 1)
            row = acc[:, bass.ds(final, 1), :].rearrange("p a d -> p (a d)")
            dve.tensor_tensor(row, row, part[:, 0:D], ALU.add).then_inc(added, 1)

        @block.scalar
        def _(act):
            def indices(c, b):
                act.copy(src_i[:, b], T.src_t[:, bass.ds(c * JA, JA)]).then_inc(src_ready, 1)

            def body(c, b, i):
                act.wait_ge(e_ready, c + 1)
                if from_(c, 2):
                    act.wait_ge(att_ready, c - 1)
                act.activation(ex[:, b % 2], e_s[:, b % 2], ACT.Exp).then_inc(ex_ready, 1)
                if not isinstance(c, int) or c + 4 < NC:
                    indices(c + 4, b)

            for c in range(4):
                indices(c, c)
            by_four(act, body, NC, 1)

        @block.tensor
        def _(pe):
            pe.wait_ge(cleared, 1)
            for k in range(2):
                pe.sem_inc(hot_used[k], 1)

            def pair(b, n):
                pe.wait_ge(added, n + 2)
                for k in range(2):
                    pe.wait_ge(hot_ready[k], n + 2)
                    for t in range(HJ):
                        j = k * HJ + t
                        mm = pe.matmul(part[:, 0:D], hot[k][:, t], rows[:, b, j, 0:D], start=j == 0, stop=j == JA - 1)
                    mm.then_inc(hot_used[k], 1)

            def chunk(c, b, i, regs, ahead):
                done, first, last, pairs = regs
                pair(b, pairs)
                with pe.If(first < last):
                    with pe.Fori(1, last - first + 1) as d:
                        pair(b, pairs + d)
                ahead()
                pe.wait_ge(hot_used[1], done + 1)
                pe.sem_inc(chunk_done, 1)

            def load(c):
                done = pe.value_load(T.plan_a[0:1, 2, bass.ds(c + 1, 1)], min_val=0, max_val=T.NB * NC) + (c + 1)
                return (done,) + planned(pe, T, c, False)[1:]

            by_four_ahead(pe, load, chunk, NC, 0)


def mix(nc, T):
    NG = T.x.shape[0] // G
    E = T.W1.shape[0]
    NACT = 3 * 16
    with ExitStack() as ctx:
        m = Memory(nc, ctx, "mx")
        sb, ps, sem = m.sb, m.ps, m.sem
        w_o = sb("w_o", [P, K, D])
        w_r = sb("w_r", [P, K, E])
        b_r = sb("b_r", [P, E])
        gamma = sb("gamma", [P, K])
        beta = sb("beta", [P, K])
        b_out = sb("b_out", [1, 2, D])
        bias = sb("bias", [1, D])
        one_row = sb("one_row", [1, R])
        eight_i = sb("eight_i", [R, S, E], I32)
        eight = sb("eight", [R, S, E])
        start_i = sb("start_i", [R, S, E], I32)
        start = sb("start", [R, S, E])
        half = sb("half", [R, S])
        ones = sb("ones", [R, R])
        below = sb("below", [R, R])
        x = sb("x", [R, 2, S, D])
        agg = sb("agg", [R, 2, S, D])
        qT = sb("qT", [P, 2, K, G])
        aggT = sb("aggT", [P, K, G])
        head_of = sb("head_of", [HEADS, K, P])
        den = sb("den", [R, S, HEADS])
        rec = sb("rec", [R, S, HEADS])
        recT = sb("recT", [HEADS, G])
        scale = sb("scale", [P, K, G])
        oT = sb("oT", [P, K, G])
        x1 = sb("x1", [R, 2, S, D])
        stats = sb("stats", [R, 2, S, 6])
        mv = sb("mv", [R, 2, S, 2])
        var = sb("var", [R, 2, S])
        rstd = sb("rstd", [R, 2, S])
        xn1 = sb("xn1", [R, S, D])
        xn = sb("xn", [R, 4, S, D])
        xhT = sb("xhT", [P, K, G])
        raw = sb("raw", [R, 2, S * E])
        logit = sb("logit", [R, S, E])
        top = sb("top", [R, S, 8])
        top_i = sb("top_i", [R, S, 8], U32)
        top_f = sb("top_f", [R, S, 8])
        gap = sb("gap", [R, S])
        odds = sb("odds", [R, S])
        both = sb("both", [R, S])
        pick = sb("pick", [R, 2, S, E])
        mask = sb("mask", [R, S, E])
        seen = sb("seen", [R, E])
        new = sb("new", [R, E])
        place = sb("place", [R, S, E])
        picked = sb("picked", [R, 2, S, E])
        slot = sb("slot", [R, 2, S])
        slot_i = sb("slot_i", [R, 4, 2, S], I32)
        slots = sb("slots", [R, 2, NG * S])
        slot_all = sb("slot_all", [R, 2, NG * S])
        moved = sb("moved", [R, 2, NG * S])
        delta = sb("delta", [R, E])
        count = sb("count", [R, E])
        steps_f = sb("steps_f", [R, E])
        count_i = sb("count_i", [R, E], I32)
        steps_i = sb("steps_i", [R, E], I32)
        one8 = sb("one8", [R, E])
        before = sb("before", [R, E])

        bank = [ps(f"bank{n}", [P, 512]) for n in range(8)]
        weights_in, consts_made, consts_ready, bias_ready = (sem("weights_in"), sem("consts_made"), sem("consts_ready"),
                                                             sem("bias_ready"))
        acts_in = [sem(f"acts_in{b}") for b in range(2)]
        x1_stored = [sem(f"x1_stored{b}") for b in range(2)]
        rows_sent = [sem(f"rows_sent{b}") for b in range(4)]
        agg_turned, aggT_ready = sem("agg_turned"), sem("aggT_ready")
        den_mm, num_mm, den_ready, rec_ready = sem("den_mm"), sem("num_mm"), sem("den_ready"), sem("rec_ready")
        rec_turned, recT_ready, scale_mm, scale_ready, oT_ready = (sem("rec_turned"), sem("recT_ready"), sem("scale_mm"),
                                                                   sem("scale_ready"), sem("oT_ready"))
        band_ready, heads_ready = sem("band_ready"), sem("heads_ready")
        x1_mm, x1_ready = sem("x1_mm"), sem("x1_ready")
        stats_ready, mv_ready, var_ready, rstd_ready = sem("stats_ready"), sem("mv_ready"), sem("var_ready"), sem("rstd_ready")
        xn1_ready, xn_ready = sem("xn1_ready"), sem("xn_ready")
        xn_turned, xhT_ready, logit_mm, raw_ready = sem("xn_turned"), sem("xhT_ready"), sem("logit_mm"), sem("raw_ready")
        logit_ready, top_ready, found, gap_ready = sem("logit_ready"), sem("top_ready"), sem("found"), sem("gap_ready")
        topf_ready, pick_ready, mask_ready, rank_mm = sem("topf_ready"), sem("pick_ready"), sem("mask_ready"), sem("rank_mm")
        odds_ready, both_ready, gate_ready = sem("odds_ready"), sem("both_ready"), sem("gate_ready")
        new_ready, seen_ready, place_ready = sem("new_ready"), sem("seen_ready"), sem("place_ready")
        picked_ready, slot_ready, sloti_ready = sem("picked_ready"), sem("slot_ready"), sem("sloti_ready")
        final, rows_gone = sem("final"), sem("rows_gone")

        block = ctx.enter_context(nc.Block())
        x_rows = T.x.rearrange("(g s p) d -> g p s d", s=S, p=R)
        x1_rows = T.x1_table.rearrange("(g s p) d -> g p s d", s=S, p=R)
        agg_rows = T.agg[0:NG * G, :].rearrange("(g s p) d -> g p s d", s=S, p=R)
        q_cols = T.q_table.rearrange("k p (g n) -> g p k n", n=G)

        def pipeline(eng, step, last):
            for g in range(4):
                step(g, g, 0)
            with eng.Fori(1, (NG - 1) // 4) as i:
                for b in range(4):
                    step(i * 4 + b, b, i)
            for g in range(NG - 1, last + 1):
                step(g, g % 4, g // 4)

        def has(g, lag):
            return not isinstance(g, int) or 0 <= g - lag < NG

        def after(eng, semaphore, value):
            if not isinstance(value, int) or value > 0:
                eng.wait_ge(semaphore, value)

        @block.sync
        def _(sp):
            sp.dma_start(w_o[:], T.wo.rearrange("(c p) o -> p c o", p=P)).then_inc(weights_in, 16)
            sp.dma_start(b_r[:], T.br.partition_broadcast(P)).then_inc(weights_in, 16)
            for k in range(K):
                for dst, vec in ((gamma, T.gamma), (beta, T.beta)):
                    sp.dma_start(dst[:, k:k + 1], vec[k * P:(k + 1) * P].rearrange("(p a) -> p a", a=1)).then_inc(weights_in, 16)
                sp.dma_start(w_r[:, k, :], T.Wr[k * P:(k + 1) * P, :]).then_inc(weights_in, 16)
            sp.dma_start(b_out[:, 0], T.b_fc.rearrange("(a d) -> a d", a=1)).then_inc(weights_in, 16)
            sp.dma_start(b_out[:, 1], T.bo.rearrange("(a d) -> a d", a=1)).then_inc(weights_in, 16)

            def step(g, b, u):
                c = b % 2
                if has(g, 0):
                    after(sp, x1_ready, g - 1)
                    sp.dma_start(x[:, c], x_rows[g]).then_inc(acts_in[c], 16)
                    sp.dma_start(agg[:, c], agg_rows[g]).then_inc(acts_in[c], 16)
                    sp.dma_start(qT[:, c], q_cols[g]).then_inc(acts_in[c], 16)
                if has(g, 1):
                    sp.wait_ge(x1_ready, g)
                    sp.dma_start(x1_rows[g - 1], x1[:, 1 - c]).then_inc(x1_stored[1 - c], 16)

            pipeline(sp, step, NG)
            for c in range(2):
                sp.wait_ge(x1_stored[c], 16 * ((NG + 1 - c) // 2))

        @block.gpsimd
        def _(pool):
            pool.iota(eight_i[:], [[0, S], [1, E]], base=0, channel_multiplier=0)
            pool.iota(start_i[:], [[0, S], [CAP, E]], base=0, channel_multiplier=0)
            pool.memset(half[:], -0.5)
            pool.memset(one_row[:], 1.0)
            pool.memset(seen[:], 0.0)
            pool.memset(ones[:], 1.0).then_inc(consts_made, 1)
            pool.wait_ge(consts_made, 1)
            pool.tensor_copy(eight[:], eight_i[:])
            pool.tensor_copy(start[:], start_i[:])
            pool.memset(head_of[:], 1.0).then_inc(band_ready, 1)
            pool.wait_ge(band_ready, 1)
            pool.affine_select(out=head_of[:], in_=head_of[:], compare_op=ALU.is_gt, fill=0.0, base=1,
                               pattern=[[P, K], [1, P]], channel_multiplier=-HD).then_inc(band_ready, 1)
            pool.wait_ge(band_ready, 2)
            pool.affine_select(out=head_of[:], in_=head_of[:], compare_op=ALU.is_gt, fill=0.0, base=HD,
                               pattern=[[-P, K], [-1, P]], channel_multiplier=HD).then_inc(heads_ready, 1)
            pool.affine_select(out=below[:], in_=ones[:], compare_op=ALU.is_gt, fill=0.0, base=0,
                               pattern=[[1, R]], channel_multiplier=-1).then_inc(consts_ready, 1)

            def inverse_root(g, n):
                pool.wait_ge(mv_ready, g * 2 + n + 1)
                pool.sem_inc(T.passed, 1)
                pool.tensor_scalar(var[:, n], mv[:, n, :, 1], EPS, None, ALU.add).then_inc(var_ready, 1)
                pool.wait_ge(var_ready, g * 2 + n + 1)
                pool.tensor_tensor(rstd[:, n], var[:, n], half[:], ALU.pow).then_inc(rstd_ready, 1)

            def send(g, b, c):
                pool.wait_ge(sloti_ready, g + 1)
                pool.sem_inc(T.passed, 1)
                for s in range(S):
                    pool.indirect_dma_start(
                        out=T.lists, out_offset=bass.IndirectOffsetOnAxis(ap=slot_i[:, b, c, s:s + 1], axis=0),
                        in_=xn[:, b, s, :], in_offset=None,
                    ).then_inc(rows_sent[b], 16)

            def step(g, b, u):
                for n in range(2):
                    if has(g, 1):
                        inverse_root(g - 1, n)
                    if has(g, 3):
                        send(g - 3, (b + 1) % 4, n)
                if has(g, 4):
                    pool.wait_ge(rows_sent[b], u * (16 * 2 * S))
                    pool.sem_inc(rows_gone, 1)

            pool.sem_inc(rows_gone, 1)
            pipeline(pool, step, NG + 2)
            for b in range(4):
                pool.wait_ge(rows_sent[b], 16 * 2 * S * ((NG + 3 - b) // 4))

        @block.tensor
        def _(pe):
            pe.wait_ge(weights_in, 16 * (4 + 3 * K))
            pe.wait_ge(consts_ready, 1)
            pe.wait_ge(bias_ready, 1)
            pe.wait_ge(heads_ready, 1)

            def residual(g, b, u):
                c = b % 2
                pe.wait_ge(acts_in[c], (g - c) * (NACT // 2) + NACT)
                after(pe, xhT_ready, (g - 1) * K)
                for k in range(K):
                    for s in range(S):
                        mm = pe.transpose(bank[k][:, s * R:(s + 1) * R], agg[:, c, s, k * P:(k + 1) * P], T.ident[0:R, 0:R])
                    mm.then_inc(agg_turned, 1)
                after(pe, raw_ready, g - 1)
                after(pe, place_ready, g - 2)
                after(pe, oT_ready, g * K)
                after(pe, scale_ready, g * K)
                for s in range(S):
                    for k in range(K):
                        at = (s * K + k) * (HEADS // K)
                        mm = pe.matmul(bank[4][0:R, at:at + HEADS // K], qT[:, c, k, s * R:(s + 1) * R], T.ksum[:, k, 0:P:HD],
                                       start=True, stop=True)
                mm.then_inc(den_mm, 1)
                for k in range(K):
                    pe.matmul(bank[2 + k][:, 0:G], T.kv[:, k], qT[:, c, k], start=True, stop=True).then_inc(num_mm, 1)
                pe.wait_ge(rec_ready, g + 1)
                for s in range(S):
                    mm = pe.transpose(bank[5][0:HEADS, s * R:(s + 1) * R], rec[:, s, :], T.ident[0:R, 0:R])
                mm.then_inc(rec_turned, 1)
                pe.wait_ge(aggT_ready, g * K + K)
                after(pe, x1_ready, g)
                for s in range(S):
                    out = bank[6 + s // 2][0:R, (s % 2) * D:(s % 2 + 1) * D]
                    pe.matmul(out, one_row[:], bias[:], start=True, stop=False)
                    for k in range(K):
                        pe.matmul(out, aggT[:, k, s * R:(s + 1) * R], T.w_fcT[:, k], start=False, stop=False)
                    if s == 0:
                        pe.wait_ge(recT_ready, g + 1)
                        for k in range(K):
                            pe.matmul(bank[4 + k][:, 0:G], head_of[:, k, :], recT[:], start=True, stop=True).then_inc(scale_mm, 1)
                        pe.wait_ge(oT_ready, g * K + K)
                    for k in range(K):
                        mm = pe.matmul(out, oT[:, k, s * R:(s + 1) * R], w_o[:, k], start=False, stop=k == K - 1)
                    if s % 2:
                        mm.then_inc(x1_mm, 1)

            def ranks(g):
                pe.wait_ge(mask_ready, g + 1)
                after(pe, seen_ready, g)
                out = bank[3][0:R, 0:S * E].rearrange("p (s e) -> p s e", e=E)
                pe.matmul(out, below[:], mask[:], start=True, stop=False)
                for n in range(1, S):
                    pe.matmul(out[:, n:S], ones[:], mask[:, 0:S - n], start=False, stop=False)
                pe.matmul(out, ones[:], seen[:].unsqueeze(1).broadcast_to([R, S, E]), start=False, stop=True).then_inc(rank_mm, 1)

            def logits(g, b, there):
                pe.wait_ge(xn_ready, g + 1)
                if there:
                    pe.wait_ge(aggT_ready, (g + 1) * K + K)
                for k in range(K):
                    for s in range(S):
                        mm = pe.transpose(bank[k][:, s * R:(s + 1) * R], xn[:, b, s, k * P:(k + 1) * P], T.ident[0:R, 0:R])
                    mm.then_inc(xn_turned, 1)
                pe.wait_ge(xhT_ready, g * K + K)
                for s in range(S):
                    for k in range(K):
                        mm = pe.matmul(bank[2][0:R, s * E:(s + 1) * E], xhT[:, k, s * R:(s + 1) * R], w_r[:, k],
                                       start=k == 0, stop=k == K - 1)
                mm.then_inc(logit_mm, 1)

            def step(g, b, u):
                if has(g, 0):
                    residual(g, b, u)
                if has(g, 2):
                    ranks(g - 2)
                if has(g, 1):
                    logits(g - 1, (b + 3) % 4, has(g, 0))

            pipeline(pe, step, NG + 1)
            pe.wait_ge(seen_ready, NG)
            pe.wait_ge(place_ready, NG)
            pe.matmul(bank[3][0:R, 0:E], ones[:], seen[:], start=True, stop=True).then_inc(rank_mm, 1)

        @block.scalar
        def _(act):
            act.wait_ge(weights_in, 16 * (4 + 3 * K))

            def step(g, b, u):
                c = b % 2
                if has(g, 0):
                    after(act, x1_mm, g * 2)
                    for k in range(K):
                        act.wait_ge(agg_turned, g * K + k + 1)
                        act.copy(aggT[:, k], bank[k][:, 0:G]).then_inc(aggT_ready, 1)
                    after(act, scale_mm, g * K)
                    act.wait_ge(rec_turned, g + 1)
                    act.copy(recT[:], bank[5][0:HEADS, 0:G]).then_inc(recT_ready, 1)
                    after(act, oT_ready, g * K)
                    for k in range(K):
                        act.wait_ge(scale_mm, g * K + k + 1)
                        act.copy(scale[:, k], bank[4 + k][:, 0:G]).then_inc(scale_ready, 1)
                if has(g, 2):
                    act.wait_ge(gap_ready, g - 1)
                    after(act, gate_ready, (g - 2) * 2)
                    act.activation(odds[:], gap[:], ACT.Exp).then_inc(odds_ready, 1)
                if has(g, 1):
                    after(act, logit_mm, g - 1)
                    for k in range(K):
                        act.wait_ge(xn_turned, (g - 1) * K + k + 1)
                        act.activation(xhT[:, k], bank[k][:, 0:G], ACT.Identity, bias=beta[:, k:k + 1],
                                       scale=gamma[:, k:k + 1]).then_inc(xhT_ready, 1)
                    act.wait_ge(logit_mm, g)
                    after(act, logit_ready, g - 2)
                    act.copy(raw[:, 1 - c], bank[2][0:R, 0:S * E]).then_inc(raw_ready, 1)

            pipeline(act, step, NG + 1)

        @block.vector
        def _(dve):
            dve.wait_ge(weights_in, 16 * (4 + 3 * K))
            dve.wait_ge(consts_ready, 1)
            dve.tensor_tensor(bias[:], b_out[:, 0], b_out[:, 1], ALU.add).then_inc(bias_ready, 1)

            def moments(g, n, rows):
                for s in range(S):
                    last = dve.bn_stats(stats[:, n, s], rows[:, s])
                last.then_inc(stats_ready, 1)
                dve.wait_ge(stats_ready, g * 2 + n + 1)
                dve.sem_inc(T.passed, 1)
                for s in range(S):
                    last = dve.bn_aggr(mv[:, n, s], stats[:, n, s])
                last.then_inc(mv_ready, 1)

            def normalize(g, n, out, rows, ready):
                dve.wait_ge(rstd_ready, g * 2 + n + 1)
                for s in range(S):
                    last = dve.tensor_scalar(out[:, s], rows[:, s], mv[:, n, s, 0:1], rstd[:, n, s:s + 1], ALU.subtract, ALU.mult)
                last.then_inc(ready, 1)

            def reciprocals(g):
                dve.wait_ge(den_mm, g + 1)
                dve.tensor_scalar(den[:], bank[4][0:R, 0:S * HEADS].rearrange("p (s h) -> p s h", h=HEADS), 1e-6, None,
                                  ALU.add).then_inc(den_ready, 1)
                dve.wait_ge(den_ready, g + 1)
                after(dve, rec_turned, g)
                dve.reciprocal(rec[:], den[:]).then_inc(rec_ready, 1)

            def attention(g):
                for k in range(K):
                    dve.wait_ge(scale_ready, g * K + k + 1)
                    dve.wait_ge(num_mm, g * K + k + 1)
                    dve.tensor_tensor(oT[:, k], bank[2 + k][:, 0:G], scale[:, k], ALU.mult).then_inc(oT_ready, 1)

            def pick_experts(g, c):
                dve.wait_ge(raw_ready, g + 1)
                dve.tensor_tensor(logit[:], raw[:, c].rearrange("p (s e) -> p s e", e=E),
                                  b_r[0:R].unsqueeze(1).broadcast_to([R, S, E]), ALU.add).then_inc(logit_ready, 1)
                dve.wait_ge(logit_ready, g + 1)
                dve.sem_inc(T.passed, 1)
                for s in range(S):
                    last = dve.max(top[:, s], logit[:, s])
                last.then_inc(top_ready, 1)
                dve.wait_ge(top_ready, g + 1)
                dve.sem_inc(T.passed, 1)
                for s in range(S):
                    last = dve.max_index(top_i[:, s], top[:, s], logit[:, s])
                last.then_inc(found, 1)
                dve.tensor_tensor(gap[:], top[:, :, 1], top[:, :, 0], ALU.subtract).then_inc(gap_ready, 1)
                dve.wait_ge(found, g + 1)
                dve.tensor_copy(top_f[:, :, 0:2], top_i[:, :, 0:2]).then_inc(topf_ready, 1)
                dve.wait_ge(topf_ready, g + 1)
                for n in range(2):
                    last = dve.tensor_tensor(pick[:, n], eight[:], top_f[:, :, n:n + 1].broadcast_to([R, S, E]), ALU.is_equal)
                last.then_inc(pick_ready, 1)
                dve.wait_ge(pick_ready, g + 1)
                dve.tensor_tensor(mask[:], pick[:, 0], pick[:, 1], ALU.add).then_inc(mask_ready, 1)

            def places(g, b):
                dve.wait_ge(odds_ready, g + 1)
                dve.tensor_scalar(both[:], odds[:], 1.0, None, ALU.add).then_inc(both_ready, 1)
                dve.wait_ge(mask_ready, g + 1)
                dve.tensor_reduce(new[:], mask[:].rearrange("p s e -> p e s"), AX.X, ALU.add).then_inc(new_ready, 1)
                dve.wait_ge(both_ready, g + 1)
                dve.reciprocal(T.gate[:, 0, bass.ds(g * S, S)], both[:]).then_inc(gate_ready, 1)
                dve.wait_ge(rank_mm, g + 1)
                dve.tensor_tensor(place[:], bank[3][0:R, 0:S * E].rearrange("p (s e) -> p s e", e=E), start[:], ALU.add).then_inc(place_ready, 1)
                dve.wait_ge(gate_ready, g * 2 + 1)
                dve.tensor_tensor(T.gate[:, 1, bass.ds(g * S, S)], T.gate[:, 0, bass.ds(g * S, S)], odds[:], ALU.mult).then_inc(gate_ready, 1)
                dve.wait_ge(place_ready, g + 1)
                for n in range(2):
                    last = dve.tensor_tensor(picked[:, n], pick[:, n], place[:], ALU.mult)
                last.then_inc(picked_ready, 1)
                dve.wait_ge(new_ready, g + 1)
                dve.tensor_tensor(seen[:], seen[:], new[:], ALU.add).then_inc(seen_ready, 1)
                dve.wait_ge(picked_ready, g + 1)
                dve.tensor_reduce(slot[:], picked[:], AX.X, ALU.add).then_inc(slot_ready, 1)
                dve.wait_ge(slot_ready, g + 1)
                dve.tensor_copy(slots[:, :, bass.ds(g * S, S)], slot[:])
                dve.tensor_copy(slot_i[:, b], slot[:]).then_inc(sloti_ready, 1)

            def step(g, b, u):
                c = b % 2
                if has(g, 1):
                    after(dve, x1_ready, g)
                    moments(g - 1, 0, x1[:, 1 - c])
                if has(g, 0):
                    reciprocals(g)
                if has(g, 1):
                    after(dve, mv_ready, (g - 1) * 2)
                    normalize(g - 1, 0, xn1, x1[:, 1 - c], xn1_ready)
                    dve.wait_ge(xn1_ready, g)
                    moments(g - 1, 1, xn1)
                if has(g, 0):
                    after(dve, x1_mm, g * 2)
                    attention(g)
                if has(g, 2):
                    pick_experts(g - 2, c)
                if has(g, 1):
                    b1 = (b + 3) % 4
                    after(dve, rows_gone, g - 3)
                    normalize(g - 1, 1, xn[:, b1], xn1, xn_ready)
                if has(g, 0):
                    after(dve, x1_stored[c], (g - c) * 8)
                    for s in range(S):
                        if s % 2 == 0:
                            dve.wait_ge(x1_mm, g * 2 + s // 2 + 1)
                        last = dve.tensor_tensor(x1[:, c, s], x[:, c, s], bank[6 + s // 2][0:R, (s % 2) * D:(s % 2 + 1) * D], ALU.add)
                    last.then_inc(x1_ready, 1)
                if has(g, 2):
                    places(g - 2, (b + 2) % 4)

            pipeline(dve, step, NG + 1)
            dve.wait_ge(rank_mm, NG + 1)
            done = 0
            for make in (
                lambda: dve.tensor_copy(count[:], bank[3][0:R, 0:E]),
                lambda: dve.tensor_copy(T.moe[:, 0, 0:E], count[0:1]),
                lambda: dve.tensor_scalar(steps_f[:], count[:], BLK - 1.0, None, ALU.add),
                lambda: dve.tensor_copy(count_i[:], steps_f[:]),
                lambda: dve.tensor_scalar(steps_i[:], count_i[:], BLK.bit_length() - 1, None, ALU.arith_shift_right),
                lambda: dve.tensor_copy(T.moe[:, 1, 0:E], steps_i[0:1]),
                lambda: dve.tensor_copy(steps_f[:], steps_i[:]),
                lambda: dve.memset(one8[:], 1.0),
                lambda: dve.memset(T.moe[:, 2, 0:1], 0),
                lambda: dve.tensor_tensor_scan(before[:], one8[:], steps_f[:], 0.0, ALU.mult, ALU.add),
                lambda: dve.tensor_copy(T.moe[:, 2, 1:E + 1], before[0:1]),
                lambda: dve.tensor_scalar(delta[:], steps_f[:], float(BLK), -float(CAP), ALU.mult, ALU.add),
                lambda: dve.tensor_copy(slot_all[:], slots[:]),
            ):
                done += 1
                make().then_inc(final, 1)
                dve.wait_ge(final, done)
            for e in range(1, E):
                for make in (
                    lambda: dve.tensor_scalar(moved[:], slots[:], e * CAP - 0.5, delta[:, e - 1:e], ALU.is_gt, ALU.mult),
                    lambda: dve.tensor_tensor(slot_all[:], slot_all[:], moved[:], ALU.add),
                ):
                    done += 1
                    make().then_inc(final, 1)
                    dve.wait_ge(final, done)
            dve.tensor_copy(T.slot[:], slot_all[:])


def experts(nc, T):
    E, _, H = T.W1.shape
    M = H // P
    A = BLK // P
    MAX = CAP // BLK
    with ExitStack() as ctx:
        m = Memory(nc, ctx, "ex")
        sb, ps, sem = m.sb, m.ps, m.sem
        w1 = sb("w1", [P, 2, K, H])
        w2 = sb("w2", [P, 2, M, D])
        b2 = sb("b2", [P, 2, D])
        b1_rows = sb("b1_rows", [E * M, P])
        b1 = sb("b1", [P, E * M])
        gamma = sb("gamma", [P, K])
        beta = sb("beta", [P, K])
        zeros = sb("zeros", [P, A, D])
        x = sb("x", [P, A, D])
        xT = sb("xT", [P, K, BLK])
        hid = sb("hid", [P, M, BLK])
        y = sb("y", [P, A, D])
        tp = [ps(f"tp{k}", [P, 512]) for k in range(K)]
        hp = [ps(f"hp{k}", [P, 512]) for k in range(M)]
        yp = [ps(f"yp{k}", [P, 512]) for k in range(2)]

        zeroed, tails_in, consts_in, b1_turned, b1_ready = (sem("zeroed"), sem("tails_in"), sem("consts_in"),
                                                            sem("b1_turned"), sem("b1_ready"))
        weights_in = [sem(f"weights_in{b}") for b in range(2)]
        x_in, x_turned, xT_ready = sem("x_in"), sem("x_turned"), sem("xT_ready")
        hid_mm, hid_ready, y_mm, y_ready, y_out = sem("hid_mm"), sem("hid_ready"), sem("y_mm"), sem("y_ready"), sem("y_out")
        y_free, spare_out = sem("y_free"), sem("spare_out")

        block = ctx.enter_context(nc.Block())

        def planned(eng, e):
            n = eng.value_load(T.moe[0:1, 1, bass.ds(e, 1)], min_val=0, max_val=MAX)
            base = eng.value_load(T.moe[0:1, 2, bass.ds(e, 1)], min_val=0, max_val=2 * MAX)
            return n, base

        def blocks(eng, body, before=None):
            with eng.Fori(0, E // 2) as i:
                for b in range(2):
                    e = i * 2 + b
                    n, base = planned(eng, e)
                    if before is not None:
                        before(e, b, i)
                    with eng.If(n > 0):
                        with eng.Fori(0, n) as k:
                            body(e, b, base + k, k)

        @block.sync
        def _(sp):
            sp.dma_start(b1_rows[:], T.b1.rearrange("e (m p) -> (e m) p", p=P)).then_inc(consts_in, 16)
            for k in range(K):
                for dst, vec in ((gamma, T.gamma), (beta, T.beta)):
                    sp.dma_start(dst[:, k:k + 1], vec[k * P:(k + 1) * P].rearrange("(p a) -> p a", a=1)).then_inc(consts_in, 16)
            sp.wait_ge(zeroed, 1)
            with sp.Fori(0, E) as e:
                n = sp.value_load(T.moe[0:1, 0, bass.ds(e, 1)], min_val=0, max_val=CAP - BLK)
                sp.dma_start(T.lists[bass.ds(e * CAP + n, BLK), :].rearrange("(p a) d -> p a d", p=P), zeros[:]).then_inc(tails_in, 16)
            sp.wait_ge(tails_in, 16 * E)
            for t in range(FULL, BLOCKS):
                sp.dma_start(T.results[t * BLK:(t + 1) * BLK, :].rearrange("(p a) d -> p a d", p=P), zeros[:]).then_inc(spare_out, 16)

            def load(row):
                sp.dma_start(x[:], T.lists[bass.ds(row, BLK), :].rearrange("(a p) d -> p a d", p=P)).then_inc(x_in, 16)

            def body(e, b, t, k):
                sp.wait_ge(x_turned, t * K + 1)
                load(e * CAP + k * BLK)

            blocks(sp, body)
            total = sp.value_load(T.moe[0:1, 2, E:E + 1], min_val=0, max_val=BLOCKS)
            sp.wait_ge(x_turned, total * K + 1)
            load(0)

        @block.gpsimd
        def _(pool):
            pool.memset(zeros[:], 0.0).then_inc(zeroed, 1)
            pool.sem_inc(y_free, 1)
            pool.wait_ge(spare_out, 16 * (BLOCKS - FULL))

            def body(e, b, t, k):
                pool.wait_ge(y_ready, t * 2 + 4)
                pool.sem_inc(T.passed, 1)
                row = nc.s_assert_within(t * BLK, 0, (BLOCKS - 1) * BLK, skip_runtime_bounds_check_because="the lists have at most BLOCKS blocks")
                pool.dma_start(T.results[bass.ds(row, BLK), :].rearrange("(a p) d -> p a d", p=P), y[:]).then_inc(y_out, 16)
                pool.wait_ge(y_out, t * 16 + 16)
                pool.sem_inc(y_free, 1)

            blocks(pool, body)

        @block.tensor
        def _(pe):
            pe.sem_inc(x_turned, 1)
            pe.sem_inc(y_mm, 1)
            pe.wait_ge(consts_in, 16 * (1 + 2 * K))
            pe.transpose(yp[0][:, 0:E * M], b1_rows[:], T.ident[0:E * M, 0:E * M]).then_inc(b1_turned, 1)

            def turn():
                for k in range(K):
                    for a in range(A):
                        mm = pe.transpose(tp[k][:, a * P:(a + 1) * P], x[:, a, k * P:(k + 1) * P], T.ident[:])
                    mm.then_inc(x_turned, 1)

            pe.wait_ge(x_in, 16)
            turn()
            pe.wait_ge(b1_ready, 1)

            def before(e, b, i):
                pe.wait_ge(weights_in[b], i * 48 + 48)

            def body(e, b, t, k_):
                pe.wait_ge(xT_ready, t * K + K)
                for n in range(M):
                    for k in range(K):
                        mm = pe.matmul(hp[n][:, 0:BLK], w1[:, b, k, n * P:(n + 1) * P], xT[:, k], start=k == 0, stop=k == K - 1)
                    mm.then_inc(hid_mm, 1)
                pe.wait_ge(x_in, t * 16 + 32)
                turn()
                pe.wait_ge(hid_ready, t * M + M)
                for a in range(A):
                    if a % 2 == 0:
                        pe.wait_ge(y_ready, t * 2 + a // 2 + 1)
                    for n in range(M):
                        mm = pe.matmul(yp[a // 2][:, (a % 2) * D:(a % 2 + 1) * D], hid[:, n, a * P:(a + 1) * P], w2[:, b, n],
                                       start=n == 0, stop=n == M - 1)
                    if a % 2:
                        mm.then_inc(y_mm, 1)

            blocks(pe, body, before)

        @block.scalar
        def _(act):
            def weights(e, b):
                one = bass.ds(e, 1)
                act.dma_start(w1[:, b], T.W1[one].rearrange("a (c p) h -> p (a c) h", p=P)).then_inc(weights_in[b], 16)
                act.dma_start(w2[:, b], T.W2[one].rearrange("a (c p) d -> p (a c) d", p=P)).then_inc(weights_in[b], 16)
                act.dma_start(b2[:, b], T.b2[one].rearrange("a d -> (a d)").partition_broadcast(P)).then_inc(weights_in[b], 16)

            weights(0, 0)
            act.wait_ge(b1_ready, 1)
            with act.Fori(0, E // 2) as i:
                for b in range(2):
                    e = i * 2 + b
                    n, base = planned(act, e)
                    act.wait_ge(y_mm, base * 2 + 1)
                    act.wait_ge(y_ready, base * 2 + 2)
                    act.sem_inc(T.passed, 1)
                    if b == 0:
                        weights(e + 1, 1)
                    else:
                        with act.If(i < E // 2 - 1):
                            weights(nc.s_assert_within(e + 1, 2, E - 1, skip_runtime_bounds_check_because="i is below its last"), 0)
                    with act.If(n > 0):
                        with act.Fori(0, n) as k:
                            t = base + k
                            act.wait_ge(y_mm, t * 2 + 1)
                            for j in range(M):
                                act.wait_ge(hid_mm, t * M + j + 1)
                                act.activation(hid[:, j], hp[j][:, 0:BLK], ACT.Gelu,
                                               bias=b1[:, bass.ds(e * M + j, 1)]).then_inc(hid_ready, 1)

        @block.vector
        def _(dve):
            dve.sem_inc(y_ready, 2)
            dve.wait_ge(b1_turned, 1)
            dve.tensor_copy(b1[:], yp[0][:, 0:E * M]).then_inc(b1_ready, 1)
            dve.wait_ge(consts_in, 16 * (1 + 2 * K))

            def body(e, b, t, k_):
                dve.wait_ge(hid_mm, t * M + M)
                for k in range(K):
                    dve.wait_ge(x_turned, t * K + K + k + 2)
                    dve.tensor_scalar(xT[:, k], tp[k][:, 0:BLK], gamma[:, k:k + 1], beta[:, k:k + 1], ALU.mult, ALU.add).then_inc(xT_ready, 1)
                dve.wait_ge(y_free, t + 1)
                for j in range(2):
                    dve.wait_ge(y_mm, t * 2 + j + 2)
                    dve.tensor_tensor(y[:, 2 * j:2 * j + 2], yp[j][:].rearrange("p (a d) -> p a d", d=D),
                                      b2[:, b].unsqueeze(1).broadcast_to([P, 2, D]), ALU.add).then_inc(y_ready, 1)

            for k in range(K):
                dve.wait_ge(x_turned, k + 2)
                dve.tensor_scalar(xT[:, k], tp[k][:, 0:BLK], gamma[:, k:k + 1], beta[:, k:k + 1], ALU.mult, ALU.add).then_inc(xT_ready, 1)

            def before(e, b, i):
                dve.wait_ge(weights_in[b], i * 48 + 48)
                dve.sem_inc(T.passed, 1)

            blocks(dve, body, before)


def combine(nc, T):
    NG = T.x.shape[0] // G
    with ExitStack() as ctx:
        m = Memory(nc, ctx, "co")
        sb, sem = m.sb, m.sem
        slot_i = sb("slot_i", [R, 2, 2, S], I32)
        x1 = sb("x1", [R, 2, S, D])
        res = sb("res", [R, 2, 2, S, D])
        first = sb("first", [R, 2, S, D])
        out = sb("out", [R, 2, S, D])
        slot_ready, rows_in = sem("slot_ready"), [sem(f"rows_in{b}") for b in range(2)]
        x1_in = [sem(f"x1_in{b}") for b in range(2)]
        first_ready, out_ready = sem("first_ready"), sem("out_ready")
        out_stored = [sem(f"out_stored{b}") for b in range(2)]
        block = ctx.enter_context(nc.Block())
        x1_rows = T.x1_table.rearrange("(g s p) d -> g p s d", s=S, p=R)
        out_rows = T.out.rearrange("(g s p) d -> g p s d", s=S, p=R)

        def run(eng, step):
            for g in range(3):
                step(g, g % 2, g // 2)
            with eng.Fori(1, (NG - 1) // 2) as i:
                step(i * 2 + 1, 1, i)
                step(i * 2 + 2, 0, i + 1)

        @block.sync
        def _(sp):
            def step(g, b, u):
                if not (isinstance(g, int) and g < 2):
                    sp.wait_ge(first_ready, g - 1)
                sp.dma_start(x1[:, b], x1_rows[g]).then_inc(x1_in[b], 16)
                if not (isinstance(g, int) and g < 1):
                    sp.wait_ge(out_ready, g)
                    sp.dma_start(out_rows[g - 1], out[:, 1 - b]).then_inc(out_stored[1 - b], 16)

            run(sp, step)
            sp.wait_ge(out_ready, NG)
            sp.dma_start(out_rows[NG - 1], out[:, (NG - 1) % 2]).then_inc(out_stored[(NG - 1) % 2], 16)
            for b in range(2):
                sp.wait_ge(out_stored[b], 16 * ((NG + 1 - b) // 2))

        @block.gpsimd
        def _(pool):
            def step(g, b, u):
                pool.wait_ge(slot_ready, g + 1)
                pool.sem_inc(T.passed, 1)
                for s in range(S):
                    for n in range(2):
                        pool.indirect_dma_start(
                            out=res[:, b, n, s, :], out_offset=None, in_=T.results,
                            in_offset=bass.IndirectOffsetOnAxis(ap=slot_i[:, b, n, s:s + 1], axis=0),
                        ).then_inc(rows_in[b], 16)

            run(pool, step)

        @block.vector
        def _(dve):
            def places(g, b):
                dve.tensor_copy(slot_i[:, b], T.slot[:, :, bass.ds(g * S, S)]).then_inc(slot_ready, 1)

            def add(g, b, u):
                dve.wait_ge(x1_in[b], u * 16 + 16)
                dve.wait_ge(rows_in[b], u * (16 * 2 * S) + 16 * 2 * S)
                for n, into, base, ready in ((0, first, x1, first_ready), (1, out, first, out_ready)):
                    if n:
                        dve.wait_ge(first_ready, g + 1)
                        if not (isinstance(g, int) and g < 2):
                            dve.wait_ge(out_stored[b], u * 16)
                    for s in range(S):
                        last = dve.scalar_tensor_tensor(out=into[:, b, s], in0=res[:, b, n, s], scalar=T.gate[:, n, bass.ds(g * S + s, 1)],
                                                        in1=base[:, b, s], op0=ALU.mult, op1=ALU.add)
                    last.then_inc(ready, 1)

            places(0, 0)
            places(1, 1)
            for g in range(2):
                add(g, g % 2, 0)
                dve.wait_ge(out_ready, g + 1)
                places(g + 2, g % 2)
            with dve.Fori(1, (NG - 3) // 2) as i:
                for b in range(2):
                    add(i * 2 + b, b, i)
                    dve.wait_ge(out_ready, i * 2 + b + 1)
                    places(i * 2 + b + 2, b)
            for g in range(NG - 3, NG):
                add(g, g % 2, g // 2)
                if g + 2 < NG:
                    dve.wait_ge(out_ready, g + 1)
                    places(g + 2, g % 2)


class Tensors:

    def __init__(self, out, x, src, dst, W_s, W_t, W_attn, W_fc, b_fc, wq, bq, wk, bk, wv, bv, wo, bo,
                 gamma, beta, Wr, br, W1, b1, W2, b2):
        self.out, self.x, self.src, self.dst = out, x, src, dst
        self.W_s, self.W_t, self.W_attn, self.W_fc, self.b_fc = W_s, W_t, W_attn, W_fc, b_fc
        self.wq, self.bq, self.wk, self.bk, self.wv, self.bv, self.wo, self.bo = wq, bq, wk, bk, wv, bv, wo, bo
        self.gamma, self.beta, self.Wr, self.br = gamma, beta, Wr, br
        self.W1, self.b1, self.W2, self.b2 = W1, b1, W2, b2


def build(nc, out, **arrays):
    T = Tensors(out, **arrays)
    N = T.x.shape[0]
    T.NB = -(-N // P)
    T.xn_table = nc.dram_tensor("xn_table", [T.NB * P, XW], F32).ap()
    T.ps_table = nc.dram_tensor("ps_table", [N, D], F32).ap()
    T.pt_table = nc.dram_tensor("pt_table", [N, D], F32).ap()
    T.dst_flat = nc.dram_tensor("dst_flat", [T.src.shape[0]], F32).ap()
    T.src_flat = nc.dram_tensor("src_flat", [T.src.shape[0]], F32).ap()
    T.e_flat = nc.dram_tensor("e_flat", [T.src.shape[0]], F32).ap()
    T.x1_table = nc.dram_tensor("x1_table", [N, D], F32).ap()
    T.lists = nc.dram_tensor("lists", [T.W1.shape[0] * CAP, D], F32).ap()
    T.results = nc.dram_tensor("results", [BLOCKS * BLK, D], F32).ap()
    T.agg = nc.dram_tensor("agg", [T.NB * P, D], F32).ap()
    T.q_table = nc.dram_tensor("q_table", [K, P, N], F32).ap()
    with ExitStack() as ctx:
        m = Memory(nc, ctx, "all")
        T.ident = m.sb("ident", [P, P])
        T.w_fcT = m.sb("w_fcT", [P, K, D])
        T.kv = m.sb("kv", [P, K, P])
        T.ksum = m.sb("ksum", [P, K, P])
        T.src_t = m.sb("src_t", [R, T.src.shape[0] // R])
        T.dst_t = m.sb("dst_t", [R, T.src.shape[0] // R])
        T.src_low = m.sb("src_low", [R, 2, T.src.shape[0] // R], mybir.dt.bfloat16)
        T.e = m.sb("e", [R, T.src.shape[0] // R])
        T.shift = m.sb("shift", [P, T.NB, 2])
        T.plan = m.sb("plan", [1, 3, T.src.shape[0] // C + 1], I32)
        T.plan_a = m.sb("plan_a", [1, 3, T.src.shape[0] // CA + 1], I32)
        T.gate = m.sb("gate", [R, 2, N // R])
        T.slot = m.sb("slot", [R, 2, N // R], I32)
        T.moe = m.sb("moe", [1, 3, T.W1.shape[0] + 1], I32)
        T.far_i = m.sb("far_i", [1, 1], I32)
        T.passed = m.sem("passed")
        for step in STEPS:
            step(nc, T)


STEPS = [project, edges, extent, reshift, aggregate, mix, experts, combine]


_INS = {
    "x": "x", "src": "src", "dst": "dst", "L0_gnn_W_s": "W_s", "L0_gnn_W_t": "W_t", "L0_gnn_W_attn": "W_attn",
    "L0_gnn_W_fc": "W_fc", "L0_gnn_b_fc": "b_fc", "L0_mix_wq": "wq", "L0_mix_bq": "bq", "L0_mix_wk": "wk",
    "L0_mix_bk": "bk", "L0_mix_wv": "wv", "L0_mix_bv": "bv", "L0_mix_wo": "wo", "L0_mix_bo": "bo",
    "L0_ffn_gamma": "gamma", "L0_ffn_beta": "beta", "L0_ffn_Wr": "Wr", "L0_ffn_br": "br", "L0_ffn_W1": "W1",
    "L0_ffn_b1": "b1", "L0_ffn_W2": "W2", "L0_ffn_b2": "b2",
}


def kernel(**inputs):
    import numpy as np
    import concourse.bacc as bacc
    from concourse.bass_utils import run_bass_kernel_spmd

    nc = bacc.Bacc("TRN2", target_bir_lowering=False, num_devices=1)
    arrays, args = {}, {}
    for name, short in _INS.items():
        a = np.ascontiguousarray(inputs[name])
        arrays[f"in_{short}"] = a
        args[short] = nc.dram_tensor(f"in_{short}", a.shape, mybir.dt.from_np(a.dtype), kind="ExternalInput").ap()
    out = nc.dram_tensor("out_x", inputs["x"].shape, F32, kind="ExternalOutput").ap()
    build(nc, out, **args)
    r = run_bass_kernel_spmd(nc, [arrays], core_ids=[0])
    return r.results[0]["out_x"]
```
